# Optimizing a Trainium2 kernel written in Bass

```python
import numpy as np
import jax
import jax.numpy as jnp

def _softmax(x, axis=-1):
    return jax.nn.softmax(x, axis=axis)

def _gelu(x):
    return jax.nn.gelu(x, approximate=True)

def _silu(x):
    return jax.nn.silu(x)

def _sigmoid(x):
    return jax.nn.sigmoid(x)

def _layernorm(x, axis=-1, eps=1e-05):
    m = jnp.mean(x, axis=axis, keepdims=True)
    v = jnp.var(x, axis=axis, keepdims=True)
    return (x - m) / jnp.sqrt(v + eps)

def _scatter_add(tgt, idx, src, axis=0):
    return tgt.at[idx].add(src)

def _segment_sum(src, seg, n):
    return jax.ops.segment_sum(src, seg, n)
kernel_name = 'mk_vit_tower_cls_d2_tok_img768_r4_ea8677'

def setup_inputs(seed: int=0):
    np.random.seed(seed)
    _w = jnp.asarray

    def _rec_inputs():
        import jax
        import jax.numpy as jnp
        _rk = jax.random.key(seed)
        x = -0.000356955 + 1 * jax.random.normal(jax.random.fold_in(_rk, 1), (32, 3, 96, 96), jnp.float32)
        cls_tok = 0.02 * jax.random.normal(jax.random.fold_in(_rk, 5), (1, 1, 192), jnp.float32)
        return (x, cls_tok)
    x, cls_tok = _rec_inputs()

    def _L0_tok_setup():
        import jax, jax.numpy as jnp
        import numpy as np
        PATCH = 16
        POS_GRID = (14, 14)
        EMBED = 192
        C_IN = 3

        def _nearest_resize(x, out_h, out_w):
            _, _, h, w = x.shape
            ih = jnp.arange(out_h) * h // out_h
            iw = jnp.arange(out_w) * w // out_w
            return x[:, :, ih][:, :, :, iw]
        key = jax.random.key(seed)
        k1, k2, k3, k4, k5 = jax.random.split(key, 5)
        im = jax.random.normal(k1, (128, C_IN, 224, 224), dtype=jnp.float32)
        W = jax.random.normal(k2, (C_IN * PATCH * PATCH, EMBED), dtype=jnp.float32) * 0.02
        b = jax.random.normal(k3, (EMBED,), dtype=jnp.float32) * 0.02
        positions = jax.random.normal(k4, (1, EMBED, POS_GRID[0], POS_GRID[1]), dtype=jnp.float32)
        cls_embedding = jax.random.normal(k5, (1, 1, EMBED), dtype=jnp.float32)
        return {'im': im, 'W': W, 'b': b, 'positions': positions, 'cls_embedding': cls_embedding}
    _L0_tok_all = _L0_tok_setup()
    _L0_tok_in = {k: v for k, v in _L0_tok_all.items() if k in ('W', 'b', 'positions', 'cls_embedding')}
    del _L0_tok_all

    def _L0_attn_setup():
        import jax, jax.numpy as jnp
        import numpy as np
        D_MODEL = 192
        D_STATE = 16
        DT_MIN, DT_MAX = (0.001, 0.1)

        def _mlp(x, w1, b1, w2, b2):
            return jax.nn.silu(x @ w1 + b1) @ w2 + b2

        def _ssm_forward(x, A_w1, A_b1, A_w2, A_b2, B_w1, B_b1, B_w2, B_b2, C_w1, C_b1, C_w2, C_b2, d_w1, d_b1, d_w2, d_b2, D_param, log_dt):
            Bsz, L, Dm = x.shape
            N = A_w2.shape[1]
            A_log = -jnp.abs(_mlp(x, A_w1, A_b1, A_w2, A_b2))
            Bv = _mlp(x, B_w1, B_b1, B_w2, B_b2)
            Cv = _mlp(x, C_w1, C_b1, C_w2, C_b2)
            delta = jax.nn.sigmoid(_mlp(x, d_w1, d_b1, d_w2, d_b2))
            dt = jnp.exp(log_dt)

            def step(state, inp):
                a, b, c, dlt, u_t = inp
                dA = jnp.exp(a[:, None, :] * dt[None, :, None])
                dB = b[:, None, :] * dt[None, :, None]
                cur = u_t[:, :, None] * dB
                state = (dlt[:, :, None] * state + (1.0 - dlt[:, :, None]) * cur) * dA
                y = jnp.sum(state * c[:, None, :], axis=2) + u_t * D_param
                return (state, y)
            init = jnp.zeros((Bsz, Dm, N), x.dtype)
            xs = (jnp.swapaxes(A_log, 0, 1), jnp.swapaxes(Bv, 0, 1), jnp.swapaxes(Cv, 0, 1), jnp.swapaxes(delta, 0, 1), jnp.swapaxes(x, 0, 1))
            _, ys = jax.lax.scan(step, init, xs)
            return jnp.swapaxes(ys, 0, 1)
        key = jax.random.key(seed)
        ks = jax.random.split(key, 16)
        d, n = (D_MODEL, D_STATE)

        def lin(k, fan_in, fan_out):
            kw, kb = jax.random.split(k)
            s = 1.0 / np.sqrt(fan_in)
            return (jax.random.uniform(kw, (fan_in, fan_out), jnp.float32, -s, s), jax.random.uniform(kb, (fan_out,), jnp.float32, -s, s))
        A_w1, A_b1 = lin(ks[0], d, 2 * d)
        A_w2, A_b2 = lin(ks[1], 2 * d, n)
        B_w1, B_b1 = lin(ks[2], d, 2 * d)
        B_w2, B_b2 = lin(ks[3], 2 * d, n)
        C_w1, C_b1 = lin(ks[4], d, 2 * d)
        C_w2, C_b2 = lin(ks[5], 2 * d, n)
        d_w1, d_b1 = lin(ks[6], d, d)
        d_w2, d_b2 = lin(ks[7], d, d)
        D_param = jax.random.normal(ks[8], (d,), jnp.float32)
        log_dt = jnp.linspace(np.log(DT_MIN), np.log(DT_MAX), d).astype(jnp.float32)
        x = jax.random.normal(ks[9], (4, 512, d), jnp.float32)
        return {'x': x, 'A_w1': A_w1, 'A_b1': A_b1, 'A_w2': A_w2, 'A_b2': A_b2, 'B_w1': B_w1, 'B_b1': B_b1, 'B_w2': B_w2, 'B_b2': B_b2, 'C_w1': C_w1, 'C_b1': C_b1, 'C_w2': C_w2, 'C_b2': C_b2, 'd_w1': d_w1, 'd_b1': d_b1, 'd_w2': d_w2, 'd_b2': d_b2, 'D_param': D_param, 'log_dt': log_dt}
    _L0_attn_all = _L0_attn_setup()
    _L0_attn_in = {k: v for k, v in _L0_attn_all.items() if k in ('A_w1', 'A_b1', 'A_w2', 'A_b2', 'B_w1', 'B_b1', 'B_w2', 'B_b2', 'C_w1', 'C_b1', 'C_w2', 'C_b2', 'd_w1', 'd_b1', 'd_w2', 'd_b2', 'D_param', 'log_dt')}
    del _L0_attn_all

    def _L0_ffn_setup():
        import jax, jax.numpy as jnp
        import numpy as np
        B, S, H, F, E, TOP_K = (4, 512, 192, 768, 8, 2)
        key = jax.random.key(seed)
        ks = jax.random.split(key, 6)
        x = jax.random.normal(ks[0], (B, S, H), dtype=jnp.float32)
        Wr = jax.random.normal(ks[1], (E, H), dtype=jnp.float32) * 0.02
        Wi = jax.random.normal(ks[2], (E, F, H), dtype=jnp.float32) * 0.02
        bi = jnp.zeros((E, F), dtype=jnp.float32)
        Wo = jax.random.normal(ks[3], (E, H, F), dtype=jnp.float32) * 0.02
        bo = jnp.zeros((E, H), dtype=jnp.float32)
        return {'x': x, 'Wr': Wr, 'Wi': Wi, 'bi': bi, 'Wo': Wo, 'bo': bo}
    _L0_ffn_all = _L0_ffn_setup()
    _L0_ffn_in = {k: v for k, v in _L0_ffn_all.items() if k in ('Wr', 'Wi', 'bi', 'Wo', 'bo')}
    del _L0_ffn_all

    def _L1_attn_setup():
        import jax, jax.numpy as jnp
        import numpy as np
        B, L, D = (2, 1024, 192)
        BN = 96
        DI = 192
        NS = 16
        DC = 4
        R = 24

        def _ln(x, g, b):
            m = x.mean(-1, keepdims=True)
            v = ((x - m) ** 2).mean(-1, keepdims=True)
            return (x - m) / jnp.sqrt(v + 1e-05) * g + b

        def _mamba(x, in_W, conv_w, conv_b, xproj_W, dt_W, dt_b, A_log, Dp, out_W):
            Bb, Ll, _ = x.shape
            xz = x @ in_W
            xs, z = jnp.split(xz, 2, axis=-1)
            xc = jnp.transpose(xs, (0, 2, 1))
            xc = jax.lax.conv_general_dilated(xc, conv_w[:, None, :], (1,), [(DC - 1, 0)], dimension_numbers=('NCH', 'OIH', 'NCH'), feature_group_count=DI)
            xc = jax.nn.silu(xc + conv_b[None, :, None])
            u = jnp.transpose(xc, (0, 2, 1))
            x_dbl = u @ xproj_W
            dt, Bm, Cm = jnp.split(x_dbl, [R, R + NS], axis=-1)
            dt = jax.nn.softplus(dt @ dt_W + dt_b)
            A = -jnp.exp(A_log)

            def step(h, inp):
                dt_t, B_t, C_t, u_t = inp
                dA = jnp.exp(dt_t[:, :, None] * A)
                h = dA * h + (dt_t * u_t)[:, :, None] * B_t[:, None, :]
                y = (h * C_t[:, None, :]).sum(-1)
                return (h, y)
            tm = lambda a: jnp.transpose(a, (1, 0, 2))
            h0 = jnp.zeros((Bb, DI, NS), x.dtype)
            _, ys = jax.lax.scan(step, h0, (tm(dt), tm(Bm), tm(Cm), tm(u)))
            y = jnp.transpose(ys, (1, 0, 2)) + u * Dp
            y = y * jax.nn.silu(z)
            return y @ out_W
        key = jax.random.key(seed)
        ks = jax.random.split(key, 32)
        n = lambda i, shape, s=0.02: jax.random.normal(ks[i], shape, jnp.float32) * s
        inp = {'x': jax.random.normal(ks[0], (B, L, D), jnp.float32), 'down_W': n(1, (D, BN)), 'down_b': jnp.zeros((BN,), jnp.float32), 'up_W': n(2, (BN, D)), 'up_b': jnp.zeros((D,), jnp.float32)}
        A_log = jnp.log(jnp.tile(jnp.arange(1, NS + 1, dtype=jnp.float32), (DI, 1)))
        for pi, p in enumerate(['f', 'b']):
            o = 3 + pi * 10
            inp[p + '_in_W'] = n(o, (BN, 2 * DI))
            inp[p + '_conv_w'] = n(o + 1, (DI, DC), 0.1)
            inp[p + '_conv_b'] = jnp.zeros((DI,), jnp.float32)
            inp[p + '_xproj_W'] = n(o + 2, (DI, R + 2 * NS))
            inp[p + '_dt_W'] = n(o + 3, (R, DI), 0.1)
            inp[p + '_dt_b'] = n(o + 4, (DI,), 0.5)
            inp[p + '_A_log'] = A_log
            inp[p + '_D'] = jnp.ones((DI,), jnp.float32)
            inp[p + '_out_W'] = n(o + 5, (DI, BN))
            inp[p + '_ln_g'] = jnp.ones((BN,), jnp.float32)
            inp[p + '_ln_b'] = jnp.zeros((BN,), jnp.float32)
        return inp
    _L1_attn_all = _L1_attn_setup()
    _L1_attn_in = {k: v for k, v in _L1_attn_all.items() if k in ('down_W', 'down_b', 'up_W', 'up_b', 'f_in_W', 'f_conv_w', 'f_conv_b', 'f_xproj_W', 'f_dt_W', 'f_dt_b', 'f_A_log', 'f_D', 'f_out_W', 'f_ln_g', 'f_ln_b', 'b_in_W', 'b_conv_w', 'b_conv_b', 'b_xproj_W', 'b_dt_W', 'b_dt_b', 'b_A_log', 'b_D', 'b_out_W', 'b_ln_g', 'b_ln_b')}
    del _L1_attn_all

    def _L1_ffn_setup():
        import jax, jax.numpy as jnp
        import numpy as np
        B, S, H = (4, 2048, 192)
        E, K = (8, 2)
        key = jax.random.key(seed)
        ks = jax.random.split(key, 5)
        scale = 1.0 / np.sqrt(H)
        x = jax.random.normal(ks[0], (B, S, H), dtype=jnp.float32)
        router_w = jax.random.uniform(ks[1], (E, H), jnp.float32, -scale, scale)
        router_b = jax.random.uniform(ks[2], (E,), jnp.float32, -scale, scale)
        expert_w = jax.random.uniform(ks[3], (E, H, H), jnp.float32, -scale, scale)
        expert_b = jax.random.uniform(ks[4], (E, H), jnp.float32, -scale, scale)
        return {'x': x, 'router_w': router_w, 'router_b': router_b, 'expert_w': expert_w, 'expert_b': expert_b}
    _L1_ffn_all = _L1_ffn_setup()
    _L1_ffn_in = {k: v for k, v in _L1_ffn_all.items() if k in ('router_w', 'router_b', 'expert_w', 'expert_b')}
    del _L1_ffn_all
    return {'x': x, 'cls_tok': cls_tok, 'L0_tok_W': _L0_tok_in['W'], 'L0_tok_b': _L0_tok_in['b'], 'L0_tok_positions': _L0_tok_in['positions'], 'L0_tok_cls_embedding': _L0_tok_in['cls_embedding'], 'L0_attn_A_w1': _L0_attn_in['A_w1'], 'L0_attn_A_b1': _L0_attn_in['A_b1'], 'L0_attn_A_w2': _L0_attn_in['A_w2'], 'L0_attn_A_b2': _L0_attn_in['A_b2'], 'L0_attn_B_w1': _L0_attn_in['B_w1'], 'L0_attn_B_b1': _L0_attn_in['B_b1'], 'L0_attn_B_w2': _L0_attn_in['B_w2'], 'L0_attn_B_b2': _L0_attn_in['B_b2'], 'L0_attn_C_w1': _L0_attn_in['C_w1'], 'L0_attn_C_b1': _L0_attn_in['C_b1'], 'L0_attn_C_w2': _L0_attn_in['C_w2'], 'L0_attn_C_b2': _L0_attn_in['C_b2'], 'L0_attn_d_w1': _L0_attn_in['d_w1'], 'L0_attn_d_b1': _L0_attn_in['d_b1'], 'L0_attn_d_w2': _L0_attn_in['d_w2'], 'L0_attn_d_b2': _L0_attn_in['d_b2'], 'L0_attn_D_param': _L0_attn_in['D_param'], 'L0_attn_log_dt': _L0_attn_in['log_dt'], 'L0_ffn_Wr': _L0_ffn_in['Wr'], 'L0_ffn_Wi': _L0_ffn_in['Wi'], 'L0_ffn_bi': _L0_ffn_in['bi'], 'L0_ffn_Wo': _L0_ffn_in['Wo'], 'L0_ffn_bo': _L0_ffn_in['bo'], 'L1_attn_down_W': _L1_attn_in['down_W'], 'L1_attn_down_b': _L1_attn_in['down_b'], 'L1_attn_up_W': _L1_attn_in['up_W'], 'L1_attn_up_b': _L1_attn_in['up_b'], 'L1_attn_f_in_W': _L1_attn_in['f_in_W'], 'L1_attn_f_conv_w': _L1_attn_in['f_conv_w'], 'L1_attn_f_conv_b': _L1_attn_in['f_conv_b'], 'L1_attn_f_xproj_W': _L1_attn_in['f_xproj_W'], 'L1_attn_f_dt_W': _L1_attn_in['f_dt_W'], 'L1_attn_f_dt_b': _L1_attn_in['f_dt_b'], 'L1_attn_f_A_log': _L1_attn_in['f_A_log'], 'L1_attn_f_D': _L1_attn_in['f_D'], 'L1_attn_f_out_W': _L1_attn_in['f_out_W'], 'L1_attn_f_ln_g': _L1_attn_in['f_ln_g'], 'L1_attn_f_ln_b': _L1_attn_in['f_ln_b'], 'L1_attn_b_in_W': _L1_attn_in['b_in_W'], 'L1_attn_b_conv_w': _L1_attn_in['b_conv_w'], 'L1_attn_b_conv_b': _L1_attn_in['b_conv_b'], 'L1_attn_b_xproj_W': _L1_attn_in['b_xproj_W'], 'L1_attn_b_dt_W': _L1_attn_in['b_dt_W'], 'L1_attn_b_dt_b': _L1_attn_in['b_dt_b'], 'L1_attn_b_A_log': _L1_attn_in['b_A_log'], 'L1_attn_b_D': _L1_attn_in['b_D'], 'L1_attn_b_out_W': _L1_attn_in['b_out_W'], 'L1_attn_b_ln_g': _L1_attn_in['b_ln_g'], 'L1_attn_b_ln_b': _L1_attn_in['b_ln_b'], 'L1_ffn_router_w': _L1_ffn_in['router_w'], 'L1_ffn_router_b': _L1_ffn_in['router_b'], 'L1_ffn_expert_w': _L1_ffn_in['expert_w'], 'L1_ffn_expert_b': _L1_ffn_in['expert_b']}

def reference(x, cls_tok, L0_tok_W, L0_tok_b, L0_tok_positions, L0_tok_cls_embedding, L0_attn_A_w1, L0_attn_A_b1, L0_attn_A_w2, L0_attn_A_b2, L0_attn_B_w1, L0_attn_B_b1, L0_attn_B_w2, L0_attn_B_b2, L0_attn_C_w1, L0_attn_C_b1, L0_attn_C_w2, L0_attn_C_b2, L0_attn_d_w1, L0_attn_d_b1, L0_attn_d_w2, L0_attn_d_b2, L0_attn_D_param, L0_attn_log_dt, L0_ffn_Wr, L0_ffn_Wi, L0_ffn_bi, L0_ffn_Wo, L0_ffn_bo, L1_attn_down_W, L1_attn_down_b, L1_attn_up_W, L1_attn_up_b, L1_attn_f_in_W, L1_attn_f_conv_w, L1_attn_f_conv_b, L1_attn_f_xproj_W, L1_attn_f_dt_W, L1_attn_f_dt_b, L1_attn_f_A_log, L1_attn_f_D, L1_attn_f_out_W, L1_attn_f_ln_g, L1_attn_f_ln_b, L1_attn_b_in_W, L1_attn_b_conv_w, L1_attn_b_conv_b, L1_attn_b_xproj_W, L1_attn_b_dt_W, L1_attn_b_dt_b, L1_attn_b_A_log, L1_attn_b_D, L1_attn_b_out_W, L1_attn_b_ln_g, L1_attn_b_ln_b, L1_ffn_router_w, L1_ffn_router_b, L1_ffn_expert_w, L1_ffn_expert_b):
    import jax
    import jax.numpy as jnp

    def _L0_tok_ref(im, W, b, positions, cls_embedding):
        import jax, jax.numpy as jnp
        import numpy as np
        PATCH = 16
        POS_GRID = (14, 14)
        EMBED = 192
        C_IN = 3

        def _nearest_resize(x, out_h, out_w):
            _, _, h, w = x.shape
            ih = jnp.arange(out_h) * h // out_h
            iw = jnp.arange(out_w) * w // out_w
            return x[:, :, ih][:, :, :, iw]
        B, C, H, Wd = im.shape
        ph, pw = (PATCH, PATCH)
        gh, gw = (H // ph, Wd // pw)
        patches = im.reshape(B, C, gh, ph, gw, pw)
        patches = patches.transpose(0, 2, 4, 1, 3, 5).reshape(B, gh * gw, C * ph * pw)
        pos = _nearest_resize(positions, gh, gw)
        pos = pos.reshape(1, EMBED, gh * gw).transpose(0, 2, 1)
        embeds = jnp.einsum('bsp,pd->bsd', patches, W) + b + pos
        cls_tok = jnp.broadcast_to(cls_embedding, (B, 1, EMBED))
        return jnp.concatenate((cls_tok, embeds), axis=1)

    def _L0_attn_ref(x, A_w1, A_b1, A_w2, A_b2, B_w1, B_b1, B_w2, B_b2, C_w1, C_b1, C_w2, C_b2, d_w1, d_b1, d_w2, d_b2, D_param, log_dt):
        import jax, jax.numpy as jnp
        import numpy as np
        D_MODEL = 192
        D_STATE = 16
        DT_MIN, DT_MAX = (0.001, 0.1)

        def _mlp(x, w1, b1, w2, b2):
            return jax.nn.silu(x @ w1 + b1) @ w2 + b2

        def _ssm_forward(x, A_w1, A_b1, A_w2, A_b2, B_w1, B_b1, B_w2, B_b2, C_w1, C_b1, C_w2, C_b2, d_w1, d_b1, d_w2, d_b2, D_param, log_dt):
            Bsz, L, Dm = x.shape
            N = A_w2.shape[1]
            A_log = -jnp.abs(_mlp(x, A_w1, A_b1, A_w2, A_b2))
            Bv = _mlp(x, B_w1, B_b1, B_w2, B_b2)
            Cv = _mlp(x, C_w1, C_b1, C_w2, C_b2)
            delta = jax.nn.sigmoid(_mlp(x, d_w1, d_b1, d_w2, d_b2))
            dt = jnp.exp(log_dt)

            def step(state, inp):
                a, b, c, dlt, u_t = inp
                dA = jnp.exp(a[:, None, :] * dt[None, :, None])
                dB = b[:, None, :] * dt[None, :, None]
                cur = u_t[:, :, None] * dB
                state = (dlt[:, :, None] * state + (1.0 - dlt[:, :, None]) * cur) * dA
                y = jnp.sum(state * c[:, None, :], axis=2) + u_t * D_param
                return (state, y)
            init = jnp.zeros((Bsz, Dm, N), x.dtype)
            xs = (jnp.swapaxes(A_log, 0, 1), jnp.swapaxes(Bv, 0, 1), jnp.swapaxes(Cv, 0, 1), jnp.swapaxes(delta, 0, 1), jnp.swapaxes(x, 0, 1))
            _, ys = jax.lax.scan(step, init, xs)
            return jnp.swapaxes(ys, 0, 1)
        return _ssm_forward(x, A_w1, A_b1, A_w2, A_b2, B_w1, B_b1, B_w2, B_b2, C_w1, C_b1, C_w2, C_b2, d_w1, d_b1, d_w2, d_b2, D_param, log_dt)

    def _L0_ffn_ref(x, Wr, Wi, bi, Wo, bo):
        import jax, jax.numpy as jnp
        import numpy as np
        B, S, H, F, E, TOP_K = (4, 512, 192, 768, 8, 2)
        xf = x.reshape(-1, x.shape[-1])
        router_logits = jnp.einsum('th,eh->te', xf, Wr)
        topk_vals, topk_idx = jax.lax.top_k(router_logits, TOP_K)
        routing_weights = jax.nn.softmax(topk_vals, axis=-1)
        h = jnp.einsum('th,efh->etf', xf, Wi) + bi[:, None, :]
        h = jax.nn.gelu(h, approximate=False)
        expert_out = jnp.einsum('etf,ehf->eth', h, Wo) + bo[:, None, :]
        expert_out = jnp.transpose(expert_out, (1, 0, 2))
        gathered = jnp.take_along_axis(expert_out, topk_idx[:, :, None], axis=1)
        out = jnp.einsum('tk,tkh->th', routing_weights, gathered)
        return out.reshape(x.shape)

    def _L1_attn_ref(x, down_W, down_b, up_W, up_b, f_in_W, f_conv_w, f_conv_b, f_xproj_W, f_dt_W, f_dt_b, f_A_log, f_D, f_out_W, f_ln_g, f_ln_b, b_in_W, b_conv_w, b_conv_b, b_xproj_W, b_dt_W, b_dt_b, b_A_log, b_D, b_out_W, b_ln_g, b_ln_b):
        import jax, jax.numpy as jnp
        import numpy as np
        B, L, D = (2, 1024, 192)
        BN = 96
        DI = 192
        NS = 16
        DC = 4
        R = 24

        def _ln(x, g, b):
            m = x.mean(-1, keepdims=True)
            v = ((x - m) ** 2).mean(-1, keepdims=True)
            return (x - m) / jnp.sqrt(v + 1e-05) * g + b

        def _mamba(x, in_W, conv_w, conv_b, xproj_W, dt_W, dt_b, A_log, Dp, out_W):
            Bb, Ll, _ = x.shape
            xz = x @ in_W
            xs, z = jnp.split(xz, 2, axis=-1)
            xc = jnp.transpose(xs, (0, 2, 1))
            xc = jax.lax.conv_general_dilated(xc, conv_w[:, None, :], (1,), [(DC - 1, 0)], dimension_numbers=('NCH', 'OIH', 'NCH'), feature_group_count=DI)
            xc = jax.nn.silu(xc + conv_b[None, :, None])
            u = jnp.transpose(xc, (0, 2, 1))
            x_dbl = u @ xproj_W
            dt, Bm, Cm = jnp.split(x_dbl, [R, R + NS], axis=-1)
            dt = jax.nn.softplus(dt @ dt_W + dt_b)
            A = -jnp.exp(A_log)

            def step(h, inp):
                dt_t, B_t, C_t, u_t = inp
                dA = jnp.exp(dt_t[:, :, None] * A)
                h = dA * h + (dt_t * u_t)[:, :, None] * B_t[:, None, :]
                y = (h * C_t[:, None, :]).sum(-1)
                return (h, y)
            tm = lambda a: jnp.transpose(a, (1, 0, 2))
            h0 = jnp.zeros((Bb, DI, NS), x.dtype)
            _, ys = jax.lax.scan(step, h0, (tm(dt), tm(Bm), tm(Cm), tm(u)))
            y = jnp.transpose(ys, (1, 0, 2)) + u * Dp
            y = y * jax.nn.silu(z)
            return y @ out_W
        h = x @ down_W + down_b
        fwd = _ln(_mamba(h, f_in_W, f_conv_w, f_conv_b, f_xproj_W, f_dt_W, f_dt_b, f_A_log, f_D, f_out_W), f_ln_g, f_ln_b)
        bwd = _ln(_mamba(h[:, ::-1], b_in_W, b_conv_w, b_conv_b, b_xproj_W, b_dt_W, b_dt_b, b_A_log, b_D, b_out_W), b_ln_g, b_ln_b)
        y = fwd + bwd[:, ::-1]
        return y @ up_W + up_b

    def _L1_ffn_ref(x, router_w, router_b, expert_w, expert_b):
        import jax, jax.numpy as jnp
        import numpy as np
        B, S, H = (4, 2048, 192)
        E, K = (8, 2)
        scores = jnp.einsum('bsh,eh->bse', x, router_w) + router_b
        probs = jax.nn.softmax(scores, axis=-1)
        top_probs, expert_ids = jax.lax.top_k(probs, K)
        y = jnp.einsum('bsh,edh->bsed', x, expert_w) + expert_b
        out_k = jnp.take_along_axis(y, expert_ids[..., None], axis=2)
        w = top_probs / (jnp.sum(top_probs, axis=-1, keepdims=True) + 1e-09)
        out = jnp.einsum('bsk,bskh->bsh', w, out_k)
        return out
    h = _L0_tok_ref(x, L0_tok_W, L0_tok_b, L0_tok_positions, L0_tok_cls_embedding)
    h = jnp.concatenate([jnp.broadcast_to(cls_tok, (h.shape[0], 1, h.shape[2])), h], axis=1)
    h = h + _L0_attn_ref(_layernorm(h, axis=-1), L0_attn_A_w1, L0_attn_A_b1, L0_attn_A_w2, L0_attn_A_b2, L0_attn_B_w1, L0_attn_B_b1, L0_attn_B_w2, L0_attn_B_b2, L0_attn_C_w1, L0_attn_C_b1, L0_attn_C_w2, L0_attn_C_b2, L0_attn_d_w1, L0_attn_d_b1, L0_attn_d_w2, L0_attn_d_b2, L0_attn_D_param, L0_attn_log_dt)
    h = h + _L0_ffn_ref(_layernorm(h, axis=-1), L0_ffn_Wr, L0_ffn_Wi, L0_ffn_bi, L0_ffn_Wo, L0_ffn_bo)
    h = h + _L1_attn_ref(_layernorm(h, axis=-1), L1_attn_down_W, L1_attn_down_b, L1_attn_up_W, L1_attn_up_b, L1_attn_f_in_W, L1_attn_f_conv_w, L1_attn_f_conv_b, L1_attn_f_xproj_W, L1_attn_f_dt_W, L1_attn_f_dt_b, L1_attn_f_A_log, L1_attn_f_D, L1_attn_f_out_W, L1_attn_f_ln_g, L1_attn_f_ln_b, L1_attn_b_in_W, L1_attn_b_conv_w, L1_attn_b_conv_b, L1_attn_b_xproj_W, L1_attn_b_dt_W, L1_attn_b_dt_b, L1_attn_b_A_log, L1_attn_b_D, L1_attn_b_out_W, L1_attn_b_ln_g, L1_attn_b_ln_b)
    h = h + _L1_ffn_ref(_layernorm(h, axis=-1), L1_ffn_router_w, L1_ffn_router_b, L1_ffn_expert_w, L1_ffn_expert_b)
    return h

_drawn_inputs = setup_inputs


def setup_inputs(seed=0):
    import zlib

    import numpy as np

    out = dict(_drawn_inputs(seed))
    spreads = {'L0_ffn_bi': (0.0, 0.311),
     'L0_ffn_bo': (0.0, 0.1),
     'L1_attn_down_b': (0.0, 0.683),
     'L1_attn_up_b': (0.0, 0.1),
     'L1_attn_f_conv_b': (0.0, 0.1),
     'L1_attn_f_D': (1.0, 0.6),
     'L1_attn_f_ln_g': (1.0, 0.6),
     'L1_attn_f_ln_b': (0.0, 0.267),
     'L1_attn_b_conv_b': (0.0, 0.1),
     'L1_attn_b_D': (1.0, 0.6),
     'L1_attn_b_ln_g': (1.0, 0.6),
     'L1_attn_b_ln_b': (0.0, 0.325)}
    factors = {'L0_attn_A_w1': 8.0,
     'L0_attn_A_b1': 8.0,
     'L0_attn_A_w2': 8.0,
     'L0_attn_A_b2': 8.0,
     'L0_attn_B_w1': 64.0,
     'L0_attn_B_b1': 64.0,
     'L0_attn_B_w2': 62.936,
     'L0_attn_B_b2': 64.0,
     'L0_attn_C_w1': 64.0,
     'L0_attn_C_b1': 64.0,
     'L0_attn_C_w2': 64.0,
     'L0_attn_C_b2': 64.0,
     'L0_attn_d_w1': 64.0,
     'L0_attn_d_b1': 64.0,
     'L0_attn_d_w2': 64.0,
     'L0_attn_d_b2': 64.0,
     'L0_attn_log_dt': 64.0,
     'L1_attn_f_conv_w': 8.0,
     'L1_attn_f_xproj_W': 8.0,
     'L1_attn_f_dt_W': 8.0,
     'L1_attn_f_dt_b': 8.0,
     'L1_attn_f_A_log': 39.142,
     'L1_attn_b_conv_w': 7.478,
     'L1_attn_b_xproj_W': 8.0,
     'L1_attn_b_dt_W': 8.0,
     'L1_attn_b_dt_b': 8.0,
     'L1_attn_b_A_log': 8.0,
     'L1_ffn_expert_b': 2.944}
    for name, (base, spread) in spreads.items():
        noise = np.random.default_rng([zlib.crc32(name.encode()), seed]).standard_normal(out[name].shape)
        drawn = base * np.exp(spread * noise) if base else spread * noise
        out[name] = jnp.asarray(drawn.astype(out[name].dtype))
    for name, factor in factors.items():
        out[name] = (out[name] * factor).astype(out[name].dtype)
    return out
```

```python
import numpy as np
import concourse.bass as bass
from concourse import mybir
from contextlib import ExitStack

BATCH, SEQ, D = 32, 38, 192
GROUPS = 4
IMG = BATCH // GROUPS
T = IMG * SEQ
HALF = T // 2
GRID = 6
NP = GRID * GRID
KP, PDIM = 6, 128
DM, DR = 128, 64
PK = T + HALF
NSEQ = PK // SEQ
NS = 16
NC = 2
STEPS = NS // NC
EXPERTS, FFN = 8, 768
FT = FFN // 128
BN, RANK = 96, 24
TILES, TW = 3, 102
STARTS = (0, 101, 202)
EPS = 1e-5
A_MIN, A_MAX = 1e-13, 3e22
RESTART = 1e16
NBLK = 128


def _layout(widths):
    at, out = 0, {}
    for name, width in widths:
        out[name] = (at, width)
        at += width
    return out, at


W128 = [
    ("tok_W", KP * D), ("posm", NP), ("posr", NP), ("tok_b", 2), ("cls_m", 2), ("cls_r", 2),
    ("ident", 128), ("log_dt", 2), ("sign", 1), ("fAlog", 2 * NS), ("bAlog", 2 * NS),
    ("m1_w", 1344), ("m1_b", 11), ("m2_w0", 6 * NBLK), ("m2_w1", 3 * NBLK), ("m2_b", 2),
    ("d_w2", D), ("d_b2", 2), ("D0", 2), ("rank", EXPERTS),
    ("r_w", EXPERTS), ("bo", D), ("bi", EXPERTS * FT),
    ("wi", EXPERTS * FFN), ("wo", EXPERTS * FT * D),
    ("down", BN), ("down_b", 1), ("up", D), ("up_b", 2),
]
for _d in "fb":
    W128 += [(_d + "in", 2 * D), (_d + "cw", 8), (_d + "cb", 2), (_d + "xdt", RANK), (_d + "xbc", NBLK),
             (_d + "xdt_r", RANK), (_d + "xbc_r", NBLK), (_d + "dtw", D), (_d + "dtb", 2),
             (_d + "Dp", 2), (_d + "out", BN), (_d + "out_r", BN), (_d + "lng", 2)]
W128 += [("er_w", EXPERTS), ("er_b", 1), ("ew", EXPERTS * D), ("eb", D)]
AT, C128 = _layout(W128)
W64 = [("m1_w", 1344), ("d_w2", D), ("r_w", EXPERTS), ("wi", EXPERTS * FFN), ("down", BN),
       ("er_w", EXPERTS), ("ew", EXPERTS * D)]
ATR, C64 = _layout(W64)
SEG128 = [0, AT["rank"][0], AT["down"][0], C128]
SEG64 = [0, ATR["r_w"][0], ATR["down"][0], C64]


class Signal:

    def __init__(self, sem, per_group):
        self.sem, self.per_group = sem, per_group

    def after(self, g, k):
        return g * self.per_group + k


def vit_tower(nc, x_p, c128, c64, sel_d, out_m, out_r):
    fp32, bf16 = mybir.dt.float32, mybir.dt.bfloat16
    ALU, ACT, AX = mybir.AluOpType, mybir.ActivationFunctionType, mybir.AxisListType
    with ExitStack() as ctx:
        def sb(name, shape, dt=fp32):
            return ctx.enter_context(nc.sbuf_tensor(name, shape, dt))

        def sem(name):
            return ctx.enter_context(nc.semaphore(name))

        def sig(name, per_group):
            return Signal(sem(name), per_group)

        CM = sb("CM", [128, C128])
        CR = sb("CR", [DR, C64])
        SELF = sb("SELF", [128, 2 * NS])
        SEL = sb("SEL", [128, 2 * NS], bf16)
        ones_d = sb("ones_d", [128, 128])
        ones_bn = sb("ones_bn", [BN, BN])
        eps_col = sb("eps_col", [128, 1])
        posb_m = sb("posb_m", [128, NP])
        posb_r = sb("posb_r", [DR, NP])
        dt0 = sb("dt0", [128, 2])
        neg_dt0 = sb("neg_dt0", [128, 2])
        negA = sb("negA", [128, 4 * NS])

        def cm(name, a=0, b=None, p=128, p0=0):
            at, width = AT[name]
            return CM[p0:p, at + a:at + (width if b is None else b)]

        def cr(name, a=0, b=None):
            at, width = ATR[name]
            return CR[:, at + a:at + (width if b is None else b)]

        xp = sb("xp", [128, KP, IMG * NP])
        Hm = sb("Hm", [128, T])
        Hr = sb("Hr", [DR, T])
        Cm = sb("Cm", [128, T])
        Cr = sb("Cr", [DR, T])
        SQr = sb("SQr", [DR, T])
        VE = sb("VE", [128, T])
        RS = sb("RS", [128, T])
        Xm = sb("Xm", [128, T])
        Xr = sb("Xr", [DR, T])
        HIDr = sb("HIDr", [DR, T])
        V = sb("V", [NBLK, T])
        R = sb("R", [NBLK, T])
        S3 = sb("S3", [NBLK, 2, T], bf16)
        DL = sb("DL", [128, PK])
        UP = sb("UP", [128, PK])
        OM = sb("OM", [128, PK])
        WV = sb("WV", [128, PK])
        decay_buf = sb("decay_buf", [128, 2, 2, NC, PK])
        input_buf = sb("input_buf", [128, 2, 2, NC, PK])
        dA, aP = decay_buf[:, 0], decay_buf[:, 1]
        BB, PR = input_buf[:, 0], input_buf[:, 1]
        HG = decay_buf[:, :, :, :, :].rearrange("p a b n k -> p (a b n k)")[:, 0:2 * FT * T].rearrange("p (e f t) -> p e f t", f=FT, t=T)
        HID = input_buf[:, :, :, :, :].rearrange("p a b n k -> p (a b n k)")[:, 0:10 * T].rearrange("p (j t) -> p j t", t=T)
        ST = sb("ST", [128, NC, PK])
        TM = sb("TM", [128, PK])
        gate = sb("gate", [128, 10, TILES, EXPERTS])
        gs = sb("gs", [128, 8, TILES])
        ACC = sb("ACC", [128, TILES, D])
        HB = sb("HB", [BN, T])
        ZS = sb("ZS", [128, PK])
        YS = sb("YS", [BN, 2, T])

        SQm = RS[:, :]
        LG = R[0:EXPERTS, :]
        WTT = VE[0:EXPERTS, :]
        XS = ST[:, 0, :]
        LZ = ST[:, 1, :]
        CV = WV[:, :]
        DT24 = RS[0:RANK, :]
        YT = V[0:BN, :]

        PS = ctx.enter_context(nc.psum_tensor("PS", [128, 8, 512], fp32))

        s_const = [sem(f"s_const{i}") for i in range(3)]
        s_sel = sem("s_sel")
        s_x = sem("s_x")
        s_out = sem("s_out")
        sel_ready = sem("sel_ready")
        prep_dve = sem("prep_dve")
        prep_act = sem("prep_act")
        tok_mm = sig("tok_mm", 2)
        residual = sig("residual", 5)
        stored = sig("stored", 32)
        ln_mean = sig("ln_mean", 4)
        ln_centred = sig("ln_centred", 8)
        ln_squares = sig("ln_squares", 8)
        ln_var = sig("ln_var", 4)
        ln_log = sig("ln_log", 6)
        ln_rstd = sig("ln_rstd", 6)
        ln_x = sig("ln_x", 4)
        bn_mean = sig("bn_mean", 2)
        bn_centred = sig("bn_centred", 2)
        bn_squares = sig("bn_squares", 2)
        bn_var = sig("bn_var", 2)
        hid_mm = sig("hid_mm", 11)
        hid_ready = sig("hid_ready", 11)
        set_mm = sig("set_mm", 4)
        set_copied = sig("set_copied", 8)
        set_ready = sig("set_ready", 4)
        delta_mm = sig("delta_mm", 1)
        delta_ready = sig("delta_ready", 1)
        packed_x = sig("packed_x", 1)
        w_ready = sig("w_ready", 3)
        a_bc = sig("a_bc", STEPS)
        b_bc = sig("b_bc", 3 * STEPS)
        c_bc = sig("c_bc", 3 * STEPS)
        da_ready = sig("da_ready", 3 * STEPS)
        ap_ready = sig("ap_ready", STEPS)
        b_read = sig("b_read", 3 * STEPS)
        b_times_a = sig("b_times_a", STEPS)
        scanned = sig("scanned", 3 * STEPS)
        prod_ready = sig("prod_ready", 3 * STEPS)
        summed = sig("summed", 3 * STEPS)
        logits_mm = sig("logits_mm", 2)
        logits_ready = sig("logits_ready", 2)
        logits_T = sig("logits_T", 2)
        gap_ready = sig("gap_ready", 2)
        ratio_ready = sig("ratio_ready", 2)
        gates_ready = sig("gates_ready", 2)
        gates_T = sig("gates_T", 2)
        gates_T_ready = sig("gates_T_ready", 2)
        bias_mm = sig("bias_mm", 2)
        acc_started = sig("acc_started", 2)
        up_mm = sig("up_mm", EXPERTS * FT)
        gelu_ready = sig("gelu_ready", EXPERTS * FT)
        down_mm = sig("down_mm", EXPERTS)
        acc_done = sig("acc_done", EXPERTS * TILES)
        lin_mm = sig("lin_mm", TILES)
        lin_acc = sig("lin_acc", TILES * EXPERTS)
        back_T = sig("back_T", 2)
        bott_mm = sig("bott_mm", 1)
        bott_ready = sig("bott_ready", 1)
        in_mm = sig("in_mm", 2)
        in_copied = sig("in_copied", 2)
        conv_ready = sig("conv_ready", 2)
        u_ready = sig("u_ready", 2)
        dt24_mm = sig("dt24_mm", 2)
        dt24_ready = sig("dt24_ready", 2)
        dt_mm = sig("dt_mm", 2)
        dt_raw = sig("dt_raw", 2)
        abs_dt = sig("abs_dt", 2)
        exp_dt = sig("exp_dt", 2)
        log_dt_ready = sig("log_dt_ready", 2)
        y_gated = sig("y_gated", 2)
        out_mm = sig("out_mm", 2)
        out_copied = sig("out_copied", 2)
        bn_done = sig("bn_done", 2)
        up_proj = sig("up_proj", 1)
        y_sum = sig("y_sum", 1)
        shift_ready = sig("shift_ready", 1)
        shift_exp = sig("shift_exp", 1)
        abs_ready = sig("abs_ready", 1)
        chain = sem("chain")

        block = ctx.enter_context(nc.Block())

        def seqs(ap):
            return ap.rearrange("p (s t) -> p s t", t=SEQ)

        PARTS = [(slice(0, 128), slice(0, T), slice(0, T), slice(0, DM)),
                 (slice(0, DR), slice(T, PK), slice(0, HALF), slice(DM, D)),
                 (slice(DR, 128), slice(T, PK), slice(HALF, T), slice(DM, D))]

        @block.sync
        def _(sp):
            sp.dma_start(xp[:, :, :], x_p[0, :, :, :]).then_inc(s_x, 16)
            sp.sem_inc(stored.sem, 16)
            for i in range(3):
                a, b = SEG128[i], SEG128[i + 1]
                sp.dma_start(CM[:, a:b], c128[:, a:b]).then_inc(s_const[i], 16)
                a, b = SEG64[i], SEG64[i + 1]
                sp.dma_start(CR[:, a:b], c64[:, a:b]).then_inc(s_const[i], 16)

            def store(g):
                sp.wait_ge(residual.sem, residual.after(g, 5))
                sp.dma_start(out_m[bass.ds(g, 1), :, :].rearrange("g p t -> p (g t)"), Hm[:, :]).then_inc(stored.sem, 16)
                sp.dma_start(out_r[bass.ds(g, 1), :, :].rearrange("g p t -> p (g t)"), Hr[:, :]).then_inc(stored.sem, 16)

            with sp.Fori(0, GROUPS - 1) as g:
                sp.wait_ge(tok_mm.sem, tok_mm.after(g, 2))
                sp.dma_start(xp[:, :, :], x_p[bass.ds(g + 1, 1), :, :, :].rearrange("g p k t -> p (g k) t")).then_inc(s_x, 16)
                store(g)
            store(GROUPS - 1)
            sp.wait_ge(stored.sem, stored.after(GROUPS, 0) + 16)

        @block.gpsimd
        def _(pool):
            nc.gpsimd.memset(ones_d[:, :], 1.0 / D)
            nc.gpsimd.memset(ones_bn[:, :], 1.0 / BN)
            nc.gpsimd.memset(eps_col[:, :], EPS).then_inc(prep_dve, 1)
            pool.wait_ge(prep_dve, 1)
            with pool.Fori(0, GROUPS) as g:
                pool.wait_ge(w_ready.sem, w_ready.after(g, 1))
                for c in range(STEPS):
                    pool.wait_ge(da_ready.sem, da_ready.after(g, c + 1))
                    if c >= 2:
                        pool.wait_ge(scanned.sem, scanned.after(g, c - 1))
                    nc.gpsimd.tensor_tensor(aP[:, c % 2], dA[:, c % 2],
                                            DL[:, :].unsqueeze(1).broadcast_to([128, NC, PK]),
                                            ALU.mult).then_inc(ap_ready.sem, 1)

        @block.scalar
        def _(act):
            act.dma_start(SELF[:, :], sel_d[:, :]).then_inc(s_sel, 16)
            act.wait_ge(s_const[0], 32)
            nc.scalar.activation(dt0[:, :], cm("log_dt"), ACT.Exp).then_inc(prep_act, 1)
            act.wait_ge(prep_act, 1)
            nc.scalar.mul(neg_dt0[:, :], dt0[:, :], -1.0)
            nc.scalar.activation(posb_m[:, :], cm("posm"), ACT.Identity, bias=cm("tok_b", 0, 1))
            nc.scalar.activation(posb_r[:, :], cm("posr", p=DR), ACT.Identity, bias=cm("tok_b", 1, 2, p=DR)).then_inc(prep_act, 1)
            act.wait_ge(sel_ready, 2)
            nc.scalar.activation(negA[:, :], negA[:, :], ACT.Exp).then_inc(prep_act, 1)
            act.wait_ge(prep_act, 4)
            with act.Fori(0, GROUPS) as g:
                def squares(i):
                    act.wait_ge(ln_centred.sem, ln_centred.after(g, 2 * i + 1))
                    nc.scalar.activation(SQm[:, :], Cm[:, :], ACT.Square).then_inc(ln_squares.sem, 1)
                    act.wait_ge(ln_centred.sem, ln_centred.after(g, 2 * i + 2))
                    nc.scalar.activation(SQr[:, :], Cr[:, :], ACT.Square).then_inc(ln_squares.sem, 1)
                    act.wait_ge(ln_var.sem, ln_var.after(g, i + 1))
                    rstd((0, 1, 2, 5)[i], PS[:, 3, 0:T], 128)

                def rstd(i, var, rows):
                    nc.scalar.activation(VE[0:rows, :], var, ACT.Ln, bias=eps_col[0:rows, :]).then_inc(ln_log.sem, 1)
                    act.wait_ge(ln_log.sem, ln_log.after(g, i + 1))
                    nc.scalar.activation(RS[0:rows, :], VE[0:rows, :], ACT.Exp, scale=-0.5).then_inc(ln_rstd.sem, 1)

                def copy_set(i, buf, bank, bias):
                    act.wait_ge(set_mm.sem, set_mm.after(g, i + 1))
                    kw = {} if bias is None else {"bias": bias}
                    nc.scalar.activation(V[:, :], PS[:, bank, 0:T], ACT.Identity, **kw).then_inc(set_copied.sem, 1)
                    if i == 0:
                        act.wait_ge(abs_ready.sem, abs_ready.after(g, 1))
                        nc.scalar.activation(S3[:, buf, :], V[:, :], ACT.Copy).then_inc(set_copied.sem, 1)
                    else:
                        nc.scalar.activation(S3[:, buf, :], PS[:, bank, 0:T], ACT.Identity, **kw).then_inc(set_copied.sem, 1)

                def logits(i, bias):
                    act.wait_ge(logits_mm.sem, logits_mm.after(g, i + 1))
                    kw = {} if bias is None else {"bias": bias}
                    nc.scalar.activation(LG[:, :], PS[0:EXPERTS, 0, 0:T], ACT.Identity, **kw).then_inc(logits_ready.sem, 1)
                    act.wait_ge(gap_ready.sem, gap_ready.after(g, i + 1))
                    nc.scalar.activation(gs[0:TW, 3, :], gs[0:TW, 2, :], ACT.Exp).then_inc(ratio_ready.sem, 1)
                    if i == 1:
                        act.wait_ge(shift_ready.sem, shift_ready.after(g, 1))
                        nc.scalar.activation(gate[0:TW, 7], gate[0:TW, 6], ACT.Exp).then_inc(shift_exp.sem, 1)

                squares(0)
                for j in range(11):
                    act.wait_ge(hid_mm.sem, hid_mm.after(g, j + 1))
                    dst = HID[:, j, :] if j < 10 else HIDr[:, :]
                    rows = 128 if j < 10 else DR
                    nc.scalar.activation(dst, PS[0:rows, 4 + j % 4, 0:T], ACT.Silu,
                                         bias=cm("m1_b", j, j + 1, p=rows)).then_inc(hid_ready.sem, 1)
                copy_set(0, 0, 0, cm("m2_b", 0, 1))
                act.wait_ge(set_ready.sem, set_ready.after(g, 1))
                copy_set(1, 1, 1, cm("m2_b", 1, 2))
                nc.scalar.activation(UP[:, 0:T], Xm[:, :], ACT.Copy)
                nc.scalar.activation(UP[0:DR, T:PK], Xr[:, 0:HALF], ACT.Copy)
                nc.scalar.activation(UP[DR:128, T:PK], Xr[:, HALF:T], ACT.Copy).then_inc(packed_x.sem, 1)
                act.wait_ge(delta_mm.sem, delta_mm.after(g, 1))
                nc.scalar.activation(DL[:, 0:T], PS[:, 2, 0:T], ACT.Sigmoid, bias=cm("d_b2", 0, 1))
                nc.scalar.activation(DL[:, T:PK], PS[:, 2, T:PK], ACT.Sigmoid, bias=cm("d_b2", 1, 2)).then_inc(delta_ready.sem, 1)
                for c in range(STEPS):
                    act.wait_ge(a_bc.sem, a_bc.after(g, c + 1))
                    if c >= 2:
                        act.wait_ge(b_times_a.sem, b_times_a.after(g, c - 1))
                        act.wait_ge(ap_ready.sem, ap_ready.after(g, c - 1))
                    for k, cols in enumerate((slice(0, T), slice(T, PK))):
                        last = nc.scalar.activation(dA[:, c % 2, :, cols], PS[:, 4:6, cols], ACT.Exp,
                                                    scale=neg_dt0[:, k:k + 1])
                    last.then_inc(da_ready.sem, 1)
                squares(1)
                act.wait_ge(s_const[1], 32)
                act.wait_ge(s_const[2], 32)
                logits(0, None)
                for e in range(EXPERTS):
                    for f in range(FT):
                        n = e * FT + f
                        act.wait_ge(up_mm.sem, up_mm.after(g, n + 1))
                        if e >= 2 and f == 0:
                            act.wait_ge(down_mm.sem, down_mm.after(g, e - 1))
                        nc.scalar.activation(HG[:, e % 2, f, :], PS[:, 4 + n % 4, 0:T], ACT.Gelu,
                                             bias=cm("bi", n, n + 1)).then_inc(gelu_ready.sem, 1)
                squares(2)
                act.wait_ge(bott_mm.sem, bott_mm.after(g, 1))
                nc.scalar.activation(HB[:, :], PS[0:BN, 0, 0:T], ACT.Identity, bias=cm("down_b", p=BN)).then_inc(bott_ready.sem, 1)
                for k, d in enumerate("fb"):
                    act.wait_ge(in_mm.sem, in_mm.after(g, k + 1))
                    nc.scalar.activation(XS[:, :], PS[:, 1, 0:PK], ACT.Copy).then_inc(in_copied.sem, 1)
                    nc.scalar.activation(ZS[:, :], PS[:, 2, 0:PK], ACT.Silu)
                    act.wait_ge(conv_ready.sem, conv_ready.after(g, k + 1))
                    nc.scalar.activation(UP[:, :], CV[:, :], ACT.Silu)
                    nc.scalar.activation(Xr[:, 0:HALF], CV[0:DR, T:PK], ACT.Silu)
                    nc.scalar.activation(Xr[:, HALF:T], CV[DR:128, T:PK], ACT.Silu).then_inc(u_ready.sem, 1)
                    act.wait_ge(dt24_mm.sem, dt24_mm.after(g, k + 1))
                    nc.scalar.activation(DT24[:, :], PS[0:RANK, 0, 0:T], ACT.Copy).then_inc(dt24_ready.sem, 1)
                    copy_set(2 + k, k, 1, None)
                    act.wait_ge(dt_mm.sem, dt_mm.after(g, k + 1))
                    nc.scalar.activation(DL[:, 0:T], PS[:, 2, 0:T], ACT.Identity, bias=cm(d + "dtb", 0, 1))
                    nc.scalar.activation(DL[:, T:PK], PS[:, 2, T:PK], ACT.Identity, bias=cm(d + "dtb", 1, 2)).then_inc(dt_raw.sem, 1)
                    act.wait_ge(abs_dt.sem, abs_dt.after(g, k + 1))
                    nc.scalar.activation(OM[:, :], TM[:, :], ACT.Exp, scale=-1.0).then_inc(exp_dt.sem, 1)
                    act.wait_ge(exp_dt.sem, exp_dt.after(g, k + 1))
                    nc.scalar.activation(LZ[:, :], OM[:, :], ACT.Ln, bias=1.0).then_inc(log_dt_ready.sem, 1)
                    act.wait_ge(w_ready.sem, w_ready.after(g, 2 + k))
                    for c in range(STEPS):
                        n = (1 + k) * STEPS + c
                        if c >= 2:
                            act.wait_ge(scanned.sem, scanned.after(g, n - 1))
                        for i in range(NC):
                            for h, cols in enumerate((slice(0, T), slice(T, PK))):
                                col = (2 * k + h) * NS + c * NC + i
                                last = nc.scalar.activation(dA[:, c % 2, i, cols], DL[:, cols], ACT.Exp,
                                                            scale=negA[:, col:col + 1])
                        last.then_inc(da_ready.sem, 1)
                    act.wait_ge(out_mm.sem, out_mm.after(g, k + 1))
                    nc.scalar.activation(YT[:, :], PS[0:BN, 0, 0:T], ACT.Copy).then_inc(out_copied.sem, 1)
                    act.wait_ge(bn_centred.sem, bn_centred.after(g, k + 1))
                    nc.scalar.activation(SQm[0:BN, :], Cm[0:BN, :], ACT.Square).then_inc(bn_squares.sem, 1)
                    act.wait_ge(bn_var.sem, bn_var.after(g, k + 1))
                    rstd(3 + k, PS[0:BN, 2, 0:T], BN)
                squares(3)
                logits(1, cm("er_b", p=EXPERTS))

        links = [0]
        CHAIN_PER_GROUP = 67

        @block.vector
        def _(dve):
            dve.wait_ge(s_sel, 16)
            nc.vector.tensor_copy(SEL[:, :], SELF[:, :]).then_inc(sel_ready, 1)
            dve.wait_ge(s_const[0], 32)
            nc.vector.tensor_scalar(negA[:, 0:2 * NS], cm("fAlog"), float(np.log(A_MAX)), None, ALU.min)
            nc.vector.tensor_scalar(negA[:, 2 * NS:4 * NS], cm("bAlog"), float(np.log(A_MAX)), None, ALU.min).then_inc(sel_ready, 1)
            dve.wait_ge(prep_act, 3)
            nc.vector.tensor_scalar(negA[:, :], negA[:, :], -1.0, -A_MIN, ALU.mult, ALU.min).then_inc(prep_act, 1)
            with dve.Fori(0, GROUPS) as g:
                links[0] = 0

                def link(ins):
                    links[0] += 1
                    ins.then_inc(chain, 1)
                    dve.wait_ge(chain, g * CHAIN_PER_GROUP + links[0])

                def centre_and_scale(i, li):
                    dve.wait_ge(ln_mean.sem, ln_mean.after(g, li + 1))
                    nc.vector.tensor_tensor(Cm[:, :], Hm[:, :], PS[:, 2, 0:T], ALU.subtract).then_inc(ln_centred.sem, 1)
                    nc.vector.tensor_tensor(Cr[:, :], Hr[:, :], PS[0:DR, 2, 0:T], ALU.subtract).then_inc(ln_centred.sem, 1)
                    dve.wait_ge(ln_rstd.sem, ln_rstd.after(g, i + 1))
                    nc.vector.tensor_tensor(Xm[:, :], Cm[:, :], RS[:, :], ALU.mult)
                    nc.vector.tensor_tensor(Xr[:, :], Cr[:, :], RS[0:DR, :], ALU.mult).then_inc(ln_x.sem, 1)

                def split_set(i, buf, is_abs=False):
                    dve.wait_ge(set_copied.sem, set_copied.after(g, 2 * i + 1))
                    if is_abs:
                        nc.vector.scalar_tensor_tensor(V[:, :], V[:, :], cm("sign"), V[:, :], ALU.mult, ALU.max).then_inc(abs_ready.sem, 1)
                    dve.wait_ge(set_copied.sem, set_copied.after(g, 2 * i + 2))
                    link(nc.vector.tensor_tensor(R[64:128, :], V[64:128, :], S3[64:128, buf, :], ALU.subtract))
                    link(nc.vector.tensor_copy(S3[64:128, buf, :], R[64:128, :]))
                    nc.vector.tensor_tensor(S3[96:128, buf, :], R[96:128, :], S3[96:128, buf, :], ALU.subtract).then_inc(set_ready.sem, 1)

                def gates(i):
                    L, q, oh1, oh2, L2, w = (gate[0:TW, j] for j in (0, 1, 2, 3, 4, 5))
                    m1, m2, gap, ratio, den, inv, w2, rk = (gs[0:TW, j] for j in range(8))

                    def over(ap):
                        return ap.unsqueeze(2).broadcast_to([TW, TILES, EXPERTS])

                    rank = cm("rank", p=TW).unsqueeze(1).broadcast_to([TW, TILES, EXPERTS])
                    dve.wait_ge(logits_T.sem, logits_T.after(g, i + 1))
                    link(nc.vector.tensor_copy(L, PS[0:TW, 1, 0:TILES * EXPERTS].rearrange("p (t e) -> p t e", e=EXPERTS)))

                    def pick(src, m, oh):
                        link(nc.vector.tensor_reduce(m, src, AX.X, ALU.max))
                        link(nc.vector.tensor_tensor(q, src, over(m), ALU.is_equal))
                        link(nc.vector.tensor_tensor(q, q, rank, ALU.mult))
                        link(nc.vector.tensor_reduce(rk, q, AX.X, ALU.max))
                        link(nc.vector.tensor_tensor(oh, q, over(rk), ALU.is_equal))

                    pick(L, m1, oh1)
                    link(nc.vector.scalar_tensor_tensor(L2, oh1, -3.0e38, L, ALU.mult, ALU.add))
                    pick(L2, m2, oh2)
                    nc.vector.tensor_tensor(gap, m2, m1, ALU.subtract).then_inc(gap_ready.sem, 1)
                    dve.wait_ge(ratio_ready.sem, ratio_ready.after(g, i + 1))
                    if i == 0:
                        link(nc.vector.tensor_scalar(den, ratio, 1.0, None, ALU.add))
                    else:
                        nc.vector.tensor_tensor(gate[0:TW, 6], L, over(m1), ALU.subtract).then_inc(shift_ready.sem, 1)
                        dve.wait_ge(shift_exp.sem, shift_exp.after(g, 1))
                        link(nc.vector.tensor_reduce(rk, gate[0:TW, 7], AX.X, ALU.add))
                        link(nc.vector.tensor_scalar(den, ratio, 1.0, None, ALU.add))
                        link(nc.vector.scalar_tensor_tensor(den, rk, 1e-9, den, ALU.mult, ALU.add))
                    link(nc.vector.reciprocal(inv, den))
                    link(nc.vector.tensor_tensor(w2, ratio, inv, ALU.mult))
                    link(nc.vector.tensor_tensor(oh1, oh1, over(inv), ALU.mult))
                    link(nc.vector.tensor_tensor(oh2, oh2, over(w2), ALU.mult))
                    nc.vector.tensor_tensor(w, oh1, oh2, ALU.add).then_inc(gates_ready.sem, 1)
                    dve.wait_ge(gates_T.sem, gates_T.after(g, i + 1))
                    nc.vector.tensor_copy(WTT[:, :], PS[0:EXPERTS, 2, 0:T]).then_inc(gates_T_ready.sem, 1)
                    dve.wait_ge(bias_mm.sem, bias_mm.after(g, i + 1))
                    nc.vector.tensor_copy(ACC[0:TW, 0:2, :], PS[0:TW, 0, 0:2 * D].rearrange("p (t n) -> p t n", n=D))
                    nc.vector.tensor_copy(ACC[0:TW, 2, :], PS[0:TW, 1, 0:D]).then_inc(acc_started.sem, 1)
                    dve.wait_ge(acc_started.sem, acc_started.after(g, i + 1))

                def add_back(i):
                    dve.wait_ge(back_T.sem, back_T.after(g, i + 1))
                    nc.vector.tensor_tensor(Hm[:, :], Hm[:, :], PS[:, 4, 0:T], ALU.add)
                    nc.vector.tensor_tensor(Hr[:, :], Hr[:, :], PS[0:DR, 5, 0:T], ALU.add).then_inc(residual.sem, 1)

                dve.wait_ge(prep_act, 3)
                dve.wait_ge(stored.sem, stored.after(g, 0) + 16)
                for k in range(2):
                    Hs, rows, pos, cls = ((Hm, 128, posb_m, "cls_m"), (Hr, DR, posb_r, "cls_r"))[k]
                    hv = seqs(Hs[:, :])
                    nc.vector.tensor_copy(hv[:, :, 0:2], cm(cls, p=rows).unsqueeze(1).broadcast_to([rows, IMG, 2]))
                    dve.wait_ge(tok_mm.sem, tok_mm.after(g, k + 1))
                    last = nc.vector.tensor_tensor(hv[:, :, 2:SEQ],
                                                   PS[0:rows, k, 0:IMG * NP].rearrange("p (b t) -> p b t", t=NP),
                                                   pos[:, :].unsqueeze(1).broadcast_to([rows, IMG, NP]), ALU.add)
                last.then_inc(residual.sem, 1)
                dve.wait_ge(residual.sem, residual.after(g, 1))
                centre_and_scale(0, 0)
                split_set(0, 0, is_abs=True)
                split_set(1, 1)
                dve.wait_ge(delta_ready.sem, delta_ready.after(g, 1))
                dve.wait_ge(packed_x.sem, packed_x.after(g, 1))
                link(nc.vector.tensor_scalar(OM[:, :], DL[:, :], -1.0, 1.0, ALU.mult, ALU.add))
                nc.vector.scalar_tensor_tensor(WV[:, 0:T], OM[:, 0:T], dt0[:, 0:1], UP[:, 0:T], ALU.mult, ALU.mult)
                link(nc.vector.scalar_tensor_tensor(WV[:, T:PK], OM[:, T:PK], dt0[:, 1:2], UP[:, T:PK], ALU.mult, ALU.mult))
                nc.vector.memset(seqs(DL[:, :])[:, :, 0:1], 0.0).then_inc(w_ready.sem, 1)

                def flat(ap, back):
                    ap = ap.rearrange("p n t -> p (n t)")
                    return ap[:, ::-1] if back else ap

                def scan_steps(k, back):
                    wb = WV[:, :].unsqueeze(1).broadcast_to([128, NC, PK])
                    for c in range(STEPS):
                        n = k * STEPS + c
                        dve.wait_ge(b_bc.sem, b_bc.after(g, n + 1))
                        nc.vector.tensor_tensor(BB[:, c % 2], wb, PS[:, 6:8, 0:PK], ALU.mult).then_inc(b_read.sem, 1)
                        dve.wait_ge(b_read.sem, b_read.after(g, n + 1))
                        dve.wait_ge(da_ready.sem, da_ready.after(g, n + 1))
                        if k == 0:
                            nc.vector.tensor_tensor(BB[:, c % 2], BB[:, c % 2], dA[:, c % 2], ALU.mult).then_inc(b_times_a.sem, 1)
                            dve.wait_ge(b_times_a.sem, b_times_a.after(g, c + 1))
                            dve.wait_ge(ap_ready.sem, ap_ready.after(g, c + 1))
                        decay = aP if k == 0 else dA
                        nc.vector.tensor_tensor_scan(flat(ST[:, :, :], back), flat(decay[:, c % 2], back),
                                                     flat(BB[:, c % 2], back), 0.0, ALU.mult, ALU.add).then_inc(scanned.sem, 1)
                        dve.wait_ge(scanned.sem, scanned.after(g, n + 1))
                        dve.wait_ge(c_bc.sem, c_bc.after(g, n + 1))
                        if c >= 2:
                            dve.wait_ge(summed.sem, summed.after(g, n - 1))
                        nc.vector.tensor_tensor(PR[:, c % 2], ST[:, :, :], PS[:, 0:2, 0:PK], ALU.mult).then_inc(prod_ready.sem, 1)
                    dve.wait_ge(summed.sem, summed.after(g, (k + 1) * STEPS))

                scan_steps(0, False)
                nc.vector.scalar_tensor_tensor(TM[:, 0:T], Xm[:, :], cm("D0", 0, 1), PS[:, 3, 0:T], ALU.mult, ALU.add)
                nc.vector.scalar_tensor_tensor(OM[0:DR, 0:HALF], Xr[:, 0:HALF], cm("D0", 1, 2, p=DR), PS[0:DR, 3, T:PK], ALU.mult, ALU.add)
                link(nc.vector.scalar_tensor_tensor(OM[0:DR, HALF:T], Xr[:, HALF:T], cm("D0", 1, 2, p=DR), PS[DR:128, 3, T:PK], ALU.mult, ALU.add))
                nc.vector.tensor_tensor(Hm[:, :], Hm[:, :], TM[:, 0:T], ALU.add)
                nc.vector.tensor_tensor(Hr[:, :], Hr[:, :], OM[0:DR, 0:T], ALU.add).then_inc(residual.sem, 1)
                dve.wait_ge(residual.sem, residual.after(g, 2))

                dve.wait_ge(s_const[1], 32)
                dve.wait_ge(s_const[2], 32)
                centre_and_scale(1, 1)
                gates(0)
                for e in range(EXPERTS):
                    dve.wait_ge(down_mm.sem, down_mm.after(g, e + 1))
                    if e:
                        dve.wait_ge(acc_done.sem, acc_done.after(g, TILES * e))
                    for t in range(TILES):
                        src = PS[0:TW, 2, t * D:(t + 1) * D] if t < 2 else PS[0:TW, 3, 0:D]
                        nc.vector.scalar_tensor_tensor(ACC[0:TW, t, :], src, gate[0:TW, 5, t, e:e + 1], ACC[0:TW, t, :],
                                                       ALU.mult, ALU.add).then_inc(acc_done.sem, 1)
                add_back(0)
                dve.wait_ge(residual.sem, residual.after(g, 3))

                centre_and_scale(2, 2)
                for k, d in enumerate("fb"):
                    back = d == "b"
                    dve.wait_ge(in_copied.sem, in_copied.after(g, k + 1))
                    for h, cols in enumerate((slice(0, T), slice(T, PK))):
                        last = nc.vector.tensor_scalar(CV[:, cols], XS[:, cols], cm(d + "cw", 4 * h + 3, 4 * h + 4),
                                                       cm(d + "cb", h, h + 1), ALU.mult, ALU.add)
                    link(last)
                    for s in range(1, 4):
                        for h, cols in enumerate((slice(0, T), slice(T, PK))):
                            src, dst = seqs(XS[:, cols]), seqs(CV[:, cols])
                            if back:
                                src, dst = src[:, :, s:SEQ], dst[:, :, 0:SEQ - s]
                            else:
                                src, dst = src[:, :, 0:SEQ - s], dst[:, :, s:SEQ]
                            last = nc.vector.scalar_tensor_tensor(dst, src, cm(d + "cw", 4 * h + 3 - s, 4 * h + 4 - s), dst,
                                                                  ALU.mult, ALU.add)
                        if s < 3:
                            link(last)
                        else:
                            last.then_inc(conv_ready.sem, 1)
                    split_set(2 + k, k)
                    dve.wait_ge(dt_raw.sem, dt_raw.after(g, k + 1))
                    nc.vector.scalar_tensor_tensor(TM[:, :], DL[:, :], -1.0, DL[:, :], ALU.mult, ALU.max).then_inc(abs_dt.sem, 1)
                    dve.wait_ge(exp_dt.sem, exp_dt.after(g, k + 1))
                    link(nc.vector.tensor_scalar(TM[:, :], OM[:, :], 1.0, -1.0, ALU.add, ALU.add))
                    dve.wait_ge(log_dt_ready.sem, log_dt_ready.after(g, k + 1))
                    link(nc.vector.tensor_tensor(OM[:, :], OM[:, :], TM[:, :], ALU.subtract))
                    link(nc.vector.tensor_tensor(OM[:, :], OM[:, :], LZ[:, :], ALU.add))
                    link(nc.vector.scalar_tensor_tensor(DL[:, :], DL[:, :], 0.0, OM[:, :], ALU.max, ALU.add))
                    link(nc.vector.tensor_tensor(WV[:, :], DL[:, :], UP[:, :], ALU.mult))
                    first = slice(SEQ - 1, SEQ) if back else slice(0, 1)
                    nc.vector.memset(seqs(DL[:, :])[:, :, first], RESTART).then_inc(w_ready.sem, 1)
                    scan_steps(1 + k, back)
                    nc.vector.scalar_tensor_tensor(TM[:, 0:T], UP[:, 0:T], cm(d + "Dp", 0, 1), PS[:, 3, 0:T], ALU.mult, ALU.add)
                    link(nc.vector.scalar_tensor_tensor(TM[:, T:PK], UP[:, T:PK], cm(d + "Dp", 1, 2), PS[:, 3, T:PK], ALU.mult, ALU.add))
                    nc.vector.tensor_tensor(CV[:, 0:T], TM[:, 0:T], ZS[:, 0:T], ALU.mult)
                    nc.vector.tensor_tensor(Cr[:, 0:HALF], TM[0:DR, T:PK], ZS[0:DR, T:PK], ALU.mult)
                    nc.vector.tensor_tensor(Cr[:, HALF:T], TM[DR:128, T:PK], ZS[DR:128, T:PK], ALU.mult).then_inc(y_gated.sem, 1)
                    dve.wait_ge(out_copied.sem, out_copied.after(g, k + 1))
                    dve.wait_ge(bn_mean.sem, bn_mean.after(g, k + 1))
                    nc.vector.tensor_tensor(Cm[0:BN, :], YT[:, :], PS[0:BN, 1, 0:T], ALU.subtract).then_inc(bn_centred.sem, 1)
                    dve.wait_ge(ln_rstd.sem, ln_rstd.after(g, 4 + k))
                    link(nc.vector.tensor_tensor(Cm[0:BN, :], Cm[0:BN, :], RS[0:BN, :], ALU.mult))
                    nc.vector.tensor_scalar(YS[:, k, :], Cm[0:BN, :], cm(d + "lng", 0, 1, p=BN), cm(d + "lng", 1, 2, p=BN),
                                            ALU.mult, ALU.add).then_inc(bn_done.sem, 1)
                dve.wait_ge(bn_done.sem, bn_done.after(g, 2))
                nc.vector.tensor_tensor(YS[:, 0, :], YS[:, 0, :], YS[:, 1, :], ALU.add).then_inc(y_sum.sem, 1)
                dve.wait_ge(up_proj.sem, up_proj.after(g, 1))
                nc.vector.scalar_tensor_tensor(Hm[:, :], PS[:, 4, 0:T], cm("up_b", 0, 1), Hm[:, :], ALU.add, ALU.add)
                nc.vector.scalar_tensor_tensor(Hr[:, :], PS[0:DR, 5, 0:T], cm("up_b", 1, 2, p=DR), Hr[:, :], ALU.add, ALU.add).then_inc(residual.sem, 1)
                dve.wait_ge(residual.sem, residual.after(g, 4))

                centre_and_scale(5, 3)
                gates(1)
                for t in range(TILES):
                    dve.wait_ge(lin_mm.sem, lin_mm.after(g, t + 1))
                    for e in range(EXPERTS):
                        n = t * EXPERTS + e
                        nc.vector.scalar_tensor_tensor(ACC[0:TW, t, :], PS[0:TW, 4 + e // 2, (e % 2) * D:(e % 2 + 1) * D],
                                                       gate[0:TW, 5, t, e:e + 1], ACC[0:TW, t, :],
                                                       ALU.mult, ALU.add).then_inc(lin_acc.sem, 1)
                        dve.wait_ge(lin_acc.sem, lin_acc.after(g, n + 1))
                add_back(1)
                assert links[0] == CHAIN_PER_GROUP, links[0]

        @block.tensor
        def _(pe):
            pe.wait_ge(prep_dve, 1)
            pe.wait_ge(sel_ready, 2)
            with pe.Fori(0, GROUPS) as g:
                def mm(out, lhsT, rhs, first, last):
                    return nc.tensor.matmul(out, lhsT, rhs, start=first, stop=last)

                def both(out, wm, wr, first=True, last=True):
                    mm(out, wm, Xm[:, :], first, False)
                    return mm(out, wr, Xr[:, :], False, last)

                def stats(li):
                    pe.wait_ge(residual.sem, residual.after(g, li + 1))
                    mm(PS[:, 2, 0:T], ones_d[:, :], Hm[:, :], True, False)
                    mm(PS[:, 2, 0:T], ones_d[0:DR, :], Hr[:, :], False, True).then_inc(ln_mean.sem, 1)
                    pe.wait_ge(ln_squares.sem, ln_squares.after(g, 2 * li + 2))
                    mm(PS[:, 3, 0:T], ones_d[:, :], SQm[:, :], True, False)
                    mm(PS[:, 3, 0:T], ones_d[0:DR, :], SQr[:, :], False, True).then_inc(ln_var.sem, 1)
                    pe.wait_ge(ln_x.sem, ln_x.after(g, li + 1))

                def broadcast(bank, buf, state):
                    for rows, cols, toks, _ in PARTS:
                        last = mm(PS[rows, bank, cols], SEL[:, state:state + 1].broadcast_to([128, rows.stop - rows.start]),
                                  S3[:, buf, toks], True, True)
                    return last

                def scan_steps(k, sets):
                    (bb, boff), (cb, coff) = sets

                    def spread(c):
                        n = k * STEPS + c
                        if k == 0:
                            if c:
                                pe.wait_ge(da_ready.sem, da_ready.after(g, c))
                            for i in range(NC):
                                last = broadcast(4 + i, 0, c * NC + i)
                            last.then_inc(a_bc.sem, 1)
                        if n:
                            pe.wait_ge(b_read.sem, b_read.after(g, n))
                        for i in range(NC):
                            last = broadcast(6 + i, bb, boff + c * NC + i)
                        last.then_inc(b_bc.sem, 1)
                        if n:
                            pe.wait_ge(prod_ready.sem, prod_ready.after(g, n))
                        for i in range(NC):
                            last = broadcast(i, cb, coff + c * NC + i)
                        last.then_inc(c_bc.sem, 1)

                    spread(0)
                    for c in range(STEPS):
                        if c + 1 < STEPS:
                            spread(c + 1)
                        pe.wait_ge(prod_ready.sem, prod_ready.after(g, k * STEPS + c + 1))
                        for i in range(NC):
                            last = mm(PS[:, 3, 0:PK], cm("ident"), PR[:, c % 2, i, :], c == 0 and i == 0,
                                      c == STEPS - 1 and i == NC - 1)
                        last.then_inc(summed.sem, 1)

                def gates(i, wm, wr, bias):
                    both(PS[0:EXPERTS, 0, 0:T], wm, wr).then_inc(logits_mm.sem, 1)
                    pe.wait_ge(logits_ready.sem, logits_ready.after(g, i + 1))
                    for t, a in enumerate(STARTS):
                        last = mm(PS[0:TW, 1, t * EXPERTS:(t + 1) * EXPERTS], LG[:, a:a + TW],
                                  cm("ident", 0, EXPERTS, p=EXPERTS), True, True)
                    last.then_inc(logits_T.sem, 1)
                    pe.wait_ge(gates_ready.sem, gates_ready.after(g, i + 1))
                    for t, a in enumerate(STARTS):
                        last = nc.tensor.transpose(PS[0:EXPERTS, 2, a:a + TW], gate[0:TW, 5, t, :], cm("ident", 0, TW, p=TW))
                    last.then_inc(gates_T.sem, 1)
                    pe.wait_ge(gates_T_ready.sem, gates_T_ready.after(g, i + 1))
                    for t, a in enumerate(STARTS):
                        out = PS[0:TW, 0, t * D:(t + 1) * D] if t < 2 else PS[0:TW, 1, 0:D]
                        last = mm(out, WTT[:, a:a + TW], bias, True, True)
                    last.then_inc(bias_mm.sem, 1)
                    pe.wait_ge(acc_started.sem, acc_started.after(g, i + 1))

                def back(i):
                    for t, a in enumerate(STARTS):
                        nc.tensor.transpose(PS[:, 4, a:a + TW], ACC[0:TW, t, 0:DM], cm("ident", 0, TW, p=TW))
                        last = nc.tensor.transpose(PS[0:DR, 5, a:a + TW], ACC[0:TW, t, DM:D], cm("ident", 0, TW, p=TW))
                    last.then_inc(back_T.sem, 1)

                pe.wait_ge(s_const[0], 32)
                pe.wait_ge(s_x, 16 * g + 16)
                for k, (lo, hi) in enumerate(((0, DM), (DM, D))):
                    for j in range(KP):
                        last = mm(PS[0:hi - lo, k, 0:IMG * NP], cm("tok_W", j * D + lo, j * D + hi), xp[:, j, :], j == 0, j == KP - 1)
                    last.then_inc(tok_mm.sem, 1)
                stats(0)
                for j in range(11):
                    a, b = j * 128, min(j * 128 + 128, 1344)
                    if j >= 4:
                        pe.wait_ge(hid_ready.sem, hid_ready.after(g, j - 3))
                    both(PS[0:b - a, 4 + j % 4, 0:T], cm("m1_w", a, b), cr("m1_w", a, b)).then_inc(hid_mm.sem, 1)
                for i, (name, first, count) in enumerate((("m2_w0", 0, 6), ("m2_w1", 6, 3))):
                    pe.wait_ge(hid_ready.sem, hid_ready.after(g, first + count))
                    for j in range(count):
                        last = mm(PS[:, i, 0:T], cm(name, j * NBLK, (j + 1) * NBLK), HID[:, first + j, :], j == 0, j == count - 1)
                    last.then_inc(set_mm.sem, 1)
                pe.wait_ge(hid_ready.sem, hid_ready.after(g, 11))
                for rows, cols, toks, feats in PARTS:
                    mm(PS[rows, 2, cols], cm("d_w2", feats.start, feats.stop), HID[:, 9, toks], True, False)
                    last = mm(PS[rows, 2, cols], cr("d_w2", feats.start, feats.stop), HIDr[:, toks], False, True)
                last.then_inc(delta_mm.sem, 1)
                pe.wait_ge(set_ready.sem, set_ready.after(g, 2))
                scan_steps(0, ((0, NS), (1, 0)))

                pe.wait_ge(s_const[1], 32)
                pe.wait_ge(s_const[2], 32)
                stats(1)
                gates(0, cm("r_w"), cr("r_w"), cm("bo", p=EXPERTS))

                def widen(e):
                    for f in range(FT):
                        n = e * FT + f
                        if n >= 4:
                            pe.wait_ge(gelu_ready.sem, gelu_ready.after(g, n - 3))
                        a = e * FFN + f * 128
                        both(PS[:, 4 + n % 4, 0:T], cm("wi", a, a + 128), cr("wi", a, a + 128)).then_inc(up_mm.sem, 1)

                widen(0)
                for e in range(EXPERTS):
                    if e + 1 < EXPERTS:
                        widen(e + 1)
                    pe.wait_ge(gelu_ready.sem, gelu_ready.after(g, (e + 1) * FT))
                    if e:
                        pe.wait_ge(acc_done.sem, acc_done.after(g, e * TILES))
                    for t, a in enumerate(STARTS):
                        out = PS[0:TW, 2, t * D:(t + 1) * D] if t < 2 else PS[0:TW, 3, 0:D]
                        for f in range(FT):
                            w = (e * FT + f) * D
                            last = mm(out, HG[:, e % 2, f, a:a + TW], cm("wo", w, w + D), f == 0, f == FT - 1)
                    last.then_inc(down_mm.sem, 1)
                pe.wait_ge(acc_done.sem, acc_done.after(g, EXPERTS * TILES))
                back(0)

                stats(2)
                both(PS[0:BN, 0, 0:T], cm("down"), cr("down")).then_inc(bott_mm.sem, 1)
                pe.wait_ge(bott_ready.sem, bott_ready.after(g, 1))
                for k, d in enumerate("fb"):
                    if k:
                        pe.wait_ge(ln_log.sem, ln_log.after(g, 4))
                    for z in range(2):
                        for rows, cols, toks, feats in PARTS:
                            last = mm(PS[rows, 1 + z, cols], cm(d + "in", z * D + feats.start, z * D + feats.stop, p=BN),
                                      HB[:, toks], True, True)
                    last.then_inc(in_mm.sem, 1)
                    pe.wait_ge(u_ready.sem, u_ready.after(g, k + 1))

                    def contract(out, name, main, n):
                        src, rest = main
                        mm(out, cm(name, 0, n), src, True, False)
                        return mm(out, cm(name + "_r", 0, n, p=DR), rest, False, True)

                    contract(PS[0:RANK, 0, 0:T], d + "xdt", (UP[:, 0:T], Xr[:, :]), RANK).then_inc(dt24_mm.sem, 1)
                    contract(PS[:, 1, 0:T], d + "xbc", (UP[:, 0:T], Xr[:, :]), NBLK).then_inc(set_mm.sem, 1)
                    pe.wait_ge(dt24_ready.sem, dt24_ready.after(g, k + 1))
                    for rows, cols, toks, feats in PARTS:
                        last = mm(PS[rows, 2, cols], cm(d + "dtw", feats.start, feats.stop, p=RANK), DT24[:, toks], True, True)
                    last.then_inc(dt_mm.sem, 1)
                    pe.wait_ge(set_ready.sem, set_ready.after(g, 3 + k))
                    scan_steps(1 + k, ((k, 0), (k, NS)))
                    pe.wait_ge(y_gated.sem, y_gated.after(g, k + 1))
                    contract(PS[0:BN, 0, 0:T], d + "out", (CV[:, 0:T], Cr[:, :]), BN).then_inc(out_mm.sem, 1)
                    pe.wait_ge(out_copied.sem, out_copied.after(g, k + 1))
                    mm(PS[0:BN, 1, 0:T], ones_bn[:, :], YT[:, :], True, True).then_inc(bn_mean.sem, 1)
                    pe.wait_ge(bn_squares.sem, bn_squares.after(g, k + 1))
                    mm(PS[0:BN, 2, 0:T], ones_bn[:, :], SQm[0:BN, :], True, True).then_inc(bn_var.sem, 1)
                pe.wait_ge(y_sum.sem, y_sum.after(g, 1))
                mm(PS[:, 4, 0:T], cm("up", 0, DM, p=BN), YS[:, 0, :], True, True)
                mm(PS[0:DR, 5, 0:T], cm("up", DM, D, p=BN), YS[:, 0, :], True, True).then_inc(up_proj.sem, 1)

                stats(3)
                gates(1, cm("er_w"), cr("er_w"), cm("eb", p=EXPERTS))
                for t, a in enumerate(STARTS):
                    if t:
                        pe.wait_ge(lin_acc.sem, lin_acc.after(g, t * EXPERTS))
                    for j in range(4):
                        mm(PS[0:TW, 4 + j, 0:2 * D], Xm[:, a:a + TW], cm("ew", 2 * j * D, 2 * (j + 1) * D), True, False)
                        last = mm(PS[0:TW, 4 + j, 0:2 * D], Xr[:, a:a + TW], cr("ew", 2 * j * D, 2 * (j + 1) * D), False, True)
                    last.then_inc(lin_mm.sem, 1)
                pe.wait_ge(lin_acc.sem, lin_acc.after(g, TILES * EXPERTS))
                back(1)


def _rows(a):
    a = np.asarray(a)
    return a.reshape(a.shape[0], -1)


def _main_rest(v):
    v = np.asarray(v).reshape(D, -1)
    return np.concatenate([v[0:DM], np.concatenate([v[DM:D], v[DM:D]])], axis=1)


def _state_columns(parts):
    rows = parts[0].shape[0]
    out = np.zeros((rows, 4, 2, NS), np.float32)
    for i, w in parts.items() if isinstance(parts, dict) else enumerate(parts):
        out[:, :, i, :] = np.asarray(w)[:, None, :]
    return out.reshape(rows, NBLK)


def _arrays(inp):
    I = {k: np.asarray(v) for k, v in inp.items()}
    x = I["x"].reshape(GROUPS, IMG, 3, GRID, 16, GRID, 16).transpose(0, 2, 4, 6, 1, 3, 5)
    x_p = np.ascontiguousarray(x.reshape(GROUPS, KP, 128, IMG * NP).transpose(0, 2, 1, 3))
    c128, c64 = np.zeros((128, C128), np.float32), np.zeros((DR, C64), np.float32)

    def put(name, a):
        a = _rows(a)
        at, width = AT[name]
        assert a.shape[1] == width, (name, a.shape, width)
        c128[0:a.shape[0], at:at + width] = a

    def put_both(name, w):
        w = _rows(w)
        put(name, w[0:DM])
        at, width = ATR[name]
        c64[:, at:at + width] = w[DM:D]

    put("tok_W", I["L0_tok_W"].reshape(KP, 128, D).transpose(1, 0, 2))
    near = np.arange(GRID) * 14 // GRID
    pos = I["L0_tok_positions"][0][:, near][:, :, near].reshape(D, NP)
    put("posm", pos[0:DM])
    put("posr", pos[DM:D])
    put("tok_b", _main_rest(I["L0_tok_b"]))
    cls = np.stack([I["cls_tok"][0, 0], I["L0_tok_cls_embedding"][0, 0]], axis=1)
    put("cls_m", cls[0:DM])
    put("cls_r", cls[DM:D])
    put("ident", np.eye(128, dtype=np.float32))
    put("log_dt", _main_rest(I["L0_attn_log_dt"]))
    row = np.arange(128) % 32
    put("sign", np.where(row < NS, -1.0, 1.0).astype(np.float32)[:, None])
    a = "L0_attn_"
    put_both("m1_w", np.concatenate([I[a + n + "_w1"] for n in "ABCd"], axis=1))
    b1 = np.concatenate([I[a + n + "_b1"] for n in "ABCd"])
    b1 = np.concatenate([b1, np.zeros(64, np.float32)]).reshape(11, 128).T
    put("m1_b", b1)
    none = np.zeros((128, NS), np.float32)
    w2 = {n: I[a + n + "_w2"].reshape(3, 128, NS) for n in "ABC"}
    put("m2_w0", np.stack([_state_columns([w2["A"][j], none]) for j in range(3)] +
                          [_state_columns([none, w2["B"][j]]) for j in range(3)], axis=1))
    put("m2_w1", np.stack([_state_columns([w2["C"][j], none]) for j in range(3)], axis=1))
    bias = [_state_columns([I[a + "A_b2"][None], I[a + "B_b2"][None]]), _state_columns([I[a + "C_b2"][None], none[0:1]])]
    put("m2_b", np.stack([b[0] for b in bias], axis=1))
    put_both("d_w2", I[a + "d_w2"])
    put("d_b2", _main_rest(I[a + "d_b2"]))
    put("D0", _main_rest(I[a + "D_param"]))
    put("rank", np.broadcast_to(np.arange(EXPERTS, 0, -1, dtype=np.float32), (128, EXPERTS)))
    put_both("r_w", I["L0_ffn_Wr"].T)
    put("bo", I["L0_ffn_bo"])
    put("bi", I["L0_ffn_bi"].reshape(EXPERTS * FT, 128).T)
    put_both("wi", I["L0_ffn_Wi"].transpose(2, 0, 1))
    put("wo", I["L0_ffn_Wo"].reshape(EXPERTS, D, FT, 128).transpose(3, 0, 2, 1))
    b = "L1_attn_"
    put_both("down", I[b + "down_W"])
    put("down_b", I[b + "down_b"][:, None])
    put("up", I[b + "up_W"])
    put("up_b", _main_rest(I[b + "up_b"]))
    for d in "fb":
        p = b + d + "_"
        put(d + "in", I[p + "in_W"])
        put(d + "cw", _main_rest(I[p + "conv_w"]))
        put(d + "cb", _main_rest(I[p + "conv_b"]))
        xw = _main_rest(I[p + "xproj_W"]).reshape(128, 2, RANK + 2 * NS)
        for h, tail in enumerate(("", "_r")):
            put(d + "xdt" + tail, xw[:, h, 0:RANK])
            put(d + "xbc" + tail, _state_columns([xw[:, h, RANK:RANK + NS], xw[:, h, RANK + NS:]]))
        put(d + "dtw", I[p + "dt_W"])
        put(d + "dtb", _main_rest(I[p + "dt_b"]))
        put(d + "Alog", _main_rest(I[p + "A_log"]))
        put(d + "Dp", _main_rest(I[p + "D"]))
        ow = _main_rest(I[p + "out_W"]).reshape(128, 2, BN)
        put(d + "out", ow[:, 0])
        put(d + "out_r", ow[:, 1])
        put(d + "lng", np.stack([I[p + "ln_g"], I[p + "ln_b"]], axis=1))
    put_both("er_w", I["L1_ffn_router_w"].T)
    put("er_b", I["L1_ffn_router_b"][:, None])
    put_both("ew", I["L1_ffn_expert_w"].transpose(2, 0, 1))
    put("eb", I["L1_ffn_expert_b"])
    r, n = np.arange(128)[:, None], np.arange(2 * NS)[None, :]
    sel = ((r % 32 == n) & (r // 32 != 1)).astype(np.float32)
    return {"x_p": x_p, "c128": c128, "c64": c64, "sel_d": sel}


def kernel(**inputs):
    import concourse.bacc as bacc
    from concourse.bass_utils import run_bass_kernel_spmd

    nc = bacc.Bacc("TRN2", target_bir_lowering=False, num_devices=1)
    arrays = _arrays(inputs)
    args = [nc.dram_tensor(n, a.shape, mybir.dt.from_np(a.dtype), kind="ExternalInput").ap() for n, a in arrays.items()]
    out_m = nc.dram_tensor("out_m", (GROUPS, DM, T), mybir.dt.float32, kind="ExternalOutput").ap()
    out_r = nc.dram_tensor("out_r", (GROUPS, DR, T), mybir.dt.float32, kind="ExternalOutput").ap()
    vit_tower(nc, *args, out_m, out_r)
    got = run_bass_kernel_spmd(nc, [arrays], core_ids=[0]).results[0]
    both = np.concatenate([got["out_m"], got["out_r"]], axis=1).reshape(GROUPS, D, IMG, SEQ)
    return np.ascontiguousarray(both.transpose(0, 2, 3, 1).reshape(BATCH, SEQ, D))
```

```python
import numpy as np
import concourse.bass as bass
from concourse import mybir
from contextlib import ExitStack

BATCH, SEQ, D = 32, 38, 192
GROUPS = 4
IMG = BATCH // GROUPS
T = IMG * SEQ
HALF = T // 2
GRID = 6
NP = GRID * GRID
KP, PDIM = 6, 128
DM, DR = 128, 64
PK = T + HALF
NSEQ = PK // SEQ
NS = 16
NC = 2
STEPS = NS // NC
EXPERTS, FFN = 8, 768
FT = FFN // 128
BN, RANK = 96, 24
TILES, TW = 3, 102
STARTS = (0, 101, 202)
EPS = 1e-5
A_MIN, A_MAX = 1e-13, 3e22
RESTART = 1e16
PAIRS = GROUPS * TILES * TW * 2
CAP_BLOCKS = -(-GROUPS * TILES * TW // 128)
BLOCKS = (PAIRS + EXPERTS * 127) // 128
assert BLOCKS % 3 == 0
SCATTERS = 16 * (2 * TILES + 1)
M_CHAIN = 17
NBLK = 128


def _layout(widths):
    at, out = 0, {}
    for name, width in widths:
        out[name] = (at, width)
        at += width
    return out, at


W128 = [
    ("tok_W", KP * D), ("posm", NP), ("posr", NP), ("tok_b", 2), ("cls_m", 2), ("cls_r", 2),
    ("ident", 128), ("log_dt", 2), ("sign", 1), ("fAlog", 2 * NS), ("bAlog", 2 * NS),
    ("m1_w", 1344), ("m1_b", 11), ("m2_w0", 6 * NBLK), ("m2_w1", 3 * NBLK), ("m2_b", 2),
    ("d_w2", D), ("d_b2", 2), ("D0", 2), ("rank", EXPERTS),
    ("r_w", EXPERTS), ("eoff", EXPERTS), ("blk", CAP_BLOCKS), ("below", EXPERTS * EXPERTS), ("bid", BLOCKS), ("tri", TW),
    ("down", BN), ("down_b", 1), ("up", D), ("up_b", 2),
]
for _d in "fb":
    W128 += [(_d + "in", 2 * D), (_d + "cw", 8), (_d + "cb", 2), (_d + "xdt", RANK), (_d + "xbc", NBLK),
             (_d + "xdt_r", RANK), (_d + "xbc_r", NBLK), (_d + "dtw", D), (_d + "dtb", 2),
             (_d + "Dp", 2), (_d + "out", BN), (_d + "out_r", BN), (_d + "lng", 2)]
W128 += [("er_w", EXPERTS), ("er_b", 1), ("ew", EXPERTS * D), ("eb", D)]
AT, C128 = _layout(W128)
W64 = [("m1_w", 1344), ("d_w2", D), ("r_w", EXPERTS), ("down", BN),
       ("er_w", EXPERTS), ("ew", EXPERTS * D)]
ATR, C64 = _layout(W64)
SEG128 = [0, AT["rank"][0], AT["down"][0], C128]
SEG64 = [0, ATR["r_w"][0], ATR["down"][0], C64]


class Signal:

    def __init__(self, sem, per_group, start=0):
        self.sem, self.per_group, self.start = sem, per_group, start

    def after(self, g, k):
        return g * self.per_group + (self.start + k)


def later(signal):
    return Signal(signal.sem, signal.per_group, GROUPS * signal.per_group)


class Stage:
    pass


def vit_tower(nc, x_p, c128, c64, sel_d, ex_m, ex_r, ex_b, out_m, out_r):
    fp32, bf16, i32, u32 = mybir.dt.float32, mybir.dt.bfloat16, mybir.dt.int32, mybir.dt.uint32
    ALU, ACT, AX = mybir.AluOpType, mybir.ActivationFunctionType, mybir.AxisListType
    with ExitStack() as ctx:
        def sb(name, shape, dt=fp32):
            return ctx.enter_context(nc.sbuf_tensor(name, shape, dt))

        def sem(name):
            return ctx.enter_context(nc.semaphore(name))

        def sig(name, per_group):
            return Signal(sem(name), per_group)

        CM = sb("CM", [128, C128])
        CR = sb("CR", [DR, C64])
        SELF = sb("SELF", [128, 2 * NS])
        SEL = sb("SEL", [128, 2 * NS], bf16)
        ones_d = sb("ones_d", [128, 128])
        ones_bn = sb("ones_bn", [BN, BN])
        eps_col = sb("eps_col", [128, 1])
        posb_m = sb("posb_m", [128, NP])
        posb_r = sb("posb_r", [DR, NP])
        dt0 = sb("dt0", [128, 2])
        neg_dt0 = sb("neg_dt0", [128, 2])
        negA = sb("negA", [128, 4 * NS])

        def cm(name, a=0, b=None, p=128, p0=0):
            at, width = AT[name]
            return CM[p0:p, at + a:at + (width if b is None else b)]

        def cr(name, a=0, b=None):
            at, width = ATR[name]
            return CR[:, at + a:at + (width if b is None else b)]

        WX = sb("WX", [128, 3, FFN + FT * D + FT])
        WXR = sb("WXR", [DR, 3, FFN])
        WXB = sb("WXB", [1, 3, D])
        ones_row = sb("ones_row", [1, 128])
        ones_tw = sb("ones_tw", [TW, TW])

        P, M, Q = Stage(), Stage(), Stage()
        L = Stage()
        FW, BW = Stage(), Stage()
        PREP, GATED, NORM = Stage(), Stage(), Stage()

        def residual_buffers(s, name):
            s.Hm, s.Hr = sb(name + "_Hm", [128, T]), sb(name + "_Hr", [DR, T])
            s.Xm, s.Xr = sb(name + "_Xm", [128, T]), sb(name + "_Xr", [DR, T])

        def norm_buffers(s, name):
            s.Cm, s.Cr = sb(name + "_Cm", [128, T]), sb(name + "_Cr", [DR, T])
            s.VE = sb(name + "_VE", [128, T])
            s.RS = sb(name + "_RS", [128, T])
            s.SQm = s.RS[:, :]
            s.SQr = sb(name + "_SQr", [DR, T])

        def gate_buffers(s, name):
            s.LW = sb(name + "_LW", [EXPERTS, T])
            s.gate = sb(name + "_gate", [128, 8, TILES, EXPERTS])
            s.gs = sb(name + "_gs", [128, 8, TILES])
            s.ACC = sb(name + "_ACC", [128, TILES, D])

        def scan_buffers(s, name, sets):
            s.V = sb(name + "_V", [NBLK, T])
            s.R = sb(name + "_R", [NBLK, T])
            s.S3 = sb(name + "_S3", [NBLK, sets, T], bf16)
            s.DL = sb(name + "_DL", [128, PK])
            s.UP = sb(name + "_UP", [128, PK])
            s.OM = sb(name + "_OM", [128, PK])
            s.WV = sb(name + "_WV", [128, PK])
            s.TM = sb(name + "_TM", [128, PK])

        for s, name in ((P, "p"), (M, "m"), (Q, "q")):
            residual_buffers(s, name)
        norm_buffers(P, "p")
        M.Cm, M.Cr, M.VE, M.RS, M.SQm, M.SQr = P.Cm, P.Cr, P.VE, P.RS, P.SQm, P.SQr
        norm_buffers(Q, "q")
        gate_buffers(M, "m")
        gate_buffers(Q, "q")
        scan_buffers(P, "p", 2)
        scan_buffers(Q, "q", 1)
        xp = sb("xp", [128, KP, IMG * NP])
        HID = sb("HID", [128, 10, T])
        HIDr = sb("HIDr", [DR, T])
        HB = sb("HB", [BN, T])
        ZS = sb("ZS", [128, PK])
        YS = sb("YS", [BN, 2, T])
        Om = sb("Om", [128, T])
        Or = sb("Or", [DR, T])
        dA = sb("dA", [128, 2, NC, PK])
        aP = sb("aP", [128, 2, NC, PK])
        BB = sb("BB", [128, 2, NC, PK])
        PR = sb("PR", [128, 2, NC, PK])
        ST = sb("ST", [128, NC, PK])
        KEEP = sb("KEEP", [TW, TILES, 2 * EXPERTS + 4])
        run = sb("run", [TW, EXPERTS])
        slot_u = sb("slot_u", [TW, TILES, 2], u32)
        counts = sb("counts", [TW, 6, EXPERTS])
        steps80 = sb("steps80", [TW, EXPERTS, CAP_BLOCKS])
        block_f = sb("block_f", [TW, 5, BLOCKS])
        passed = sb("passed", [TW, 2, BLOCKS, EXPERTS])
        tab_rows = sb("tab_rows", [1, BLOCKS], i32)
        tab_expert = sb("tab_expert", [1, BLOCKS], i32)
        XTm = sb("XTm", [128, 3, 128])
        XTr = sb("XTr", [DR, 3, 128])
        YSUM = HID[:, :, :].rearrange("p j t -> p (j t)")[:, 3 * T:3 * T + PK]
        PAIR = xp[:, :, :].rearrange("p k t -> p (k t)")[:, 2 * TILES * D:2 * TILES * D + PK]
        HX = HID[:, :, :].rearrange("p j t -> p (j t)")[:, 0:3 * FT * 128].rearrange("p (b f t) -> p b f t", f=FT, t=128)
        XB, YB = (xp[:, :, :].rearrange("p k t -> p (k t)")[:, j * 3 * D:(j + 1) * 3 * D].rearrange("p (b n) -> p b n", n=D)
                  for j in range(2))
        GA = xp[0:TW, :, :].rearrange("p k t -> p (k t)")[:, 0:2 * TILES * D].rearrange("p (t k n) -> p t k n", k=2, n=D)
        XTOK = M.ACC
        ZERO = WX[:, 0, 0:CAP_BLOCKS * EXPERTS * D // 8]
        XS = aP[:, 0, 0, :]
        LZ = aP[:, 0, 1, :]
        DT24 = aP[0:RANK, 1, 1, 0:T]
        for s, src, z, ur, gr in ((FW, Q, ZS[:, :], P.Xr[:, :], HIDr[:, :]),
                                  (BW, P, aP[:, 1, 0, :], P.Xm[0:DR, :], HID[0:DR, 2, :])):
            s.V, s.R, s.S3, s.DL, s.UP, s.OM, s.WV, s.TM = src.V, src.R, src.S3, src.DL, src.UP, src.OM, src.WV, src.TM
            s.CV = src.WV[:, :]
            s.YT = src.V[0:BN, :]
            s.ZS, s.URr, s.GRr = z, ur, gr
        DIRS = (FW, BW)
        L.Cm, L.Cr, L.VE, L.RS, L.SQm, L.SQr, L.Xm, L.Xr = P.Cm, P.Cr, P.VE, P.RS, P.SQm, P.SQr, M.Xm, M.Xr
        L.Hm, L.Hr = P.Hm, P.Hr
        HBm, HBr = HID[:, 0, :], HID[0:DR, 1, :]

        PS = ctx.enter_context(nc.psum_tensor("PS", [128, 8, 512], fp32))
        B_BANK, C_BANK, Y_BANK, A_BANK = 0, 2, 4, 5
        X_BANK, Z_BANK, AFTER_BANK = 6, (5, 7), (7, 5)

        slots_d = nc.dram_tensor("slots_d", [EXPERTS * CAP_BLOCKS * 128, D], fp32, kind="Internal").ap()
        outs_d = nc.dram_tensor("outs_d", [BLOCKS * 128, D], fp32, kind="Internal").ap()
        h_md = nc.dram_tensor("h_md", [GROUPS, DM, T], fp32, kind="Internal").ap()
        h_rd = nc.dram_tensor("h_rd", [GROUPS, DR, T], fp32, kind="Internal").ap()
        keep_d = nc.dram_tensor("keep_d", [GROUPS, TW, TILES * (2 * EXPERTS + 4)], fp32, kind="Internal").ap()

        s_const = [sem(f"s_const{i}") for i in range(3)]
        s_sel = sem("s_sel")
        s_x = sem("s_x")
        turn_taken = sem("turn_taken")
        s_zero = sem("s_zero")
        h_stored, scattered, scatter_free = sig("h_stored", 32), sig("scattered", SCATTERS), sig("scatter_free", 1)
        s_block = [sem(f"s_block{i}") for i in range(3)]
        s_weights = [sem(f"s_weights{i}") for i in range(3)]
        out_rows = [sem(f"out_rows{i}") for i in range(3)]
        h_loaded, keep_loaded, gathered = sig("h_loaded", 32), sig("keep_loaded", 16), sig("gathered", 16 * 2 * TILES)
        stored, out_free = sig("stored", 32), sig("out_free", 1)
        sel_ready, prep_pool, prep_act = sem("sel_ready"), sem("prep_pool"), sem("prep_act")

        def norm_signals(s, n, count):
            s.ln_mean, s.ln_var = sig(n + "_ln_mean", count), sig(n + "_ln_var", count)
            s.ln_centred, s.ln_squares = sig(n + "_ln_centred", 2 * count), sig(n + "_ln_squares", 2 * count)
            s.ln_log, s.ln_rstd, s.ln_x = sig(n + "_ln_log", count), sig(n + "_ln_rstd", count), sig(n + "_ln_x", count)

        def gate_signals(s, n):
            s.logits_mm, s.logits_ready, s.logits_T = sig(n + "_logits_mm", 1), sig(n + "_logits_ready", 1), sig(n + "_logits_T", 1)
            s.gap_ready, s.ratio_ready = sig(n + "_gap_ready", 1), sig(n + "_ratio_ready", 1)
            s.gates_ready, s.gates_T, s.gates_T_ready = sig(n + "_gates_ready", 1), sig(n + "_gates_T", 1), sig(n + "_gates_T_ready", 1)
            s.bias_mm, s.acc_started, s.back_T = sig(n + "_bias_mm", 1), sig(n + "_acc_started", 1), sig(n + "_back_T", 1)

        def scan_signals(s, n, count):
            s.set_mm, s.set_copied, s.set_ready = sig(n + "_set_mm", 2), sig(n + "_set_copied", 4), sig(n + "_set_ready", 2)
            s.b_bc, s.c_bc, s.da_ready, s.b_read = (sig(n + x, count * STEPS) for x in ("_b_bc", "_c_bc", "_da_ready", "_b_read"))
            s.scanned, s.prod_ready, s.summed = (sig(n + x, count * STEPS) for x in ("_scanned", "_prod_ready", "_summed"))
            s.w_ready = sig(n + "_w_ready", count)

        norm_signals(P, "p", 1)
        norm_signals(M, "m", 1)
        for s, was in ((L, M), (Q, P)):
            s.ln_mean, s.ln_var, s.ln_centred, s.ln_squares = (later(x) for x in (was.ln_mean, was.ln_var, was.ln_centred, was.ln_squares))
            s.ln_log, s.ln_rstd, s.ln_x = later(was.ln_log), later(was.ln_rstd), later(was.ln_x)
        gate_signals(M, "m")
        gate_signals(Q, "q")
        scan_signals(P, "p", 1)
        scan_signals(Q, "q", 2)
        for s in (FW, BW):
            s.set_mm, s.set_copied, s.set_ready = Q.set_mm, Q.set_copied, Q.set_ready
            s.b_bc, s.c_bc, s.da_ready, s.b_read = Q.b_bc, Q.c_bc, Q.da_ready, Q.b_read
            s.scanned, s.prod_ready, s.summed = Q.scanned, Q.prod_ready, Q.summed
        P.residual, M.residual, Q.residual = sig("p_residual", 2), sig("m_residual", 1), sig("q_residual", 1)
        P.chain, M.chain, Q.chain = sig("p_chain", 7), sig("m_chain", M_CHAIN), sig("q_chain", 19)
        PREP.chain, GATED.chain, NORM.chain = sig("prep_chain", 20), sig("gated_chain", 2), sig("norm_chain", 2)
        P.work, FW.work, BW.work = P, PREP, PREP
        hb_copied = sig("hb_copied", 1)
        xtok_mm, xtok_copied = sig("xtok_mm", 2), sig("xtok_copied", 1)
        pair_ready, ranks_mm, slots_ready = sig("pair_ready", 1), sig("ranks_mm", 1), sig("slots_ready", 1)
        table, table_ready = sem("table"), sem("table_ready")
        t_mm, xt_copied, wide_mm, gelu_ready = sig("t_mm", 1), sig("xt_copied", 1), sig("wide_mm", 2), sig("gelu_ready", 2)
        narrow_mm, y_copied = sig("narrow_mm", 1), sig("y_copied", 1)
        rows_ready, rows_chain, mixed = sig("rows_ready", 1), sig("rows_chain", 3), sig("mixed", TILES)
        final = Signal(sem("final"), 1, start=1)
        y_added = sig("y_added", 2 * STEPS)
        tok_mm = sig("tok_mm", 2)
        hid_mm, hid_ready = sig("hid_mm", 11), sig("hid_ready", 11)
        abs_ready = sig("abs_ready", 1)
        delta_mm, delta_ready, packed_x = sig("delta_mm", 1), sig("delta_ready", 1), sig("packed_x", 1)
        a_bc = sig("a_bc", STEPS)
        ap_ready, b_times_a = sig("ap_ready", STEPS), sig("b_times_a", STEPS)
        lin_mm, lin_acc = sig("lin_mm", TILES * EXPERTS // 2), sig("lin_acc", TILES * EXPERTS)
        shift_ready, shift_exp = sig("shift_ready", 1), sig("shift_exp", 1)
        bott_mm, bott_ready = sig("bott_mm", 1), sig("bott_ready", 1)
        in_mm, in_copied, conv_ready, u_ready = sig("in_mm", 2), sig("in_copied", 2), sig("conv_ready", 2), sig("u_ready", 2)
        dt24_mm, dt24_ready, dt_mm, dt_raw = sig("dt24_mm", 2), sig("dt24_ready", 2), sig("dt_mm", 2), sig("dt_raw", 2)
        abs_dt, exp_dt, log_dt_ready = sig("abs_dt", 2), sig("exp_dt", 2), sig("log_dt_ready", 2)
        y_gated, out_mm, out_copied = sig("y_gated", 2), sig("out_mm", 2), sig("out_copied", 2)
        bn_mean, bn_centred, bn_squares, bn_var = sig("bn_mean", 2), sig("bn_centred", 2), sig("bn_squares", 2), sig("bn_var", 2)
        bn_log, bn_rstd, bn_done = sig("bn_log", 2), sig("bn_rstd", 2), sig("bn_done", 2)
        y_sum, up_proj = sig("y_sum", 1), sig("up_proj", 1)

        block = ctx.enter_context(nc.Block())

        TURN_BANK, OUT_BANK, WIDE_BANK = 0, 1, 2
        HALF_FT = FT // 2

        def seqs(ap):
            return ap.rearrange("p (s t) -> p s t", t=SEQ)

        PARTS = [(slice(0, 128), slice(0, T), slice(0, T), slice(0, DM)),
                 (slice(0, DR), slice(T, PK), slice(0, HALF), slice(DM, D)),
                 (slice(DR, 128), slice(T, PK), slice(HALF, T), slice(DM, D))]
        MAIN_REST = (slice(0, T), slice(T, PK))

        def first_pass(eng, body):
            body(0, None)
            with eng.Fori(1, GROUPS) as i:
                body(i, i - 1)
            body(None, GROUPS - 1)

        def over_blocks(eng, body):
            for p in range(3):
                body(0, p)
            with eng.Fori(1, BLOCKS // 3 - 1) as i:
                for p in range(3):
                    body(i, p)
            for p in range(3):
                body(BLOCKS // 3 - 1, p)

        def second_pass(eng, part_a, part_b):
            part_b(None, None, 0)
            part_a(0, None)
            part_b(0, None, 1)
            with eng.Fori(1, GROUPS - 1) as g:
                part_a(g, g - 1)
                part_b(g, g - 1, g + 1)
            part_a(GROUPS - 1, GROUPS - 2)
            part_b(GROUPS - 1, GROUPS - 2, None)
            part_a(None, GROUPS - 1)
            part_b(None, GROUPS - 1, None)

        def follower(i, p):
            return (i, p + 1) if p < 2 else (i + 1, 0)

        def previous(i, p):
            return (i, p - 1) if p else (i - 1, 2)

        def is_end(b):
            return isinstance(b, int) and b == BLOCKS - 1

        def early(b, n):
            return isinstance(b, int) and b < n

        def is_first(g):
            return isinstance(g, int) and g == 0

        def at_start(s, g, c):
            return c == 0 and (s is P or s is FW and is_first(g))

        def is_last(g):
            return isinstance(g, int) and g == GROUPS - 1

        @block.sync
        def _(sp):
            sp.dma_start(xp[:, :, :], x_p[0, :, :, :]).then_inc(s_x, 16)

            for i in range(3):
                a, b = SEG128[i], SEG128[i + 1]
                sp.dma_start(CM[:, a:b], c128[:, a:b]).then_inc(s_const[i], 16)
                a, b = SEG64[i], SEG64[i + 1]
                sp.dma_start(CR[:, a:b], c64[:, a:b]).then_inc(s_const[i], 16)
            sp.wait_ge(prep_pool, 2)
            zeros = slots_d.rearrange("(p j r) n -> p j (r n)", p=128, j=8)
            for j in range(8):
                sp.dma_start(zeros[:, j, :], ZERO).then_inc(s_zero, 16)

            def first(gP, gM):
                if gM is not None:
                    sp.wait_ge(P.residual.sem, P.residual.after(gM, 2))
                    sp.dma_start(h_md[bass.ds(gM, 1), :, :].rearrange("g p t -> p (g t)"), P.Hm[:, :]).then_inc(h_stored.sem, 16)
                    sp.dma_start(h_rd[bass.ds(gM, 1), :, :].rearrange("g p t -> p (g t)"), P.Hr[:, :]).then_inc(h_stored.sem, 16)
                if gP is not None and not is_last(gP):
                    sp.wait_ge(tok_mm.sem, tok_mm.after(gP, 2))
                    sp.dma_start(xp[:, :, :], x_p[bass.ds(gP + 1, 1), :, :, :].rearrange("g p k t -> p (g k) t")).then_inc(s_x, 16)

            first(0, None)
            with sp.Fori(1, GROUPS - 1) as i:
                first(i, i - 1)
            first(GROUPS - 1, GROUPS - 2)
            first(None, GROUPS - 1)

            sp.wait_ge(table_ready, 1)
            sp.wait_ge(s_zero, 128)
            sp.wait_ge(scattered.sem, scattered.after(GROUPS, 0))

            def load_block(i, p):
                b = 3 * i + p
                place = sp.value_load(tab_rows[0:1, bass.ds(b, 1)], min_val=0, max_val=EXPERTS * CAP_BLOCKS - 1)
                expert = sp.value_load(tab_expert[0:1, bass.ds(b, 1)], min_val=0, max_val=EXPERTS - 1)
                if not early(b, 3):
                    sp.wait_ge(t_mm.sem, t_mm.after(b - 3, 1))
                sp.dma_start(XB[:, p, :], slots_d.rearrange("(a r) n -> a r n", r=128)[bass.ds(place, 1), :, :].rearrange("a r n -> r (a n)")).then_inc(s_block[p], 16)
                if not early(b, 3):
                    sp.wait_ge(narrow_mm.sem, narrow_mm.after(b - 3, 1))
                sp.dma_start(WX[:, p, :], ex_m[bass.ds(expert, 1), :, :].rearrange("e p n -> p (e n)")).then_inc(s_weights[p], 16)
                sp.dma_start(WXR[:, p, :], ex_r[bass.ds(expert, 1), :, :].rearrange("e p n -> p (e n)")).then_inc(s_weights[p], 16)
                sp.dma_start(WXB[:, p, :], ex_b[bass.ds(expert, 1), :, :].rearrange("e p n -> p (e n)")).then_inc(s_weights[p], 16)

            over_blocks(sp, load_block)

            def load_keep(g):
                sp.dma_start(KEEP[:, :, :].rearrange("p t n -> p (t n)"), keep_d[bass.ds(g, 1), :, :].rearrange("g p n -> p (g n)")).then_inc(keep_loaded.sem, 16)

            def load_h(g):
                sp.dma_start(M.Hm[:, :], h_md[bass.ds(g, 1), :, :].rearrange("g p t -> p (g t)")).then_inc(h_loaded.sem, 16)
                sp.dma_start(M.Hr[:, :], h_rd[bass.ds(g, 1), :, :].rearrange("g p t -> p (g t)")).then_inc(h_loaded.sem, 16)

            load_keep(0)
            sp.wait_ge(h_stored.sem, h_stored.after(GROUPS, 0))
            load_h(0)

            with sp.Fori(0, GROUPS - 1) as g:
                sp.wait_ge(mixed.sem, mixed.after(g, TILES))
                load_keep(g + 1)
                sp.wait_ge(M.residual.sem, M.residual.after(g, 1))
                load_h(g + 1)

        @block.gpsimd
        def _(pool):
            pool.sem_inc(out_free.sem, 1)
            nc.gpsimd.memset(ones_d[:, :], 1.0 / D)
            nc.gpsimd.memset(ones_bn[:, :], 1.0 / BN)
            pool.sem_inc(final.sem, 1)
            pool.sem_inc(scatter_free.sem, 1)
            nc.gpsimd.memset(ones_row[:, :], 1.0)
            nc.gpsimd.memset(ones_tw[:, :], 1.0)
            nc.gpsimd.memset(eps_col[:, :], EPS).then_inc(prep_pool, 1)
            nc.gpsimd.memset(ZERO, 0.0).then_inc(prep_pool, 1)

            def first(gP, gM):
                if gM is not None:
                    pool.wait_ge(s_zero, 128)
                    pool.wait_ge(xtok_copied.sem, xtok_copied.after(gM, 1))
                    pool.wait_ge(slots_ready.sem, slots_ready.after(gM, 1))
                    pool.sem_inc(turn_taken, 1)
                    for t in range(TILES):
                        for k in range(2):
                            pool.indirect_dma_start(slots_d[:, :], bass.IndirectOffsetOnAxis(slot_u[:, t, k:k + 1], 0),
                                                    XTOK[0:TW, t, :], None).then_inc(scattered.sem, 16)
                    pool.dma_start(keep_d[bass.ds(gM, 1), :, :].rearrange("g p n -> p (g n)"),
                                   KEEP[:, :, :].rearrange("p t n -> p (t n)")).then_inc(scattered.sem, 16)
                if gP is not None:
                    pool.wait_ge(P.w_ready.sem, P.w_ready.after(gP, 1))
                    for c in range(STEPS):
                        pool.wait_ge(P.da_ready.sem, P.da_ready.after(gP, c + 1))
                        if c >= 2:
                            pool.wait_ge(P.scanned.sem, P.scanned.after(gP, c - 1))
                        nc.gpsimd.tensor_tensor(aP[:, c % 2], dA[:, c % 2],
                                                P.DL[:, :].unsqueeze(1).broadcast_to([128, NC, PK]),
                                                ALU.mult).then_inc(ap_ready.sem, 1)
                if gM is not None:
                    pool.wait_ge(scattered.sem, scattered.after(gM, SCATTERS))
                    pool.sem_inc(scatter_free.sem, 1)

            first_pass(pool, first)

            def store_block(i, p):
                b = 3 * i + p
                pool.wait_ge(y_copied.sem, y_copied.after(b, 1))
                pool.dma_start(outs_d.rearrange("(b r) n -> b r n", r=128)[bass.ds(b, 1), :, :].rearrange("b r n -> r (b n)"), YB[:, p, :]).then_inc(out_rows[p], 16)

            over_blocks(pool, store_block)
            for p in range(3):
                pool.wait_ge(out_rows[p], 16 * (BLOCKS // 3))

            def gather(g, tiles):
                for t in tiles:
                    for k in range(2):
                        pool.indirect_dma_start(GA[:, t, k, :], None, outs_d[:, :],
                                                bass.IndirectOffsetOnAxis(slot_u[:, t, k:k + 1], 0)).then_inc(gathered.sem, 16)

            pool.wait_ge(rows_ready.sem, 1)
            gather(0, range(TILES))

            def sum_step(g, k, c):
                n = k * STEPS + c
                pool.wait_ge(Q.prod_ready.sem, Q.prod_ready.after(g, n + 1))
                if c == 0:
                    nc.gpsimd.tensor_tensor(YSUM, PR[:, c % 2, 0, :], PR[:, c % 2, 1, :], ALU.add).then_inc(Q.summed.sem, 1)
                    pool.wait_ge(Q.summed.sem, Q.summed.after(g, n + 1))
                    pool.sem_inc(y_added.sem, 1)
                else:
                    pool.wait_ge(y_added.sem, y_added.after(g, n))
                    nc.gpsimd.tensor_tensor(PAIR, PR[:, c % 2, 0, :], PR[:, c % 2, 1, :], ALU.add).then_inc(Q.summed.sem, 1)
                    pool.wait_ge(Q.summed.sem, Q.summed.after(g, n + 1))
                    nc.gpsimd.tensor_tensor(YSUM, YSUM, PAIR, ALU.add).then_inc(y_added.sem, 1)

            def part_a(g, tail):
                if g is not None:
                    for c in range(STEPS):
                        sum_step(g, 0, c)
                        if not is_last(g):
                            if c == 2:
                                pool.wait_ge(rows_ready.sem, rows_ready.after(g + 1, 1))
                                pool.sem_inc(turn_taken, 1)
                            if c in (2, 3, 4):
                                gather(g + 1, (c - 2,))

            def part_b(g, tail, nxt):
                if g is not None:
                    for c in range(STEPS):
                        sum_step(g, 1, c)
                if tail is not None:
                    pool.wait_ge(final.sem, final.after(tail, 1))
                    pool.dma_start(out_m[bass.ds(tail, 1), :, :].rearrange("g p t -> p (g t)"), Om[:, :]).then_inc(stored.sem, 16)
                    pool.dma_start(out_r[bass.ds(tail, 1), :, :].rearrange("g p t -> p (g t)"), Or[:, :]).then_inc(stored.sem, 16)
                    pool.wait_ge(stored.sem, stored.after(tail, 32))
                    pool.sem_inc(out_free.sem, 1)

            second_pass(pool, part_a, part_b)

        @block.scalar
        def _(act):
            act.dma_start(SELF[:, :], sel_d[:, :]).then_inc(s_sel, 16)
            act.wait_ge(s_const[0], 32)
            act.wait_ge(prep_pool, 1)
            nc.scalar.activation(dt0[:, :], cm("log_dt"), ACT.Exp).then_inc(prep_act, 1)
            act.wait_ge(prep_act, 1)
            nc.scalar.mul(neg_dt0[:, :], dt0[:, :], -1.0)
            nc.scalar.activation(posb_m[:, :], cm("posm"), ACT.Identity, bias=cm("tok_b", 0, 1))
            nc.scalar.activation(posb_r[:, :], cm("posr", p=DR), ACT.Identity, bias=cm("tok_b", 1, 2, p=DR)).then_inc(prep_act, 1)
            act.wait_ge(sel_ready, 2)
            nc.scalar.activation(negA[:, :], negA[:, :], ACT.Exp).then_inc(prep_act, 1)
            act.wait_ge(prep_act, 4)

            def squares(s, g, li):
                act.wait_ge(s.ln_centred.sem, s.ln_centred.after(g, 2 * li + 1))
                nc.scalar.activation(s.SQm, s.Cm[:, :], ACT.Square).then_inc(s.ln_squares.sem, 1)
                act.wait_ge(s.ln_centred.sem, s.ln_centred.after(g, 2 * li + 2))
                nc.scalar.activation(s.SQr[:, :], s.Cr[:, :], ACT.Square).then_inc(s.ln_squares.sem, 1)

            def power(s, rows, var, log, rstd, g, k):
                nc.scalar.activation(s.VE[0:rows, :], var, ACT.Ln, bias=eps_col[0:rows, :]).then_inc(log.sem, 1)
                act.wait_ge(log.sem, log.after(g, k))
                nc.scalar.activation(s.RS[0:rows, :], s.VE[0:rows, :], ACT.Exp, scale=-0.5).then_inc(rstd.sem, 1)

            def rstd(s, g, li, bank):
                act.wait_ge(s.ln_var.sem, s.ln_var.after(g, li + 1))
                power(s, 128, PS[:, bank, 0:T], s.ln_log, s.ln_rstd, g, li + 1)

            def copy_set(s, g, i, buf, bank, bias, is_abs=False):
                act.wait_ge(s.set_mm.sem, s.set_mm.after(g, i + 1))
                kw = {} if bias is None else {"bias": bias}
                nc.scalar.activation(s.V[:, :], PS[:, bank, 0:T], ACT.Identity, **kw).then_inc(s.set_copied.sem, 1)
                if is_abs:
                    act.wait_ge(abs_ready.sem, abs_ready.after(g, 1))
                    nc.scalar.activation(s.S3[:, buf, :], s.V[:, :], ACT.Copy).then_inc(s.set_copied.sem, 1)
                else:
                    nc.scalar.activation(s.S3[:, buf, :], PS[:, bank, 0:T], ACT.Identity, **kw).then_inc(s.set_copied.sem, 1)

            def logits(s, g, bank, bias):
                act.wait_ge(s.logits_mm.sem, s.logits_mm.after(g, 1))
                kw = {} if bias is None else {"bias": bias}
                nc.scalar.activation(s.LW[:, :], PS[0:EXPERTS, bank, 0:T], ACT.Identity, **kw).then_inc(s.logits_ready.sem, 1)

            def ratio(s, g):
                act.wait_ge(s.gap_ready.sem, s.gap_ready.after(g, 1))
                nc.scalar.activation(s.gs[0:TW, 3, :], s.gs[0:TW, 2, :], ACT.Exp).then_inc(s.ratio_ready.sem, 1)

            def hidden(g, first, last):
                for j in range(first, last):
                    act.wait_ge(hid_mm.sem, hid_mm.after(g, j + 1))
                    dst, rows = (HID[:, j, :], 128) if j < 10 else (HIDr[:, :], DR)
                    nc.scalar.activation(dst, PS[0:rows, (7, 0, 1)[j % 3], 0:T], ACT.Silu,
                                         bias=cm("m1_b", j, j + 1, p=rows)).then_inc(hid_ready.sem, 1)

            def in_copies(g, k):
                act.wait_ge(in_mm.sem, in_mm.after(g, k + 1))
                nc.scalar.activation(XS, PS[:, X_BANK, 0:PK], ACT.Copy).then_inc(in_copied.sem, 1)
                nc.scalar.activation(DIRS[k].ZS, PS[:, Z_BANK[k], 0:PK], ACT.Silu)

            def inputs(g, k):
                s = DIRS[k]
                act.wait_ge(conv_ready.sem, conv_ready.after(g, k + 1))
                nc.scalar.activation(s.UP[:, :], s.CV, ACT.Silu)
                nc.scalar.activation(s.URr[:, 0:HALF], s.CV[0:DR, T:PK], ACT.Silu)
                nc.scalar.activation(s.URr[:, HALF:T], s.CV[DR:128, T:PK], ACT.Silu).then_inc(u_ready.sem, 1)

            def projected(g, k):
                act.wait_ge(dt24_mm.sem, dt24_mm.after(g, k + 1))
                nc.scalar.activation(DT24, PS[0:RANK, Z_BANK[k], 0:T], ACT.Copy).then_inc(dt24_ready.sem, 1)
                copy_set(DIRS[k], g, k, 0, X_BANK, None)

            def raw_steps(g, k):
                d = "fb"[k]
                act.wait_ge(dt_mm.sem, dt_mm.after(g, k + 1))
                for h, cols in enumerate(MAIN_REST):
                    last = nc.scalar.activation(DIRS[k].DL[:, cols], PS[:, Z_BANK[k], cols], ACT.Identity, bias=cm(d + "dtb", h, h + 1))
                last.then_inc(dt_raw.sem, 1)

            def softplus(g, k):
                s = DIRS[k]
                act.wait_ge(abs_dt.sem, abs_dt.after(g, k + 1))
                nc.scalar.activation(s.OM[:, :], s.TM[:, :], ACT.Exp, scale=-1.0).then_inc(exp_dt.sem, 1)
                act.wait_ge(exp_dt.sem, exp_dt.after(g, k + 1))
                nc.scalar.activation(LZ, s.OM[:, :], ACT.Ln, bias=1.0).then_inc(log_dt_ready.sem, 1)

            def q_decay(g, k, c):
                n = k * STEPS + c
                if c == 0:
                    act.wait_ge(Q.w_ready.sem, Q.w_ready.after(g, k + 1))
                if n >= 2 or not is_first(g):
                    act.wait_ge(Q.scanned.sem, Q.scanned.after(g, n - 1))
                for i in range(NC):
                    for h, cols in enumerate(MAIN_REST):
                        col = (2 * k + h) * NS + c * NC + i
                        last = nc.scalar.activation(dA[:, c % 2, i, cols], DIRS[k].DL[:, cols], ACT.Exp,
                                                    scale=negA[:, col:col + 1])
                last.then_inc(Q.da_ready.sem, 1)

            def p_decay(g, c):
                act.wait_ge(a_bc.sem, a_bc.after(g, c + 1))
                if c >= 2:
                    act.wait_ge(b_times_a.sem, b_times_a.after(g, c - 1))
                    act.wait_ge(ap_ready.sem, ap_ready.after(g, c - 1))
                for h, cols in enumerate(MAIN_REST):
                    last = nc.scalar.activation(dA[:, c % 2, :, cols], PS[:, A_BANK:A_BANK + NC, cols], ACT.Exp,
                                                scale=neg_dt0[:, h:h + 1])
                last.then_inc(P.da_ready.sem, 1)

            def output(g, k):
                act.wait_ge(out_mm.sem, out_mm.after(g, k + 1))
                nc.scalar.activation(DIRS[k].YT, PS[0:BN, AFTER_BANK[k], 0:T], ACT.Copy).then_inc(out_copied.sem, 1)

            def output_rstd(g, k):
                act.wait_ge(bn_centred.sem, bn_centred.after(g, k + 1))
                nc.scalar.activation(Q.SQm[0:BN, :], Q.Cm[0:BN, :], ACT.Square).then_inc(bn_squares.sem, 1)
                act.wait_ge(bn_var.sem, bn_var.after(g, k + 1))
                power(Q, BN, PS[0:BN, AFTER_BANK[k], 0:T], bn_log, bn_rstd, g, k + 1)

            def first(gP, gM):
                hasP, hasM = gP is not None, gM is not None
                if hasM:
                    act.wait_ge(s_const[1], 32)
                    squares(M, gM, 0)
                    rstd(M, gM, 0, 5)
                if hasP:
                    squares(P, gP, 0)
                    rstd(P, gP, 0, 7)
                if hasM:
                    logits(M, gM, 5, None)
                if hasP:
                    hidden(gP, 0, 6)
                if hasM:
                    act.wait_ge(xtok_mm.sem, xtok_mm.after(gM, 2))
                    act.wait_ge(scatter_free.sem, scatter_free.after(gM, 1))
                    nc.scalar.activation(XTOK[0:TW, 0:2, :], PS[0:TW, 2, 0:2 * D].rearrange("p (t n) -> p t n", n=D), ACT.Copy)
                    nc.scalar.activation(XTOK[0:TW, 2, :], PS[0:TW, 3, 0:D], ACT.Copy).then_inc(xtok_copied.sem, 1)
                if hasP:
                    hidden(gP, 6, 11)
                if hasM:
                    ratio(M, gM)
                if hasP:
                    copy_set(P, gP, 0, 0, 7, cm("m2_b", 0, 1), is_abs=True)
                    act.wait_ge(P.set_ready.sem, P.set_ready.after(gP, 1))
                    copy_set(P, gP, 1, 1, 0, cm("m2_b", 1, 2))
                    nc.scalar.activation(P.UP[:, 0:T], P.Xm[:, :], ACT.Copy)
                    nc.scalar.activation(P.UP[0:DR, T:PK], P.Xr[:, 0:HALF], ACT.Copy)
                    nc.scalar.activation(P.UP[DR:128, T:PK], P.Xr[:, HALF:T], ACT.Copy).then_inc(packed_x.sem, 1)
                    act.wait_ge(delta_mm.sem, delta_mm.after(gP, 1))
                    nc.scalar.activation(P.DL[:, 0:T], PS[:, 1, 0:T], ACT.Sigmoid, bias=cm("d_b2", 0, 1))
                    nc.scalar.activation(P.DL[:, T:PK], PS[:, 1, T:PK], ACT.Sigmoid, bias=cm("d_b2", 1, 2)).then_inc(delta_ready.sem, 1)
                    for c in range(STEPS):
                        p_decay(gP, c)

            first_pass(act, first)

            def gelus(i, p):
                b = 3 * i + p
                if not early(b, 3):
                    act.wait_ge(narrow_mm.sem, narrow_mm.after(b - 3, 1))
                for h in range(2):
                    act.wait_ge(wide_mm.sem, wide_mm.after(b, h + 1))
                    for j in range(HALF_FT):
                        f = h * HALF_FT + j
                        last = nc.scalar.activation(HX[:, p, f, :], PS[:, WIDE_BANK + 2 * p + h, j * 128:(j + 1) * 128], ACT.Gelu,
                                                    bias=WX[:, p, FFN + FT * D + f:FFN + FT * D + f + 1])
                    last.then_inc(gelu_ready.sem, 1)

            over_blocks(act, gelus)

            def part_a(g, tail):
                if g is not None:
                    q_decay(g, 0, 0)
                for c in range(STEPS):
                    if g is not None and c + 1 < STEPS:
                        q_decay(g, 0, c + 1)
                    if tail is not None:
                        if c == 0:
                            output(tail, 1)
                        if c == 1:
                            output_rstd(tail, 1)
                        if c == 4:
                            squares(Q, tail, 0)
                            rstd(Q, tail, 0, 5)
                        if c == 6:
                            logits(Q, tail, 5, cm("er_b", p=EXPERTS))
                        if c == 7:
                            ratio(Q, tail)
                            act.wait_ge(shift_ready.sem, shift_ready.after(tail, 1))
                            nc.scalar.activation(Q.gate[0:TW, 7], Q.gate[0:TW, 6], ACT.Exp).then_inc(shift_exp.sem, 1)
                    if g is not None:
                        if c == 0:
                            in_copies(g, 1)
                        if c == 1:
                            inputs(g, 1)
                        if c == 2:
                            projected(g, 1)
                        if c == 3:
                            raw_steps(g, 1)
                        if c == 4:
                            softplus(g, 1)

            def part_b(g, tail, nxt):
                if g is not None:
                    q_decay(g, 1, 0)
                for c in range(STEPS):
                    if g is not None:
                        if c + 1 < STEPS:
                            q_decay(g, 1, c + 1)
                        if c == 0:
                            output(g, 0)
                            act.wait_ge(M.residual.sem, M.residual.after(g, 1))
                            if tail is not None:
                                act.wait_ge(Q.residual.sem, Q.residual.after(tail, 1))
                            nc.scalar.activation(HBm, L.Hm[:, :], ACT.Copy)
                            nc.scalar.activation(HBr, L.Hr[:, :], ACT.Copy).then_inc(hb_copied.sem, 1)
                        if c == 1:
                            output_rstd(g, 0)
                    if nxt is not None:
                        if c == 2:
                            squares(L, nxt, 0)
                            rstd(L, nxt, 0, 5)
                        if c == 3:
                            act.wait_ge(bott_mm.sem, bott_mm.after(nxt, 1))
                            nc.scalar.activation(HB[:, :], PS[0:BN, 5, 0:T], ACT.Identity, bias=cm("down_b", p=BN)).then_inc(bott_ready.sem, 1)
                            in_copies(nxt, 0)
                        if c == 4:
                            inputs(nxt, 0)
                            projected(nxt, 0)
                        if c == 5:
                            raw_steps(nxt, 0)
                        if c == 6:
                            softplus(nxt, 0)

            act.wait_ge(s_const[2], 32)
            second_pass(act, part_a, part_b)

        @block.vector
        def _(dve):
            dve.wait_ge(s_sel, 16)
            nc.vector.tensor_copy(SEL[:, :], SELF[:, :]).then_inc(sel_ready, 1)
            dve.wait_ge(s_const[0], 32)
            nc.vector.tensor_scalar(negA[:, 0:2 * NS], cm("fAlog"), float(np.log(A_MAX)), None, ALU.min)
            nc.vector.tensor_scalar(negA[:, 2 * NS:4 * NS], cm("bAlog"), float(np.log(A_MAX)), None, ALU.min).then_inc(sel_ready, 1)
            dve.wait_ge(prep_act, 3)
            nc.vector.tensor_scalar(negA[:, :], negA[:, :], -1.0, -A_MIN, ALU.mult, ALU.min).then_inc(prep_act, 1)

            links = {}

            def link(s, g, ins):
                links[s] += 1
                ins.then_inc(s.chain.sem, 1)
                dve.wait_ge(s.chain.sem, s.chain.after(g, links[s]))

            def centre(s, src, g, li, bank):
                dve.wait_ge(s.ln_mean.sem, s.ln_mean.after(g, li + 1))
                nc.vector.tensor_tensor(s.Cm[:, :], src.Hm[:, :], PS[:, bank, 0:T], ALU.subtract).then_inc(s.ln_centred.sem, 1)
                nc.vector.tensor_tensor(s.Cr[:, :], src.Hr[:, :], PS[0:DR, bank, 0:T], ALU.subtract).then_inc(s.ln_centred.sem, 1)

            def scale(s, g, li):
                dve.wait_ge(s.ln_rstd.sem, s.ln_rstd.after(g, li + 1))
                nc.vector.tensor_tensor(s.Xm[:, :], s.Cm[:, :], s.RS[:, :], ALU.mult)
                nc.vector.tensor_tensor(s.Xr[:, :], s.Cr[:, :], s.RS[0:DR, :], ALU.mult).then_inc(s.ln_x.sem, 1)

            def split_set(s, g, i, buf, is_abs=False):
                dve.wait_ge(s.set_copied.sem, s.set_copied.after(g, 2 * i + 1))
                if is_abs:
                    nc.vector.scalar_tensor_tensor(s.V[:, :], s.V[:, :], cm("sign"), s.V[:, :], ALU.mult, ALU.max).then_inc(abs_ready.sem, 1)
                dve.wait_ge(s.set_copied.sem, s.set_copied.after(g, 2 * i + 2))
                link(s.work, g, nc.vector.tensor_tensor(s.R[64:128, :], s.V[64:128, :], s.S3[64:128, buf, :], ALU.subtract))
                link(s.work, g, nc.vector.tensor_copy(s.S3[64:128, buf, :], s.R[64:128, :]))
                nc.vector.tensor_tensor(s.S3[96:128, buf, :], s.R[96:128, :], s.S3[96:128, buf, :], ALU.subtract).then_inc(s.set_ready.sem, 1)

            def gate_views(s):
                L, q, oh1, oh2, L2, w = [s.gate[0:TW, j] for j in range(6)]
                if s is M:
                    oh1, oh2 = KEEP[:, :, 0:EXPERTS], KEEP[:, :, EXPERTS:2 * EXPERTS]
                return [L, q, oh1, oh2, L2, w], [s.gs[0:TW, j] for j in range(8)]

            def over(ap):
                return ap.unsqueeze(2).broadcast_to([TW, TILES, EXPERTS])

            def gates_top(s, g, bank):
                (L, q, oh1, oh2, L2, w), (m1, m2, gap, ratio, den, inv, w2, rk) = gate_views(s)
                rank = cm("rank", p=TW).unsqueeze(1).broadcast_to([TW, TILES, EXPERTS])
                dve.wait_ge(s.logits_T.sem, s.logits_T.after(g, 1))
                link(s, g, nc.vector.tensor_copy(L, PS[0:TW, bank, 0:TILES * EXPERTS].rearrange("p (t e) -> p t e", e=EXPERTS)))

                def pick(src, m, oh):
                    link(s, g, nc.vector.tensor_reduce(m, src, AX.X, ALU.max))
                    link(s, g, nc.vector.tensor_tensor(q, src, over(m), ALU.is_equal))
                    link(s, g, nc.vector.tensor_tensor(q, q, rank, ALU.mult))
                    link(s, g, nc.vector.tensor_reduce(rk, q, AX.X, ALU.max))
                    link(s, g, nc.vector.tensor_tensor(oh, q, over(rk), ALU.is_equal))

                pick(L, m1, oh1)
                link(s, g, nc.vector.scalar_tensor_tensor(L2, oh1, -3.0e38, L, ALU.mult, ALU.add))
                pick(L2, m2, oh2)
                nc.vector.tensor_tensor(gap, m2, m1, ALU.subtract).then_inc(s.gap_ready.sem, 1)
                if s is Q:
                    nc.vector.tensor_tensor(s.gate[0:TW, 6], L, over(m1), ALU.subtract).then_inc(shift_ready.sem, 1)

            def gates_weights(s, g):
                (L, q, oh1, oh2, L2, w), (m1, m2, gap, ratio, den, inv, w2, rk) = gate_views(s)
                dve.wait_ge(s.ratio_ready.sem, s.ratio_ready.after(g, 1))
                link(s, g, nc.vector.tensor_scalar(den, ratio, 1.0, None, ALU.add))
                dve.wait_ge(shift_exp.sem, shift_exp.after(g, 1))
                link(s, g, nc.vector.tensor_reduce(rk, s.gate[0:TW, 7], AX.X, ALU.add))
                link(s, g, nc.vector.scalar_tensor_tensor(den, rk, 1e-9, den, ALU.mult, ALU.add))
                link(s, g, nc.vector.reciprocal(inv, den))
                link(s, g, nc.vector.tensor_tensor(w2, ratio, inv, ALU.mult))
                link(s, g, nc.vector.tensor_tensor(oh1, oh1, over(inv), ALU.mult))
                link(s, g, nc.vector.tensor_tensor(oh2, oh2, over(w2), ALU.mult))
                nc.vector.tensor_tensor(w, oh1, oh2, ALU.add).then_inc(s.gates_ready.sem, 1)

            def route(g):
                (L, q, oh1, oh2, pos, pair), (m1, m2, gap, ratio, den, inv, w2, rk) = gate_views(M)
                kw1, kw2, slot1, slot2 = (KEEP[:, :, 2 * EXPERTS + j] for j in range(4))
                nc.vector.tensor_tensor(pair, oh1, oh2, ALU.add).then_inc(pair_ready.sem, 1)
                dve.wait_ge(M.ratio_ready.sem, M.ratio_ready.after(g, 1))
                link(M, g, nc.vector.tensor_scalar(den, ratio, 1.0, None, ALU.add))
                link(M, g, nc.vector.reciprocal(kw1, den))
                nc.vector.tensor_tensor(kw2, ratio, kw1, ALU.mult)
                dve.wait_ge(ranks_mm.sem, ranks_mm.after(g, 1))
                link(M, g, nc.vector.tensor_tensor(pos, PS[0:TW, 5, 0:TILES * EXPERTS].rearrange("p (t e) -> p t e", e=EXPERTS),
                                                   run[:, :].unsqueeze(1).broadcast_to([TW, TILES, EXPERTS]), ALU.add))
                nc.vector.tensor_tensor(run[:, :], run[:, :], PS[0:TW, 5, TILES * EXPERTS:(TILES + 1) * EXPERTS], ALU.add)
                nc.vector.tensor_tensor(q, oh1, pos, ALU.mult)
                link(M, g, nc.vector.tensor_tensor(L, oh2, pos, ALU.mult))
                nc.vector.tensor_reduce(slot1, q, AX.X, ALU.add)
                link(M, g, nc.vector.tensor_reduce(slot2, L, AX.X, ALU.add))
                nc.vector.tensor_copy(slot_u[:, :, :], KEEP[:, :, 2 * EXPERTS + 2:2 * EXPERTS + 4]).then_inc(slots_ready.sem, 1)

            def gates_rows(s, g, bank):
                dve.wait_ge(s.gates_T.sem, s.gates_T.after(g, 1))
                nc.vector.tensor_copy(s.LW[:, :], PS[0:EXPERTS, bank, 0:T]).then_inc(s.gates_T_ready.sem, 1)

            def start_sum(s, g, bank01, bank2):
                dve.wait_ge(s.bias_mm.sem, s.bias_mm.after(g, 1))
                nc.vector.tensor_copy(s.ACC[0:TW, 0:2, :], PS[0:TW, bank01, 0:2 * D].rearrange("p (t n) -> p t n", n=D))
                nc.vector.tensor_copy(s.ACC[0:TW, 2, :], PS[0:TW, bank2, 0:D]).then_inc(s.acc_started.sem, 1)
                dve.wait_ge(s.acc_started.sem, s.acc_started.after(g, 1))

            def flat(ap, back):
                ap = ap.rearrange("p n t -> p (n t)")
                return ap[:, ::-1] if back else ap

            def scan_step(s, g, k, c):
                n, back = k * STEPS + c, s is BW
                dve.wait_ge(s.b_bc.sem, s.b_bc.after(g, n + 1))
                nc.vector.tensor_tensor(BB[:, c % 2], s.WV[:, :].unsqueeze(1).broadcast_to([128, NC, PK]),
                                        PS[:, B_BANK:B_BANK + NC, 0:PK], ALU.mult).then_inc(s.b_read.sem, 1)
                dve.wait_ge(s.b_read.sem, s.b_read.after(g, n + 1))
                dve.wait_ge(s.da_ready.sem, s.da_ready.after(g, n + 1))
                if s is P:
                    nc.vector.tensor_tensor(BB[:, c % 2], BB[:, c % 2], dA[:, c % 2], ALU.mult).then_inc(b_times_a.sem, 1)
                    dve.wait_ge(b_times_a.sem, b_times_a.after(g, c + 1))
                    dve.wait_ge(ap_ready.sem, ap_ready.after(g, c + 1))
                decay = aP if s is P else dA
                nc.vector.tensor_tensor_scan(flat(ST[:, :, :], back), flat(decay[:, c % 2], back),
                                             flat(BB[:, c % 2], back), 0.0, ALU.mult, ALU.add).then_inc(s.scanned.sem, 1)

            def output_step(s, g, k, c):
                n = k * STEPS + c
                dve.wait_ge(s.scanned.sem, s.scanned.after(g, n + 1))
                dve.wait_ge(s.c_bc.sem, s.c_bc.after(g, n + 1))
                if c >= 2 or not at_start(s, g, 0):
                    dve.wait_ge(s.summed.sem, s.summed.after(g, n - 1))
                nc.vector.tensor_tensor(PR[:, c % 2], ST[:, :, :], PS[:, C_BANK:C_BANK + NC, 0:PK], ALU.mult).then_inc(s.prod_ready.sem, 1)

            def tokens(g, before):
                if before is not None:
                    dve.wait_ge(h_stored.sem, h_stored.after(before, 32))
                    dve.wait_ge(M.ln_centred.sem, M.ln_centred.after(before, 2))
                for k in range(2):
                    Hs, rows, pos, cls = ((P.Hm, 128, posb_m, "cls_m"), (P.Hr, DR, posb_r, "cls_r"))[k]
                    hv = seqs(Hs[:, :])
                    nc.vector.tensor_copy(hv[:, :, 0:2], cm(cls, p=rows).unsqueeze(1).broadcast_to([rows, IMG, 2]))
                    dve.wait_ge(tok_mm.sem, tok_mm.after(g, k + 1))
                    last = nc.vector.tensor_tensor(hv[:, :, 2:SEQ],
                                                   PS[0:rows, 7 - k, 0:IMG * NP].rearrange("p (b t) -> p b t", t=NP),
                                                   pos[:, :].unsqueeze(1).broadcast_to([rows, IMG, NP]), ALU.add)
                last.then_inc(P.residual.sem, 1)
                dve.wait_ge(P.residual.sem, P.residual.after(g, 1))

            def first_scan_input(g):
                dve.wait_ge(delta_ready.sem, delta_ready.after(g, 1))
                dve.wait_ge(packed_x.sem, packed_x.after(g, 1))
                link(P, g, nc.vector.tensor_scalar(P.OM[:, :], P.DL[:, :], -1.0, 1.0, ALU.mult, ALU.add))
                for h, cols in enumerate(MAIN_REST):
                    last = nc.vector.scalar_tensor_tensor(P.WV[:, cols], P.OM[:, cols], dt0[:, h:h + 1], P.UP[:, cols], ALU.mult, ALU.mult)
                link(P, g, last)
                nc.vector.memset(seqs(P.DL[:, :])[:, :, 0:1], 0.0).then_inc(P.w_ready.sem, 1)

            def first_scan_output(g):
                dve.wait_ge(P.summed.sem, P.summed.after(g, STEPS))
                nc.vector.scalar_tensor_tensor(P.TM[:, 0:T], P.Xm[:, :], cm("D0", 0, 1), PS[:, Y_BANK, 0:T], ALU.mult, ALU.add)
                D0r = cm("D0", 1, 2, p=DR)
                nc.vector.scalar_tensor_tensor(P.OM[0:DR, 0:HALF], P.Xr[:, 0:HALF], D0r, PS[0:DR, Y_BANK, T:PK], ALU.mult, ALU.add)
                link(P, g, nc.vector.scalar_tensor_tensor(P.OM[0:DR, HALF:T], P.Xr[:, HALF:T], D0r, PS[DR:128, Y_BANK, T:PK], ALU.mult, ALU.add))
                nc.vector.tensor_tensor(P.Hm[:, :], P.Hm[:, :], P.TM[:, 0:T], ALU.add)
                nc.vector.tensor_tensor(P.Hr[:, :], P.Hr[:, :], P.OM[0:DR, 0:T], ALU.add).then_inc(P.residual.sem, 1)

            def convolve(g, k):
                d, CV = "fb"[k], DIRS[k].CV
                links[PREP] = 10 * k
                dve.wait_ge(in_copied.sem, in_copied.after(g, k + 1))
                for h, cols in enumerate(MAIN_REST):
                    last = nc.vector.tensor_scalar(CV[:, cols], XS[:, cols], cm(d + "cw", 4 * h + 3, 4 * h + 4),
                                                   cm(d + "cb", h, h + 1), ALU.mult, ALU.add)
                link(PREP, g, last)
                for s in range(1, 4):
                    for h, cols in enumerate(MAIN_REST):
                        src, dst = seqs(XS[:, cols]), seqs(CV[:, cols])
                        if d == "b":
                            src, dst = src[:, :, s:SEQ], dst[:, :, 0:SEQ - s]
                        else:
                            src, dst = src[:, :, 0:SEQ - s], dst[:, :, s:SEQ]
                        last = nc.vector.scalar_tensor_tensor(dst, src, cm(d + "cw", 4 * h + 3 - s, 4 * h + 4 - s), dst,
                                                              ALU.mult, ALU.add)
                    if s < 3:
                        link(PREP, g, last)
                    else:
                        last.then_inc(conv_ready.sem, 1)

            def size_of_steps(g, k):
                s = DIRS[k]
                dve.wait_ge(dt_raw.sem, dt_raw.after(g, k + 1))
                nc.vector.scalar_tensor_tensor(s.TM[:, :], s.DL[:, :], -1.0, s.DL[:, :], ALU.mult, ALU.max).then_inc(abs_dt.sem, 1)

            def steps(g, k):
                s = DIRS[k]
                dve.wait_ge(exp_dt.sem, exp_dt.after(g, k + 1))
                link(PREP, g, nc.vector.tensor_scalar(s.TM[:, :], s.OM[:, :], 1.0, -1.0, ALU.add, ALU.add))
                dve.wait_ge(log_dt_ready.sem, log_dt_ready.after(g, k + 1))
                link(PREP, g, nc.vector.tensor_tensor(s.OM[:, :], s.OM[:, :], s.TM[:, :], ALU.subtract))
                link(PREP, g, nc.vector.tensor_tensor(s.OM[:, :], s.OM[:, :], LZ, ALU.add))
                link(PREP, g, nc.vector.scalar_tensor_tensor(s.DL[:, :], s.DL[:, :], 0.0, s.OM[:, :], ALU.max, ALU.add))
                link(PREP, g, nc.vector.tensor_tensor(s.WV[:, :], s.DL[:, :], s.UP[:, :], ALU.mult))
                assert links[PREP] == 10 * k + 10
                first = slice(SEQ - 1, SEQ) if k == 1 else slice(0, 1)
                nc.vector.memset(seqs(s.DL[:, :])[:, :, first], RESTART).then_inc(Q.w_ready.sem, 1)

            def gated_output(g, k):
                d, s = "fb"[k], DIRS[k]
                links[GATED] = k
                dve.wait_ge(y_added.sem, y_added.after(g, (k + 1) * STEPS))
                for h, cols in enumerate(MAIN_REST):
                    last = nc.vector.scalar_tensor_tensor(s.TM[:, cols], s.UP[:, cols], cm(d + "Dp", h, h + 1), YSUM[:, cols], ALU.mult, ALU.add)
                link(GATED, g, last)
                nc.vector.tensor_tensor(s.CV[:, 0:T], s.TM[:, 0:T], s.ZS[:, 0:T], ALU.mult)
                nc.vector.tensor_tensor(s.GRr[:, 0:HALF], s.TM[0:DR, T:PK], s.ZS[0:DR, T:PK], ALU.mult)
                nc.vector.tensor_tensor(s.GRr[:, HALF:T], s.TM[DR:128, T:PK], s.ZS[DR:128, T:PK], ALU.mult).then_inc(y_gated.sem, 1)

            def output_centre(g, k):
                dve.wait_ge(out_copied.sem, out_copied.after(g, k + 1))
                dve.wait_ge(bn_mean.sem, bn_mean.after(g, k + 1))
                nc.vector.tensor_tensor(Q.Cm[0:BN, :], DIRS[k].YT, PS[0:BN, AFTER_BANK[k], 0:T], ALU.subtract).then_inc(bn_centred.sem, 1)

            def output_norm(g, k):
                d = "fb"[k]
                links[NORM] = k
                dve.wait_ge(bn_rstd.sem, bn_rstd.after(g, k + 1))
                link(NORM, g, nc.vector.tensor_tensor(Q.Cm[0:BN, :], Q.Cm[0:BN, :], Q.RS[0:BN, :], ALU.mult))
                nc.vector.tensor_scalar(YS[:, k, :], Q.Cm[0:BN, :], cm(d + "lng", 0, 1, p=BN), cm(d + "lng", 1, 2, p=BN),
                                        ALU.mult, ALU.add).then_inc(bn_done.sem, 1)

            def first(gP, gM):
                hasP, hasM = gP is not None, gM is not None
                links.update({P: 0, M: 0})
                if hasM:
                    centre(M, P, gM, 0, 5)
                if hasP:
                    dve.wait_ge(prep_act, 3)
                    tokens(gP, gM)
                if hasM:
                    scale(M, gM, 0)
                if hasP:
                    if hasM:
                        dve.wait_ge(M.ln_x.sem, M.ln_x.after(gM, 1))
                    centre(P, P, gP, 0, 7)
                    scale(P, gP, 0)
                if hasM:
                    dve.wait_ge(scatter_free.sem, scatter_free.after(gM, 1))
                    gates_top(M, gM, 6)
                    route(gM)
                if hasP:
                    split_set(P, gP, 0, 0, is_abs=True)
                    split_set(P, gP, 1, 1)
                    first_scan_input(gP)
                    for c in range(STEPS):
                        scan_step(P, gP, 0, c)
                        output_step(P, gP, 0, c)
                    first_scan_output(gP)
                assert not hasP or links[P] == P.chain.per_group, links[P]
                assert not hasM or links[M] == M.chain.per_group, ("M", links[M])

            dve.wait_ge(s_const[1], 32)
            nc.vector.tensor_copy(run[:, :], cm("eoff", p=TW)).then_inc(table, 1)
            dve.wait_ge(table, 1)
            first_pass(dve, first)

            done = [1]

            def then(ins):
                done[0] += 1
                ins.then_inc(table, 1)
                dve.wait_ge(table, done[0])

            used, blocks, start, delta, end, last_b = (counts[:, j, :] for j in range(6))
            which, expert, before, place, place2 = (block_f[:, j, :] for j in range(5))
            dve.wait_ge(slots_ready.sem, slots_ready.after(GROUPS, 0))
            then(nc.vector.tensor_tensor(used, run[:, :], cm("eoff", p=TW), ALU.subtract))
            then(nc.vector.tensor_tensor(steps80[:, :, :], used.unsqueeze(2).broadcast_to([TW, EXPERTS, CAP_BLOCKS]),
                                         cm("blk", p=TW).unsqueeze(1).broadcast_to([TW, EXPERTS, CAP_BLOCKS]), ALU.is_gt))
            then(nc.vector.tensor_reduce(blocks, steps80[:, :, :], AX.X, ALU.add))
            then(nc.vector.tensor_tensor(steps80[:, :, 0:EXPERTS], blocks.unsqueeze(1).broadcast_to([TW, EXPERTS, EXPERTS]),
                                         cm("below", p=TW).rearrange("p (a b) -> p a b", b=EXPERTS), ALU.mult))
            then(nc.vector.tensor_reduce(start, steps80[:, :, 0:EXPERTS], AX.X, ALU.add))
            nc.vector.scalar_tensor_tensor(delta, start, 128.0, cm("eoff", p=TW), ALU.mult, ALU.subtract)
            then(nc.vector.tensor_tensor(end, start, blocks, ALU.add))
            then(nc.vector.tensor_scalar(last_b[:, 0:1], end[:, EXPERTS - 1:EXPERTS], -1.0, None, ALU.add))
            then(nc.vector.tensor_scalar(which, cm("bid", p=TW), last_b[:, 0:1], None, ALU.min))
            then(nc.vector.tensor_tensor(passed[:, 0], which.unsqueeze(2).broadcast_to([TW, BLOCKS, EXPERTS]),
                                         end.unsqueeze(1).broadcast_to([TW, BLOCKS, EXPERTS]), ALU.is_ge))
            nc.vector.tensor_reduce(expert, passed[:, 0], AX.X, ALU.add)
            then(nc.vector.tensor_tensor(passed[:, 1], passed[:, 0], blocks.unsqueeze(1).broadcast_to([TW, BLOCKS, EXPERTS]), ALU.mult))
            then(nc.vector.tensor_reduce(before, passed[:, 1], AX.X, ALU.add))
            then(nc.vector.scalar_tensor_tensor(place, expert, float(CAP_BLOCKS), which, ALU.mult, ALU.add))
            then(nc.vector.tensor_tensor(place2, place, before, ALU.subtract))
            nc.vector.tensor_copy(tab_expert[:, :], expert[0:1, :])
            nc.vector.tensor_copy(tab_rows[:, :], place2[0:1, :]).then_inc(table_ready, 1)

            def copy_x(i, p):
                b = 3 * i + p
                dve.wait_ge(t_mm.sem, t_mm.after(b, 1))
                if not early(b, 3):
                    dve.wait_ge(wide_mm.sem, wide_mm.after(b - 3, 2))
                nc.vector.tensor_copy(XTm[:, p, :], PS[:, TURN_BANK, 0:128])
                nc.vector.tensor_copy(XTr[:, p, :], PS[0:DR, TURN_BANK, 128:256]).then_inc(xt_copied.sem, 1)

            def copy_y(i, p):
                b = 3 * i + p
                dve.wait_ge(narrow_mm.sem, narrow_mm.after(b, 1))
                if not early(b, 3):
                    dve.wait_ge(out_rows[p], 16 * i)
                nc.vector.tensor_copy(YB[:, p, :], PS[:, OUT_BANK, 0:D]).then_inc(y_copied.sem, 1)

            def copies(i, p):
                b = 3 * i + p
                if not is_end(b):
                    copy_x(*follower(i, p))
                if not early(b, 1):
                    copy_y(*previous(i, p))

            copy_x(0, 0)
            over_blocks(dve, copies)
            copy_y(BLOCKS // 3 - 1, 2)

            rows_links = [0]

            def rows_link(g, ins):
                rows_links[0] += 1
                ins.then_inc(rows_chain.sem, 1)
                dve.wait_ge(rows_chain.sem, rows_chain.after(g, rows_links[0]))

            def find_rows(g):
                rows_links[0] = 0
                (L, q, oh1, oh2, L2, w), _ = gate_views(M)
                dve.wait_ge(keep_loaded.sem, keep_loaded.after(g, 16))
                db = delta.unsqueeze(1).broadcast_to([TW, TILES, EXPERTS])
                nc.vector.tensor_tensor(q, oh1, db, ALU.mult)
                rows_link(g, nc.vector.tensor_tensor(L, oh2, db, ALU.mult))
                nc.vector.tensor_reduce(L2[:, :, 0], q, AX.X, ALU.add)
                rows_link(g, nc.vector.tensor_reduce(L2[:, :, 1], L, AX.X, ALU.add))
                rows_link(g, nc.vector.tensor_tensor(w[:, :, 0:2], L2[:, :, 0:2], KEEP[:, :, 2 * EXPERTS + 2:2 * EXPERTS + 4], ALU.add))
                nc.vector.tensor_copy(slot_u[:, :, :], w[:, :, 0:2]).then_inc(rows_ready.sem, 1)

            find_rows(0)

            def combine(g):
                dve.wait_ge(gathered.sem, gathered.after(g, 16 * 2 * TILES))
                for t in range(TILES):
                    last = nc.vector.tensor_scalar(M.ACC[0:TW, t, :], GA[:, t, 0, :], KEEP[:, t, 2 * EXPERTS:2 * EXPERTS + 1], None, ALU.mult)
                last.then_inc(M.acc_started.sem, 1)
                dve.wait_ge(M.acc_started.sem, M.acc_started.after(g, 1))
                for t in range(TILES):
                    nc.vector.scalar_tensor_tensor(M.ACC[0:TW, t, :], GA[:, t, 1, :], KEEP[:, t, 2 * EXPERTS + 1:2 * EXPERTS + 2],
                                                   M.ACC[0:TW, t, :], ALU.mult, ALU.add).then_inc(mixed.sem, 1)

            def second_mixture(g, u):
                t, j = u // 4, u % 4
                dve.wait_ge(lin_mm.sem, lin_mm.after(g, u + 1))
                for e in (2 * j, 2 * j + 1):
                    nc.vector.scalar_tensor_tensor(Q.ACC[0:TW, t, :], PS[0:TW, (7, 4)[u % 2], (e % 2) * D:(e % 2 + 1) * D],
                                                   Q.gate[0:TW, 5, t, e:e + 1], Q.ACC[0:TW, t, :],
                                                   ALU.mult, ALU.add).then_inc(lin_acc.sem, 1)
                    dve.wait_ge(lin_acc.sem, lin_acc.after(g, t * EXPERTS + e + 1))

            def part_a(g, tail):
                for c in range(STEPS):
                    if g is not None:
                        scan_step(FW, g, 0, c)
                    if tail is not None:
                        if c == 1:
                            output_centre(tail, 1)
                        if c == 2:
                            output_norm(tail, 1)
                            dve.wait_ge(bn_done.sem, bn_done.after(tail, 2))
                            nc.vector.tensor_tensor(YS[:, 0, :], YS[:, 0, :], YS[:, 1, :], ALU.add).then_inc(y_sum.sem, 1)
                        if c == 3:
                            dve.wait_ge(up_proj.sem, up_proj.after(tail, 1))
                            nc.vector.scalar_tensor_tensor(Q.Hm[:, :], PS[:, 5, 0:T], cm("up_b", 0, 1), HBm, ALU.add, ALU.add)
                            nc.vector.scalar_tensor_tensor(Q.Hr[:, :], PS[0:DR, 4, 0:T], cm("up_b", 1, 2, p=DR), HBr, ALU.add, ALU.add).then_inc(Q.residual.sem, 1)
                            dve.wait_ge(Q.residual.sem, Q.residual.after(tail, 1))
                        if c == 4:
                            centre(Q, Q, tail, 0, 5)
                        if c == 7:
                            links[Q] = 0
                            gates_top(Q, tail, 4)
                    if g is not None:
                        if c == 4:
                            size_of_steps(g, 1)
                        if c == 6:
                            steps(g, 1)
                        output_step(FW, g, 0, c)
                        if c == 1:
                            if tail is not None:
                                dve.wait_ge(out_mm.sem, out_mm.after(tail, 2))
                            convolve(g, 1)
                        if c == 2 and not is_last(g):
                            find_rows(g + 1)
                        if c == 3:
                            split_set(BW, g, 1, 0)
                    if tail is not None:
                        if c == 5:
                            scale(Q, tail, 0)
                        if c == 7:
                            gates_weights(Q, tail)
                            assert links[Q] == Q.chain.per_group, ("Q", links[Q])
                if g is not None:
                    gated_output(g, 0)
                if tail is not None:
                    gates_rows(Q, tail, 5)

            def part_b(g, tail, nxt):
                for c in range(STEPS):
                    if g is not None:
                        scan_step(BW, g, 1, c)
                    if tail is not None and c >= 2:
                        second_mixture(tail, 2 * c - 4)
                    if tail is not None and c == 0:
                        start_sum(Q, tail, 5, 4)
                    if nxt is not None:
                        if c == 0:
                            combine(nxt)
                        if c == 1:
                            dve.wait_ge(M.back_T.sem, M.back_T.after(nxt, 1))
                            dve.wait_ge(h_loaded.sem, h_loaded.after(nxt, 32))
                            if g is not None:
                                dve.wait_ge(hb_copied.sem, hb_copied.after(g, 1))
                            nc.vector.tensor_tensor(L.Hm[:, :], M.Hm[:, :], PS[:, 5, 0:T], ALU.add)
                            nc.vector.tensor_tensor(L.Hr[:, :], M.Hr[:, :], PS[0:DR, 6, 0:T], ALU.add).then_inc(M.residual.sem, 1)
                            dve.wait_ge(M.residual.sem, M.residual.after(nxt, 1))
                        if c == 2:
                            centre(L, L, nxt, 0, 5)
                        if c == 3:
                            scale(L, nxt, 0)
                        if c == 4:
                            if g is not None:
                                dve.wait_ge(out_mm.sem, out_mm.after(g, 1))
                            convolve(nxt, 0)
                        if c == 6:
                            split_set(FW, nxt, 0, 0)
                            size_of_steps(nxt, 0)
                        if c == 7:
                            steps(nxt, 0)
                    if g is not None:
                        output_step(BW, g, 1, c)
                        if c == 0:
                            output_centre(g, 0)
                        if c == 1:
                            output_norm(g, 0)
                    if tail is not None and c >= 2:
                        second_mixture(tail, 2 * c - 3)
                if g is not None:
                    gated_output(g, 1)
                if tail is not None:
                    dve.wait_ge(Q.back_T.sem, Q.back_T.after(tail, 1))
                    dve.wait_ge(out_free.sem, out_free.after(tail, 1))
                    nc.vector.tensor_tensor(Om[:, :], Q.Hm[:, :], PS[:, 7, 0:T], ALU.add)
                    nc.vector.tensor_tensor(Or[:, :], Q.Hr[:, :], PS[0:DR, 4, 0:T], ALU.add).then_inc(final.sem, 1)
                    dve.wait_ge(final.sem, final.after(tail, 1))

            second_pass(dve, part_a, part_b)

        @block.tensor
        def _(pe):
            pe.wait_ge(prep_pool, 1)
            pe.wait_ge(sel_ready, 2)

            def mm(out, lhsT, rhs, first, last):
                return nc.tensor.matmul(out, lhsT, rhs, start=first, stop=last)

            def both(out, s, wm, wr):
                mm(out, wm, s.Xm[:, :], True, False)
                return mm(out, wr, s.Xr[:, :], False, True)

            def mean(s, src, g, li, bank):
                mm(PS[:, bank, 0:T], ones_d[:, :], src.Hm[:, :], True, False)
                mm(PS[:, bank, 0:T], ones_d[0:DR, :], src.Hr[:, :], False, True).then_inc(s.ln_mean.sem, 1)

            def variance(s, g, li, bank):
                pe.wait_ge(s.ln_squares.sem, s.ln_squares.after(g, 2 * li + 2))
                mm(PS[:, bank, 0:T], ones_d[:, :], s.SQm, True, False)
                mm(PS[:, bank, 0:T], ones_d[0:DR, :], s.SQr[:, :], False, True).then_inc(s.ln_var.sem, 1)

            def hidden(g, first, last):
                for j in range(first, last):
                    a, b = j * 128, min(j * 128 + 128, 1344)
                    if j >= 3:
                        pe.wait_ge(hid_ready.sem, hid_ready.after(g, j - 2))
                    both(PS[0:b - a, (7, 0, 1)[j % 3], 0:T], P, cm("m1_w", a, b), cr("m1_w", a, b)).then_inc(hid_mm.sem, 1)

            def broadcast(s, bank, buf, state):
                for rows, cols, toks, _ in PARTS:
                    last = mm(PS[rows, bank, cols], SEL[:, state:state + 1].broadcast_to([128, rows.stop - rows.start]),
                              s.S3[:, buf, toks], True, True)
                return last

            def spread_b(s, g, k, c, buf, off):
                n = k * STEPS + c
                if not at_start(s, g, c):
                    pe.wait_ge(s.b_read.sem, s.b_read.after(g, n))
                for i in range(NC):
                    last = broadcast(s, B_BANK + i, buf, off + c * NC + i)
                last.then_inc(s.b_bc.sem, 1)

            def spread_c(s, g, k, c, buf, off):
                n = k * STEPS + c
                if not at_start(s, g, c):
                    pe.wait_ge(s.prod_ready.sem, s.prod_ready.after(g, n))
                for i in range(NC):
                    last = broadcast(s, C_BANK + i, buf, off + c * NC + i)
                last.then_inc(s.c_bc.sem, 1)

            def spread_a(g, c):
                if c:
                    pe.wait_ge(P.da_ready.sem, P.da_ready.after(g, c))
                for i in range(NC):
                    last = broadcast(P, A_BANK + i, 0, c * NC + i)
                last.then_inc(a_bc.sem, 1)

            def add_states(s, g, k, c):
                pe.wait_ge(s.prod_ready.sem, s.prod_ready.after(g, k * STEPS + c + 1))
                for i in range(NC):
                    last = mm(PS[:, Y_BANK, 0:PK], cm("ident"), PR[:, c % 2, i, :], c == 0 and i == 0,
                              c == STEPS - 1 and i == NC - 1)
                last.then_inc(s.summed.sem, 1)

            def logits(s, g, bank, wm, wr):
                pe.wait_ge(s.ln_x.sem, s.ln_x.after(g, s.ln_x.per_group))
                both(PS[0:EXPERTS, bank, 0:T], s, wm, wr).then_inc(s.logits_mm.sem, 1)

            def logits_T(s, g, bank):
                pe.wait_ge(s.logits_ready.sem, s.logits_ready.after(g, 1))
                for t, a in enumerate(STARTS):
                    last = mm(PS[0:TW, bank, t * EXPERTS:(t + 1) * EXPERTS], s.LW[:, a:a + TW],
                              cm("ident", 0, EXPERTS, p=EXPERTS), True, True)
                last.then_inc(s.logits_T.sem, 1)

            def gates_T(s, g, bank):
                pe.wait_ge(s.gates_ready.sem, s.gates_ready.after(g, 1))
                for t, a in enumerate(STARTS):
                    last = nc.tensor.transpose(PS[0:EXPERTS, bank, a:a + TW], s.gate[0:TW, 5, t, :], cm("ident", 0, TW, p=TW))
                last.then_inc(s.gates_T.sem, 1)

            def biases(s, g, bank01, bank2, bias):
                pe.wait_ge(s.gates_T_ready.sem, s.gates_T_ready.after(g, 1))
                for t, a in enumerate(STARTS):
                    out = PS[0:TW, bank01, t * D:(t + 1) * D] if t < 2 else PS[0:TW, bank2, 0:D]
                    last = mm(out, s.LW[:, a:a + TW], bias, True, True)
                last.then_inc(s.bias_mm.sem, 1)

            def back(s, g, bank_m, bank_r):
                for t, a in enumerate(STARTS):
                    nc.tensor.transpose(PS[:, bank_m, a:a + TW], s.ACC[0:TW, t, 0:DM], cm("ident", 0, TW, p=TW))
                    last = nc.tensor.transpose(PS[0:DR, bank_r, a:a + TW], s.ACC[0:TW, t, DM:D], cm("ident", 0, TW, p=TW))
                last.then_inc(s.back_T.sem, 1)

            def project_in(g, k):
                for z, bank in enumerate((X_BANK, Z_BANK[k])):
                    for rows, cols, toks, feats in PARTS:
                        last = mm(PS[rows, bank, cols], cm("fb"[k] + "in", z * D + feats.start, z * D + feats.stop, p=BN),
                                  HB[:, toks], True, True)
                last.then_inc(in_mm.sem, 1)

            def contract(out, name, main, rest, n):
                mm(out, cm(name, 0, n), main, True, False)
                return mm(out, cm(name + "_r", 0, n, p=DR), rest, False, True)

            def project_states(g, k):
                d, s = "fb"[k], DIRS[k]
                pe.wait_ge(u_ready.sem, u_ready.after(g, k + 1))
                contract(PS[0:RANK, Z_BANK[k], 0:T], d + "xdt", s.UP[:, 0:T], s.URr, RANK).then_inc(dt24_mm.sem, 1)
                contract(PS[:, X_BANK, 0:T], d + "xbc", s.UP[:, 0:T], s.URr, NBLK).then_inc(Q.set_mm.sem, 1)

            def project_steps(g, k):
                pe.wait_ge(dt24_ready.sem, dt24_ready.after(g, k + 1))
                for rows, cols, toks, feats in PARTS:
                    last = mm(PS[rows, Z_BANK[k], cols], cm("fb"[k] + "dtw", feats.start, feats.stop, p=RANK), DT24[:, toks], True, True)
                last.then_inc(dt_mm.sem, 1)

            def direction_out(g, k):
                pe.wait_ge(y_gated.sem, y_gated.after(g, k + 1))
                contract(PS[0:BN, AFTER_BANK[k], 0:T], "fb"[k] + "out", DIRS[k].CV[:, 0:T], DIRS[k].GRr, BN).then_inc(out_mm.sem, 1)
                pe.wait_ge(out_copied.sem, out_copied.after(g, k + 1))
                mm(PS[0:BN, AFTER_BANK[k], 0:T], ones_bn[:, :], DIRS[k].YT, True, True).then_inc(bn_mean.sem, 1)

            def direction_var(g, k):
                pe.wait_ge(bn_squares.sem, bn_squares.after(g, k + 1))
                mm(PS[0:BN, AFTER_BANK[k], 0:T], ones_bn[:, :], Q.SQm[0:BN, :], True, True).then_inc(bn_var.sem, 1)

            def scan_start(g, k):
                pe.wait_ge(Q.set_ready.sem, Q.set_ready.after(g, k + 1))
                pe.wait_ge(dt_raw.sem, dt_raw.after(g, k + 1))
                spread_b(DIRS[k], g, k, 0, 0, 0)
                spread_c(DIRS[k], g, k, 0, 0, NS)

            def token_rows(g):
                for t, a in enumerate(STARTS):
                    bank, col = 2 + t // 2, t % 2 * D
                    mm(PS[0:TW, bank, col:col + DM], M.Xm[:, a:a + TW], cm("ident"), True, True)
                    last = mm(PS[0:TW, bank, col + DM:col + D], M.Xr[:, a:a + TW], cm("ident", 0, DR, p=DR), True, True)
                    if t:
                        last.then_inc(xtok_mm.sem, 1)

            def ranks(g):
                pe.wait_ge(pair_ready.sem, pair_ready.after(g, 1))
                tri = cm("tri", p=TW)
                for t in range(TILES + 1):
                    out = PS[0:TW, 5, t * EXPERTS:(t + 1) * EXPERTS]
                    for u in range(min(t + 1, TILES)):
                        last = mm(out, tri if u == t else ones_tw[:, :], M.gate[0:TW, 5, u, :], u == 0, u == min(t, TILES - 1))
                last.then_inc(ranks_mm.sem, 1)

            def first(gP, gM):
                hasP, hasM = gP is not None, gM is not None
                if hasM:
                    pe.wait_ge(P.residual.sem, P.residual.after(gM, 2))
                    mean(M, P, gM, 0, 5)
                if hasP:
                    pe.wait_ge(s_const[0], 32)
                    pe.wait_ge(s_x, 16 * gP + 16)
                    for k, (lo, hi) in enumerate(((0, DM), (DM, D))):
                        for j in range(KP):
                            last = mm(PS[0:hi - lo, 7 - k, 0:IMG * NP], cm("tok_W", j * D + lo, j * D + hi), xp[:, j, :], j == 0, j == KP - 1)
                        last.then_inc(tok_mm.sem, 1)
                if hasM:
                    variance(M, gM, 0, 5)
                if hasP:
                    pe.wait_ge(P.residual.sem, P.residual.after(gP, 1))
                    mean(P, P, gP, 0, 7)
                    variance(P, gP, 0, 7)
                if hasM:
                    pe.wait_ge(s_const[1], 32)
                    logits(M, gM, 5, cm("r_w"), cr("r_w"))
                    token_rows(gM)
                    logits_T(M, gM, 6)
                if hasP:
                    pe.wait_ge(P.ln_x.sem, P.ln_x.after(gP, 1))
                    hidden(gP, 0, 6)
                if hasM:
                    ranks(gM)
                if hasP:
                    hidden(gP, 6, 11)
                    pe.wait_ge(hid_ready.sem, hid_ready.after(gP, 11))
                    for i, (name, first, count, bank) in enumerate((("m2_w0", 0, 6, 7), ("m2_w1", 6, 3, 0))):
                        for j in range(count):
                            last = mm(PS[:, bank, 0:T], cm(name, j * NBLK, (j + 1) * NBLK), HID[:, first + j, :], j == 0, j == count - 1)
                        last.then_inc(P.set_mm.sem, 1)
                    for rows, cols, toks, feats in PARTS:
                        mm(PS[rows, 1, cols], cm("d_w2", feats.start, feats.stop), HID[:, 9, toks], True, False)
                        last = mm(PS[rows, 1, cols], cr("d_w2", feats.start, feats.stop), HIDr[:, toks], False, True)
                    last.then_inc(delta_mm.sem, 1)
                    pe.wait_ge(P.set_ready.sem, P.set_ready.after(gP, 2))
                    pe.wait_ge(delta_ready.sem, delta_ready.after(gP, 1))
                if hasM:
                    pe.wait_ge(slots_ready.sem, slots_ready.after(gM, 1))
                    pe.wait_ge(xtok_copied.sem, xtok_copied.after(gM, 1))
                if hasP:
                    spread_a(gP, 0)
                    spread_b(P, gP, 0, 0, 0, NS)
                    spread_c(P, gP, 0, 0, 1, 0)
                    for c in range(STEPS):
                        if c + 1 < STEPS:
                            spread_a(gP, c + 1)
                            spread_b(P, gP, 0, c + 1, 0, NS)
                            spread_c(P, gP, 0, c + 1, 1, 0)
                        add_states(P, gP, 0, c)

            first_pass(pe, first)

            def turn(i, p):
                b = 3 * i + p
                pe.wait_ge(s_block[p], 16 * i + 16)
                if not early(b, 1):
                    pe.wait_ge(xt_copied.sem, xt_copied.after(b - 1, 1))
                mm(PS[:, TURN_BANK, 0:128], XB[:, p, 0:DM], cm("ident"), True, True)
                mm(PS[0:DR, TURN_BANK, 128:256], XB[:, p, DM:D], cm("ident"), True, True).then_inc(t_mm.sem, 1)

            def widen(i, p):
                b = 3 * i + p
                pe.wait_ge(xt_copied.sem, xt_copied.after(b, 1))
                pe.wait_ge(s_weights[p], 48 * i + 48)
                if not early(b, 3):
                    pe.wait_ge(gelu_ready.sem, gelu_ready.after(b - 3, 2))
                for h in range(2):
                    for j in range(HALF_FT):
                        out, f = PS[:, WIDE_BANK + 2 * p + h, j * 128:(j + 1) * 128], h * HALF_FT + j
                        mm(out, WX[:, p, f * 128:(f + 1) * 128], XTm[:, p, :], True, False)
                        last = mm(out, WXR[:, p, f * 128:(f + 1) * 128], XTr[:, p, :], False, True)
                    last.then_inc(wide_mm.sem, 1)

            def narrow(i, p):
                b = 3 * i + p
                pe.wait_ge(gelu_ready.sem, gelu_ready.after(b, 2))
                if not early(b, 1):
                    pe.wait_ge(y_copied.sem, y_copied.after(b - 1, 1))
                out = PS[:, OUT_BANK, 0:D]
                mm(out, ones_row[:, :], WXB[:, p, :], True, False)
                for f in range(FT):
                    w = FFN + f * D
                    last = mm(out, HX[:, p, f, :], WX[:, p, w:w + D], False, f == FT - 1)
                last.then_inc(narrow_mm.sem, 1)

            def experts(i, p):
                b = 3 * i + p
                widen(i, p)
                if not is_end(b):
                    turn(*follower(i, p))
                if not early(b, 1):
                    narrow(*previous(i, p))

            turn(0, 0)
            over_blocks(pe, experts)
            narrow(BLOCKS // 3 - 1, 2)

            def second_mixture(g, beside, u):
                t, j, bank = u // 4, u % 4, (7, 4)[u % 2]
                if u == 0:
                    pe.wait_ge(Q.acc_started.sem, Q.acc_started.after(g, 1))
                    if beside is not None:
                        pe.wait_ge(bn_log.sem, bn_log.after(beside, 1))
                elif u >= 2:
                    pe.wait_ge(lin_acc.sem, lin_acc.after(g, 2 * (u - 1)))
                a = STARTS[t]
                mm(PS[0:TW, bank, 0:2 * D], Q.Xm[:, a:a + TW], cm("ew", 2 * j * D, 2 * (j + 1) * D), True, False)
                mm(PS[0:TW, bank, 0:2 * D], Q.Xr[:, a:a + TW], cr("ew", 2 * j * D, 2 * (j + 1) * D), False, True).then_inc(lin_mm.sem, 1)

            def part_a(g, tail):
                if g is not None:
                    scan_start(g, 0)
                if tail is not None:
                    pe.wait_ge(final.sem, final.after(tail, 0))
                for c in range(STEPS):
                    if g is not None and c + 1 < STEPS:
                        spread_b(FW, g, 0, c + 1, 0, 0)
                    if tail is not None:
                        if c == 0:
                            direction_out(tail, 1)
                        if c == 6:
                            logits(Q, tail, 5, cm("er_w"), cr("er_w"))
                    if g is not None and c == 2:
                        project_states(g, 1)
                    if g is not None and c + 1 < STEPS:
                        spread_c(FW, g, 0, c + 1, 0, NS)
                    if g is not None and c == 0:
                        project_in(g, 1)
                    if tail is not None:
                        if c == 1:
                            direction_var(tail, 1)
                        if c == 2:
                            pe.wait_ge(y_sum.sem, y_sum.after(tail, 1))
                            mm(PS[:, 5, 0:T], cm("up", 0, DM, p=BN), YS[:, 0, :], True, True)
                            mm(PS[0:DR, 4, 0:T], cm("up", DM, D, p=BN), YS[:, 0, :], True, True).then_inc(up_proj.sem, 1)
                        if c == 3:
                            pe.wait_ge(Q.residual.sem, Q.residual.after(tail, 1))
                            mean(Q, Q, tail, 0, 5)
                        if c == 4:
                            variance(Q, tail, 0, 5)
                        if c == 6:
                            logits_T(Q, tail, 4)
                    if g is not None and c == 2:
                        project_steps(g, 1)
                if tail is not None:
                    gates_T(Q, tail, 5)

            def part_b(g, tail, nxt):
                if g is not None:
                    scan_start(g, 1)
                if tail is not None:
                    biases(Q, tail, 5, 4, cm("eb", p=EXPERTS))
                for c in range(STEPS):
                    if g is not None and c + 1 < STEPS:
                        spread_b(BW, g, 1, c + 1, 0, 0)
                    if g is not None:
                        if c == 0:
                            direction_out(g, 0)
                        if c == 1:
                            direction_var(g, 0)
                    if nxt is not None and c == 5:
                        project_steps(nxt, 0)
                    if tail is not None and 2 <= c < STEPS - 1:
                        second_mixture(tail, g, 2 * c - 2)
                    if g is not None and c + 1 < STEPS:
                        spread_c(BW, g, 1, c + 1, 0, NS)
                    if nxt is not None:
                        if c == 0:
                            pe.wait_ge(mixed.sem, mixed.after(nxt, TILES))
                            back(M, nxt, 5, 6)
                        if c == 1:
                            pe.wait_ge(M.residual.sem, M.residual.after(nxt, 1))
                            mean(L, L, nxt, 0, 5)
                        if c == 2:
                            variance(L, nxt, 0, 5)
                        if c == 3:
                            pe.wait_ge(L.ln_x.sem, L.ln_x.after(nxt, 1))
                            both(PS[0:BN, 5, 0:T], L, cm("down"), cr("down")).then_inc(bott_mm.sem, 1)
                            pe.wait_ge(bott_ready.sem, bott_ready.after(nxt, 1))
                            project_in(nxt, 0)
                        if c == 4:
                            project_states(nxt, 0)
                    if tail is not None:
                        if c == 1:
                            second_mixture(tail, g, 0)
                            second_mixture(tail, g, 1)
                        if 2 <= c < STEPS - 1:
                            second_mixture(tail, g, 2 * c - 1)
                if tail is not None:
                    pe.wait_ge(lin_acc.sem, lin_acc.after(tail, TILES * EXPERTS))
                    back(Q, tail, 7, 4)

            second_pass(pe, part_a, part_b)


def _rows(a):
    a = np.asarray(a)
    return a.reshape(a.shape[0], -1)


def _main_rest(v):
    v = np.asarray(v).reshape(D, -1)
    return np.concatenate([v[0:DM], np.concatenate([v[DM:D], v[DM:D]])], axis=1)


def _state_columns(parts):
    rows = parts[0].shape[0]
    out = np.zeros((rows, 4, 2, NS), np.float32)
    for i, w in parts.items() if isinstance(parts, dict) else enumerate(parts):
        out[:, :, i, :] = np.asarray(w)[:, None, :]
    return out.reshape(rows, NBLK)


def _arrays(inp):
    I = {k: np.asarray(v) for k, v in inp.items()}
    x = I["x"].reshape(GROUPS, IMG, 3, GRID, 16, GRID, 16).transpose(0, 2, 4, 6, 1, 3, 5)
    x_p = np.ascontiguousarray(x.reshape(GROUPS, KP, 128, IMG * NP).transpose(0, 2, 1, 3))
    c128, c64 = np.zeros((128, C128), np.float32), np.zeros((DR, C64), np.float32)

    def put(name, a):
        a = _rows(a)
        at, width = AT[name]
        assert a.shape[1] == width, (name, a.shape, width)
        c128[0:a.shape[0], at:at + width] = a

    def put_both(name, w):
        w = _rows(w)
        put(name, w[0:DM])
        at, width = ATR[name]
        c64[:, at:at + width] = w[DM:D]

    put("tok_W", I["L0_tok_W"].reshape(KP, 128, D).transpose(1, 0, 2))
    near = np.arange(GRID) * 14 // GRID
    pos = I["L0_tok_positions"][0][:, near][:, :, near].reshape(D, NP)
    put("posm", pos[0:DM])
    put("posr", pos[DM:D])
    put("tok_b", _main_rest(I["L0_tok_b"]))
    cls = np.stack([I["cls_tok"][0, 0], I["L0_tok_cls_embedding"][0, 0]], axis=1)
    put("cls_m", cls[0:DM])
    put("cls_r", cls[DM:D])
    put("ident", np.eye(128, dtype=np.float32))
    put("log_dt", _main_rest(I["L0_attn_log_dt"]))
    row = np.arange(128) % 32
    put("sign", np.where(row < NS, -1.0, 1.0).astype(np.float32)[:, None])
    a = "L0_attn_"
    put_both("m1_w", np.concatenate([I[a + n + "_w1"] for n in "ABCd"], axis=1))
    b1 = np.concatenate([I[a + n + "_b1"] for n in "ABCd"])
    b1 = np.concatenate([b1, np.zeros(64, np.float32)]).reshape(11, 128).T
    put("m1_b", b1)
    none = np.zeros((128, NS), np.float32)
    w2 = {n: I[a + n + "_w2"].reshape(3, 128, NS) for n in "ABC"}
    put("m2_w0", np.stack([_state_columns([w2["A"][j], none]) for j in range(3)] +
                          [_state_columns([none, w2["B"][j]]) for j in range(3)], axis=1))
    put("m2_w1", np.stack([_state_columns([w2["C"][j], none]) for j in range(3)], axis=1))
    bias = [_state_columns([I[a + "A_b2"][None], I[a + "B_b2"][None]]), _state_columns([I[a + "C_b2"][None], none[0:1]])]
    put("m2_b", np.stack([b[0] for b in bias], axis=1))
    put_both("d_w2", I[a + "d_w2"])
    put("d_b2", _main_rest(I[a + "d_b2"]))
    put("D0", _main_rest(I[a + "D_param"]))
    put("rank", np.broadcast_to(np.arange(EXPERTS, 0, -1, dtype=np.float32), (128, EXPERTS)))
    put_both("r_w", I["L0_ffn_Wr"].T)
    put("eoff", np.broadcast_to(np.arange(EXPERTS, dtype=np.float32) * CAP_BLOCKS * 128, (128, EXPERTS)))
    put("blk", np.broadcast_to(np.arange(CAP_BLOCKS, dtype=np.float32) * 128, (128, CAP_BLOCKS)))
    e = np.arange(EXPERTS)
    put("below", np.broadcast_to((e[None, :] < e[:, None]).astype(np.float32).reshape(1, -1), (128, EXPERTS * EXPERTS)))
    put("bid", np.broadcast_to(np.arange(BLOCKS, dtype=np.float32), (128, BLOCKS)))
    t = np.arange(TW)
    put("tri", (t[:, None] < t[None, :]).astype(np.float32))
    wi = I["L0_ffn_Wi"].transpose(0, 2, 1)
    wo = I["L0_ffn_Wo"].reshape(EXPERTS, D, FT, 128).transpose(0, 3, 2, 1).reshape(EXPERTS, 128, FT * D)
    bi = I["L0_ffn_bi"].reshape(EXPERTS, FT, 128).transpose(0, 2, 1)
    ex_m = np.ascontiguousarray(np.concatenate([wi[:, 0:DM], wo, bi], axis=2))
    ex_r = np.ascontiguousarray(wi[:, DM:D])
    ex_b = np.ascontiguousarray(I["L0_ffn_bo"].reshape(EXPERTS, 1, D))
    b = "L1_attn_"
    put_both("down", I[b + "down_W"])
    put("down_b", I[b + "down_b"][:, None])
    put("up", I[b + "up_W"])
    put("up_b", _main_rest(I[b + "up_b"]))
    for d in "fb":
        p = b + d + "_"
        put(d + "in", I[p + "in_W"])
        put(d + "cw", _main_rest(I[p + "conv_w"]))
        put(d + "cb", _main_rest(I[p + "conv_b"]))
        xw = _main_rest(I[p + "xproj_W"]).reshape(128, 2, RANK + 2 * NS)
        for h, tail in enumerate(("", "_r")):
            put(d + "xdt" + tail, xw[:, h, 0:RANK])
            put(d + "xbc" + tail, _state_columns([xw[:, h, RANK:RANK + NS], xw[:, h, RANK + NS:]]))
        put(d + "dtw", I[p + "dt_W"])
        put(d + "dtb", _main_rest(I[p + "dt_b"]))
        put(d + "Alog", _main_rest(I[p + "A_log"]))
        put(d + "Dp", _main_rest(I[p + "D"]))
        ow = _main_rest(I[p + "out_W"]).reshape(128, 2, BN)
        put(d + "out", ow[:, 0])
        put(d + "out_r", ow[:, 1])
        put(d + "lng", np.stack([I[p + "ln_g"], I[p + "ln_b"]], axis=1))
    put_both("er_w", I["L1_ffn_router_w"].T)
    put("er_b", I["L1_ffn_router_b"][:, None])
    put_both("ew", I["L1_ffn_expert_w"].transpose(2, 0, 1))
    put("eb", I["L1_ffn_expert_b"])
    r, n = np.arange(128)[:, None], np.arange(2 * NS)[None, :]
    sel = ((r % 32 == n) & (r // 32 != 1)).astype(np.float32)
    return {"x_p": x_p, "c128": c128, "c64": c64, "sel_d": sel, "ex_m": ex_m, "ex_r": ex_r, "ex_b": ex_b}


def kernel(**inputs):
    import concourse.bacc as bacc
    from concourse.bass_utils import run_bass_kernel_spmd

    nc = bacc.Bacc("TRN2", target_bir_lowering=False, num_devices=1)
    arrays = _arrays(inputs)
    args = [nc.dram_tensor(n, a.shape, mybir.dt.from_np(a.dtype), kind="ExternalInput").ap() for n, a in arrays.items()]
    out_m = nc.dram_tensor("out_m", (GROUPS, DM, T), mybir.dt.float32, kind="ExternalOutput").ap()
    out_r = nc.dram_tensor("out_r", (GROUPS, DR, T), mybir.dt.float32, kind="ExternalOutput").ap()
    vit_tower(nc, *args, out_m, out_r)
    got = run_bass_kernel_spmd(nc, [arrays], core_ids=[0]).results[0]
    both = np.concatenate([got["out_m"], got["out_r"]], axis=1).reshape(GROUPS, D, IMG, SEQ)
    return np.ascontiguousarray(both.transpose(0, 2, 3, 1).reshape(BATCH, SEQ, D))
```

```python
import numpy as np
import concourse.bass as bass
from concourse import mybir
from contextlib import ExitStack

BATCH, SEQ, D = 32, 38, 192
GROUPS = 4
IMG = BATCH // GROUPS
T = IMG * SEQ
HALF = T // 2
GRID = 6
NP = GRID * GRID
KP, PDIM = 6, 128
DM, DR = 128, 64
PK = T + HALF
NSEQ = PK // SEQ
NS = 16
NC = 2
STEPS = NS // NC
EXPERTS, FFN = 8, 768
FT = FFN // 128
BN, RANK = 96, 24
TILES, TW = 3, 102
STARTS = (0, 101, 202)
EPS = 1e-5
A_MIN, A_MAX = 1e-13, 3e22
RESTART = 1e16
PAIRS = GROUPS * TILES * TW * 2
CAP_BLOCKS = -(-GROUPS * TILES * TW // 128)
BLOCKS = (PAIRS + EXPERTS * 127) // 128
assert BLOCKS % 3 == 0
SCATTERS = 16 * (2 * TILES + 1)
M_CHAIN = 17
NBLK = 128


def _layout(widths):
    at, out = 0, {}
    for name, width in widths:
        out[name] = (at, width)
        at += width
    return out, at


W128 = [
    ("tok_W", KP * D), ("posm", NP), ("posr", NP), ("tok_b", 2), ("cls_m", 2), ("cls_r", 2),
    ("ident", 128), ("log_dt", 2), ("sign", 1), ("fAlog", 2 * NS), ("bAlog", 2 * NS),
    ("m1_w", 1344), ("m1_b", 11), ("m2_w0", 6 * NBLK), ("m2_w1", 3 * NBLK), ("m2_b", 2),
    ("d_w2", D), ("d_b2", 2), ("D0", 2), ("rank", EXPERTS),
    ("r_w", EXPERTS), ("eoff", EXPERTS), ("blk", CAP_BLOCKS), ("below", EXPERTS * EXPERTS), ("bid", BLOCKS), ("tri", TW),
    ("down", BN), ("down_b", 1), ("up", D), ("up_b", 2),
]
for _d in "fb":
    W128 += [(_d + "in", 2 * D), (_d + "cw", 8), (_d + "cb", 2), (_d + "xdt", RANK), (_d + "xbc", NBLK),
             (_d + "xdt_r", RANK), (_d + "xbc_r", NBLK), (_d + "dtw", D), (_d + "dtb", 2),
             (_d + "Dp", 2), (_d + "out", BN), (_d + "out_r", BN), (_d + "lng", 2)]
W128 += [("er_w", EXPERTS), ("er_b", 1), ("ew", EXPERTS * D), ("eb", D)]
AT, C128 = _layout(W128)
W64 = [("m1_w", 1344), ("d_w2", D), ("r_w", EXPERTS), ("down", BN),
       ("er_w", EXPERTS), ("ew", EXPERTS * D)]
ATR, C64 = _layout(W64)
SEG128 = [0, AT["rank"][0], AT["down"][0], C128]
SEG64 = [0, ATR["r_w"][0], ATR["down"][0], C64]


class Signal:

    def __init__(self, sem, per_group, start=0):
        self.sem, self.per_group, self.start = sem, per_group, start

    def after(self, g, k):
        return g * self.per_group + (self.start + k)


def later(signal):
    return Signal(signal.sem, signal.per_group, GROUPS * signal.per_group)


class Stage:
    pass


def vit_tower(nc, x_p, c128, c64, sel_d, ex_m, ex_r, ex_b, out_m, out_r):
    fp32, bf16, i32, u32 = mybir.dt.float32, mybir.dt.bfloat16, mybir.dt.int32, mybir.dt.uint32
    ALU, ACT, AX = mybir.AluOpType, mybir.ActivationFunctionType, mybir.AxisListType
    with ExitStack() as ctx:
        def sb(name, shape, dt=fp32):
            return ctx.enter_context(nc.sbuf_tensor(name, shape, dt))

        def sem(name):
            return ctx.enter_context(nc.semaphore(name))

        def sig(name, per_group):
            return Signal(sem(name), per_group)

        CM = sb("CM", [128, C128])
        CR = sb("CR", [DR, C64])
        SELF = sb("SELF", [128, 2 * NS])
        SEL = sb("SEL", [128, 2 * NS], bf16)
        ones_d = sb("ones_d", [128, 128])
        ones_bn = sb("ones_bn", [BN, BN])
        eps_col = sb("eps_col", [128, 1])
        posb_m = sb("posb_m", [128, NP])
        posb_r = sb("posb_r", [DR, NP])
        dt0 = sb("dt0", [128, 2])
        neg_dt0 = sb("neg_dt0", [128, 2])
        negA = sb("negA", [128, 4 * NS])

        def cm(name, a=0, b=None, p=128, p0=0):
            at, width = AT[name]
            return CM[p0:p, at + a:at + (width if b is None else b)]

        def cr(name, a=0, b=None):
            at, width = ATR[name]
            return CR[:, at + a:at + (width if b is None else b)]

        WX = sb("WX", [128, 3, FFN + FT * D + FT])
        WXR = sb("WXR", [DR, 3, FFN])
        WXB = sb("WXB", [1, 3, D])
        ones_row = sb("ones_row", [1, 128])
        ones_tw = sb("ones_tw", [TW, TW])

        P, M, Q = Stage(), Stage(), Stage()
        L = Stage()
        FW, BW = Stage(), Stage()
        PREP, GATED, NORM = Stage(), Stage(), Stage()

        def residual_buffers(s, name):
            s.Hm, s.Hr = sb(name + "_Hm", [128, T]), sb(name + "_Hr", [DR, T])
            s.Xm, s.Xr = sb(name + "_Xm", [128, T]), sb(name + "_Xr", [DR, T])

        def norm_buffers(s, name):
            s.Cm, s.Cr = sb(name + "_Cm", [128, T]), sb(name + "_Cr", [DR, T])
            s.VE = sb(name + "_VE", [128, T])
            s.RS = sb(name + "_RS", [128, T])
            s.SQm = s.RS[:, :]
            s.SQr = sb(name + "_SQr", [DR, T])

        def gate_buffers(s, name):
            s.LW = sb(name + "_LW", [EXPERTS, T])
            s.gate = sb(name + "_gate", [128, 8, TILES, EXPERTS])
            s.gs = sb(name + "_gs", [128, 8, TILES])
            s.ACC = sb(name + "_ACC", [128, TILES, D])

        def scan_buffers(s, name, sets):
            s.V = sb(name + "_V", [NBLK, T])
            s.R = sb(name + "_R", [NBLK, T])
            s.S3 = sb(name + "_S3", [NBLK, sets, T], bf16)
            s.DL = sb(name + "_DL", [128, PK])
            s.UP = sb(name + "_UP", [128, PK])
            s.OM = sb(name + "_OM", [128, PK])
            s.WV = sb(name + "_WV", [128, PK])
            s.TM = sb(name + "_TM", [128, PK])

        for s, name in ((P, "p"), (M, "m"), (Q, "q")):
            residual_buffers(s, name)
        norm_buffers(P, "p")
        norm_buffers(Q, "q")
        M.Cm, M.Cr, M.VE, M.RS, M.SQm, M.SQr = Q.Cm, Q.Cr, Q.VE, Q.RS, Q.SQm, Q.SQr
        gate_buffers(M, "m")
        gate_buffers(Q, "q")
        scan_buffers(P, "p", 2)
        scan_buffers(Q, "q", 1)
        xp = sb("xp", [128, KP, IMG * NP])
        HID = sb("HID", [128, 10, T])
        HIDr = sb("HIDr", [DR, T])
        HB = sb("HB", [BN, T])
        ZS = sb("ZS", [128, PK])
        YS = sb("YS", [BN, 2, T])
        Om = sb("Om", [128, T])
        Or = sb("Or", [DR, T])
        dA = sb("dA", [128, 2, NC, PK])
        aP = sb("aP", [128, 2, NC, PK])
        BB = sb("BB", [128, 2, NC, PK])
        PR = sb("PR", [128, 2, NC, PK])
        ST = sb("ST", [128, NC, PK])
        KEEP = sb("KEEP", [TW, TILES, 2 * EXPERTS + 4])
        run = sb("run", [TW, EXPERTS])
        slot_u = sb("slot_u", [TW, TILES, 2], u32)
        counts = sb("counts", [TW, 6, EXPERTS])
        steps80 = sb("steps80", [TW, EXPERTS, CAP_BLOCKS])
        block_f = sb("block_f", [TW, 5, BLOCKS])
        tab_rows = sb("tab_rows", [1, BLOCKS], i32)
        tab_expert = sb("tab_expert", [1, BLOCKS], i32)
        XTm = sb("XTm", [128, 3, 128])
        XTr = sb("XTr", [DR, 3, 128])
        YSUM = HID[:, :, :].rearrange("p j t -> p (j t)")[:, 3 * T:3 * T + PK]
        PAIR = xp[:, :, :].rearrange("p k t -> p (k t)")[:, 2 * TILES * D:2 * TILES * D + PK]
        passed = BB[0:TW, :, :, :].rearrange("p a n k -> p (a n k)")[:, 0:2 * BLOCKS * EXPERTS].rearrange("p (a b e) -> p a b e", a=2, e=EXPERTS)
        BASE = Q.UP
        YSUM1, PAIR1 = Q.TM[:, :], Q.OM[:, :]
        HX = HID[:, :, :].rearrange("p j t -> p (j t)")[:, 0:3 * FT * 128].rearrange("p (b f t) -> p b f t", f=FT, t=128)
        XB, YB = (xp[:, :, :].rearrange("p k t -> p (k t)")[:, j * 3 * D:(j + 1) * 3 * D].rearrange("p (b n) -> p b n", n=D)
                  for j in range(2))
        GA = xp[0:TW, :, :].rearrange("p k t -> p (k t)")[:, 0:2 * TILES * D].rearrange("p (t k n) -> p t k n", k=2, n=D)
        XTOK = M.ACC
        ZERO = WX[:, 0, 0:CAP_BLOCKS * EXPERTS * D // 8]
        XS = aP[:, 0, 0, :]
        LZ = aP[:, 0, 1, :]
        DT24 = aP[0:RANK, 1, 1, 0:T]
        for s, src, z, ur, gr in ((FW, Q, ZS[:, :], P.Xr[:, :], HIDr[:, :]),
                                  (BW, P, aP[:, 1, 0, :], P.Xm[0:DR, :], HID[0:DR, 2, :])):
            s.V, s.R, s.S3, s.DL, s.UP, s.OM, s.WV, s.TM = src.V, src.R, src.S3, src.DL, src.UP, src.OM, src.WV, src.TM
            s.CV = src.WV[:, :]
            s.YT = src.V[0:BN, :]
            s.ZS, s.URr, s.GRr = z, ur, gr
        DIRS = (FW, BW)
        L.Cm, L.Cr, L.VE, L.RS, L.SQm, L.SQr, L.Xm, L.Xr = P.Cm, P.Cr, P.VE, P.RS, P.SQm, P.SQr, M.Xm, M.Xr
        L.Hm, L.Hr = P.Hm, P.Hr
        HBm, HBr = HID[:, 0, :], HID[0:DR, 1, :]

        PS = ctx.enter_context(nc.psum_tensor("PS", [128, 8, 512], fp32))
        B_BANK, C_BANK, A_BANK = 0, 2, 5
        HIDDEN_BANKS = (4, 4, 4, 4, 7, 4, 4, 7, 4, 4, 7)
        HIDDEN_BEFORE = (None, 0, 1, 2, None, 3, 5, 4, 6, 8, None)
        X_BANK, Z_BANK, AFTER_BANK = 6, (5, 7), (7, 5)

        slots_d = nc.dram_tensor("slots_d", [EXPERTS * CAP_BLOCKS * 128, D], fp32, kind="Internal").ap()
        outs_d = nc.dram_tensor("outs_d", [BLOCKS * 128, D], fp32, kind="Internal").ap()
        h_md = nc.dram_tensor("h_md", [GROUPS, DM, T], fp32, kind="Internal").ap()
        h_rd = nc.dram_tensor("h_rd", [GROUPS, DR, T], fp32, kind="Internal").ap()
        keep_d = nc.dram_tensor("keep_d", [GROUPS, TW, TILES * (2 * EXPERTS + 4)], fp32, kind="Internal").ap()

        s_const = [sem(f"s_const{i}") for i in range(3)]
        s_sel = sem("s_sel")
        s_x = sem("s_x")
        turn_taken = sem("turn_taken")
        s_zero = sem("s_zero")
        h_stored, scattered, scatter_free = sig("h_stored", 32), sig("scattered", SCATTERS), sig("scatter_free", 1)
        s_block = [sem(f"s_block{i}") for i in range(3)]
        s_weights = [sem(f"s_weights{i}") for i in range(3)]
        out_rows = [sem(f"out_rows{i}") for i in range(3)]
        h_loaded, keep_loaded, gathered = sig("h_loaded", 32), sig("keep_loaded", 16), sig("gathered", 16 * 2 * TILES)
        stored, out_free = sig("stored", 32), sig("out_free", 1)
        sel_ready, prep_pool, prep_act = sem("sel_ready"), sem("prep_pool"), sem("prep_act")

        def norm_signals(s, n, count):
            s.ln_mean, s.ln_var = sig(n + "_ln_mean", count), sig(n + "_ln_var", count)
            s.ln_centred, s.ln_squares = sig(n + "_ln_centred", 2 * count), sig(n + "_ln_squares", 2 * count)
            s.ln_log, s.ln_rstd, s.ln_x = sig(n + "_ln_log", count), sig(n + "_ln_rstd", count), sig(n + "_ln_x", count)

        def gate_signals(s, n):
            s.logits_mm, s.logits_ready, s.logits_T = sig(n + "_logits_mm", 1), sig(n + "_logits_ready", 1), sig(n + "_logits_T", 1)
            s.gap_ready, s.ratio_ready = sig(n + "_gap_ready", 1), sig(n + "_ratio_ready", 1)
            s.gates_ready, s.gates_T, s.gates_T_ready = sig(n + "_gates_ready", 1), sig(n + "_gates_T", 1), sig(n + "_gates_T_ready", 1)
            s.bias_mm, s.acc_started, s.back_T = sig(n + "_bias_mm", 1), sig(n + "_acc_started", 1), sig(n + "_back_T", 1)

        def scan_signals(s, n, count):
            s.set_mm, s.set_copied, s.set_ready = sig(n + "_set_mm", 2), sig(n + "_set_copied", 4), sig(n + "_set_ready", 2)
            s.b_bc, s.c_bc, s.da_ready, s.b_read = (sig(n + x, count * STEPS) for x in ("_b_bc", "_c_bc", "_da_ready", "_b_read"))
            s.scanned, s.prod_ready, s.summed = (sig(n + x, count * STEPS) for x in ("_scanned", "_prod_ready", "_summed"))
            s.w_ready = sig(n + "_w_ready", count)

        norm_signals(P, "p", 1)
        norm_signals(M, "m", 1)
        for s, was in ((L, M), (Q, P)):
            s.ln_mean, s.ln_var, s.ln_centred, s.ln_squares = (later(x) for x in (was.ln_mean, was.ln_var, was.ln_centred, was.ln_squares))
            s.ln_log, s.ln_rstd, s.ln_x = later(was.ln_log), later(was.ln_rstd), later(was.ln_x)
        gate_signals(M, "m")
        gate_signals(Q, "q")
        scan_signals(P, "p", 1)
        scan_signals(Q, "q", 2)
        for s in (FW, BW):
            s.set_mm, s.set_copied, s.set_ready = Q.set_mm, Q.set_copied, Q.set_ready
            s.b_bc, s.c_bc, s.da_ready, s.b_read = Q.b_bc, Q.c_bc, Q.da_ready, Q.b_read
            s.scanned, s.prod_ready, s.summed = Q.scanned, Q.prod_ready, Q.summed
        P.residual, M.residual, Q.residual = sig("p_residual", 1), sig("m_residual", 1), sig("q_residual", 1)
        P.chain, M.chain, Q.chain = sig("p_chain", 6), sig("m_chain", M_CHAIN), sig("q_chain", 19)
        PREP.chain, GATED.chain, NORM.chain = sig("prep_chain", 20), sig("gated_chain", 2), sig("norm_chain", 2)
        P.work, FW.work, BW.work = P, PREP, PREP
        hb_copied = sig("hb_copied", 1)
        xtok_mm, xtok_copied = sig("xtok_mm", 2), sig("xtok_copied", 2)
        scan_out, y1_added = sig("scan_out", 1), sig("y1_added", STEPS)
        pair_ready, ranks_mm, slots_ready = sig("pair_ready", 1), sig("ranks_mm", 1), sig("slots_ready", 1)
        table, table_ready = sem("table"), sem("table_ready")
        t_mm, xt_copied, wide_mm, gelu_ready = sig("t_mm", 1), sig("xt_copied", 1), sig("wide_mm", 2), sig("gelu_ready", 2)
        narrow_mm, y_copied = sig("narrow_mm", 1), sig("y_copied", 1)
        rows_ready, rows_chain, mixed = sig("rows_ready", 1), sig("rows_chain", 3), sig("mixed", TILES)
        final = Signal(sem("final"), 1, start=1)
        y_added = sig("y_added", 2 * STEPS)
        tok_mm = sig("tok_mm", 2)
        hid_mm, hid_ready = sig("hid_mm", 11), sig("hid_ready", 11)
        abs_ready = sig("abs_ready", 1)
        delta_mm, delta_ready, packed_x = sig("delta_mm", 1), sig("delta_ready", 1), sig("packed_x", 1)
        a_bc = sig("a_bc", STEPS)
        ap_ready, b_times_a = sig("ap_ready", STEPS), sig("b_times_a", STEPS)
        lin_mm, lin_acc = sig("lin_mm", TILES * EXPERTS // 2), sig("lin_acc", TILES * EXPERTS)
        shift_ready, shift_exp = sig("shift_ready", 1), sig("shift_exp", 1)
        bott_mm, bott_ready = sig("bott_mm", 1), sig("bott_ready", 1)
        in_mm, in_copied, conv_ready, u_ready = sig("in_mm", 2), sig("in_copied", 2), sig("conv_ready", 2), sig("u_ready", 2)
        dt24_mm, dt24_ready, dt_mm, dt_raw = sig("dt24_mm", 2), sig("dt24_ready", 2), sig("dt_mm", 2), sig("dt_raw", 2)
        abs_dt, exp_dt, log_dt_ready = sig("abs_dt", 2), sig("exp_dt", 2), sig("log_dt_ready", 2)
        y_gated, out_mm, out_copied = sig("y_gated", 2), sig("out_mm", 2), sig("out_copied", 2)
        bn_mean, bn_centred, bn_squares, bn_var = sig("bn_mean", 2), sig("bn_centred", 2), sig("bn_squares", 2), sig("bn_var", 2)
        bn_log, bn_rstd, bn_done = sig("bn_log", 2), sig("bn_rstd", 2), sig("bn_done", 2)
        y_sum, up_proj = sig("y_sum", 1), sig("up_proj", 1)

        block = ctx.enter_context(nc.Block())

        TURN_BANK, OUT_BANK, WIDE_BANK = 0, 1, 2
        HALF_FT = FT // 2

        def seqs(ap):
            return ap.rearrange("p (s t) -> p s t", t=SEQ)

        PARTS = [(slice(0, 128), slice(0, T), slice(0, T), slice(0, DM)),
                 (slice(0, DR), slice(T, PK), slice(0, HALF), slice(DM, D)),
                 (slice(DR, 128), slice(T, PK), slice(HALF, T), slice(DM, D))]
        MAIN_REST = (slice(0, T), slice(T, PK))

        def first_pass(eng, body):
            body(None, 0, None)
            body(0, 1, None)
            with eng.Fori(1, GROUPS - 1) as i:
                body(i, i + 1, i - 1)
            body(GROUPS - 1, None, GROUPS - 2)
            body(None, None, GROUPS - 1)

        def over_blocks(eng, body):
            for p in range(3):
                body(0, p)
            with eng.Fori(1, BLOCKS // 3 - 1) as i:
                for p in range(3):
                    body(i, p)
            for p in range(3):
                body(BLOCKS // 3 - 1, p)

        def second_pass(eng, part_a, part_b):
            part_b(None, None, 0)
            part_a(0, None)
            part_b(0, None, 1)
            with eng.Fori(1, GROUPS - 1) as g:
                part_a(g, g - 1)
                part_b(g, g - 1, g + 1)
            part_a(GROUPS - 1, GROUPS - 2)
            part_b(GROUPS - 1, GROUPS - 2, None)
            part_a(None, GROUPS - 1)
            part_b(None, GROUPS - 1, None)

        def follower(i, p):
            return (i, p + 1) if p < 2 else (i + 1, 0)

        def previous(i, p):
            return (i, p - 1) if p else (i - 1, 2)

        def is_end(b):
            return isinstance(b, int) and b == BLOCKS - 1

        def early(b, n):
            return isinstance(b, int) and b < n

        def is_first(g):
            return isinstance(g, int) and g == 0

        def at_start(s, g, c):
            return c == 0 and (s is P or s is FW and is_first(g))

        def is_last(g):
            return isinstance(g, int) and g == GROUPS - 1

        @block.sync
        def _(sp):
            sp.dma_start(xp[:, :, :], x_p[0, :, :, :]).then_inc(s_x, 16)

            for i in range(3):
                a, b = SEG128[i], SEG128[i + 1]
                sp.dma_start(CM[:, a:b], c128[:, a:b]).then_inc(s_const[i], 16)
                a, b = SEG64[i], SEG64[i + 1]
                sp.dma_start(CR[:, a:b], c64[:, a:b]).then_inc(s_const[i], 16)
            sp.wait_ge(prep_pool, 2)
            zeros = slots_d.rearrange("(p j r) n -> p j (r n)", p=128, j=8)
            for j in range(8):
                sp.dma_start(zeros[:, j, :], ZERO).then_inc(s_zero, 16)

            def first(s, p, m):
                if m is not None:
                    sp.wait_ge(scan_out.sem, scan_out.after(m, 1))
                    sp.dma_start(h_md[bass.ds(m, 1), :, :].rearrange("g p t -> p (g t)"), M.Hm[:, :]).then_inc(h_stored.sem, 16)
                    sp.dma_start(h_rd[bass.ds(m, 1), :, :].rearrange("g p t -> p (g t)"), M.Hr[:, :]).then_inc(h_stored.sem, 16)
                if p is not None and not is_last(p):
                    sp.wait_ge(tok_mm.sem, tok_mm.after(p, 2))
                    sp.dma_start(xp[:, :, :], x_p[bass.ds(p + 1, 1), :, :, :].rearrange("g p k t -> p (g k) t")).then_inc(s_x, 16)

            first(None, 0, None)
            first(0, 1, None)
            with sp.Fori(1, GROUPS - 2) as i:
                first(i, i + 1, i - 1)
            first(GROUPS - 2, GROUPS - 1, GROUPS - 3)
            first(GROUPS - 1, None, GROUPS - 2)
            first(None, None, GROUPS - 1)

            sp.wait_ge(table_ready, 1)
            sp.wait_ge(s_zero, 128)
            sp.wait_ge(scattered.sem, scattered.after(GROUPS, 0))

            def load_block(i, p):
                b = 3 * i + p
                place = sp.value_load(tab_rows[0:1, bass.ds(b, 1)], min_val=0, max_val=EXPERTS * CAP_BLOCKS - 1)
                expert = sp.value_load(tab_expert[0:1, bass.ds(b, 1)], min_val=0, max_val=EXPERTS - 1)
                if not early(b, 3):
                    sp.wait_ge(t_mm.sem, t_mm.after(b - 3, 1))
                sp.dma_start(XB[:, p, :], slots_d.rearrange("(a r) n -> a r n", r=128)[bass.ds(place, 1), :, :].rearrange("a r n -> r (a n)")).then_inc(s_block[p], 16)
                if not early(b, 3):
                    sp.wait_ge(narrow_mm.sem, narrow_mm.after(b - 3, 1))
                sp.dma_start(WX[:, p, :], ex_m[bass.ds(expert, 1), :, :].rearrange("e p n -> p (e n)")).then_inc(s_weights[p], 16)
                sp.dma_start(WXR[:, p, :], ex_r[bass.ds(expert, 1), :, :].rearrange("e p n -> p (e n)")).then_inc(s_weights[p], 16)
                sp.dma_start(WXB[:, p, :], ex_b[bass.ds(expert, 1), :, :].rearrange("e p n -> p (e n)")).then_inc(s_weights[p], 16)

            over_blocks(sp, load_block)

            def load_keep(g):
                sp.dma_start(KEEP[:, :, :].rearrange("p t n -> p (t n)"), keep_d[bass.ds(g, 1), :, :].rearrange("g p n -> p (g n)")).then_inc(keep_loaded.sem, 16)

            def load_h(g):
                sp.dma_start(M.Hm[:, :], h_md[bass.ds(g, 1), :, :].rearrange("g p t -> p (g t)")).then_inc(h_loaded.sem, 16)
                sp.dma_start(M.Hr[:, :], h_rd[bass.ds(g, 1), :, :].rearrange("g p t -> p (g t)")).then_inc(h_loaded.sem, 16)

            load_keep(0)
            sp.wait_ge(h_stored.sem, h_stored.after(GROUPS, 0))
            load_h(0)

            with sp.Fori(0, GROUPS - 1) as g:
                sp.wait_ge(mixed.sem, mixed.after(g, TILES))
                load_keep(g + 1)
                sp.wait_ge(M.residual.sem, M.residual.after(g, 1))
                load_h(g + 1)

        @block.gpsimd
        def _(pool):
            pool.sem_inc(out_free.sem, 1)
            nc.gpsimd.memset(ones_d[:, :], 1.0 / D)
            nc.gpsimd.memset(ones_bn[:, :], 1.0 / BN)
            pool.sem_inc(final.sem, 1)
            pool.sem_inc(scatter_free.sem, 1)
            nc.gpsimd.memset(ones_row[:, :], 1.0)
            nc.gpsimd.memset(ones_tw[:, :], 1.0)
            nc.gpsimd.memset(eps_col[:, :], EPS).then_inc(prep_pool, 1)
            nc.gpsimd.memset(ZERO, 0.0).then_inc(prep_pool, 1)

            def sum_step(s, g, k, c, y, pair, added):
                n = k * STEPS + c
                pool.wait_ge(s.prod_ready.sem, s.prod_ready.after(g, n + 1))
                if c == 0:
                    nc.gpsimd.tensor_tensor(y, PR[:, c % 2, 0, :], PR[:, c % 2, 1, :], ALU.add).then_inc(s.summed.sem, 1)
                    pool.wait_ge(s.summed.sem, s.summed.after(g, n + 1))
                    pool.sem_inc(added.sem, 1)
                else:
                    pool.wait_ge(added.sem, added.after(g, n))
                    nc.gpsimd.tensor_tensor(pair, PR[:, c % 2, 0, :], PR[:, c % 2, 1, :], ALU.add).then_inc(s.summed.sem, 1)
                    pool.wait_ge(s.summed.sem, s.summed.after(g, n + 1))
                    nc.gpsimd.tensor_tensor(y, y, pair, ALU.add).then_inc(added.sem, 1)

            def decay_step(g, c):
                pool.wait_ge(P.da_ready.sem, P.da_ready.after(g, c + 1))
                if c >= 2:
                    pool.wait_ge(P.scanned.sem, P.scanned.after(g, c - 1))
                nc.gpsimd.tensor_tensor(aP[:, c % 2], dA[:, c % 2],
                                        P.DL[:, :].unsqueeze(1).broadcast_to([128, NC, PK]),
                                        ALU.mult).then_inc(ap_ready.sem, 1)

            def first(s, p, m):
                if s is not None:
                    pool.wait_ge(P.w_ready.sem, P.w_ready.after(s, 1))
                    decay_step(s, 0)
                for c in range(STEPS):
                    if s is not None:
                        if c + 1 < STEPS:
                            decay_step(s, c + 1)
                        sum_step(P, s, 0, c, YSUM1, PAIR1, y1_added)
                    if m is not None and c == 6:
                        pool.wait_ge(s_zero, 128)
                        pool.wait_ge(xtok_copied.sem, xtok_copied.after(m, 2))
                        pool.wait_ge(slots_ready.sem, slots_ready.after(m, 1))
                        pool.sem_inc(turn_taken, 1)
                    if m is not None and c >= 6:
                        for t in ((0, 1), (2,))[c - 6]:
                            for k in range(2):
                                pool.indirect_dma_start(slots_d[:, :], bass.IndirectOffsetOnAxis(slot_u[:, t, k:k + 1], 0),
                                                        XTOK[0:TW, t, :], None).then_inc(scattered.sem, 16)
                if m is not None:
                    pool.dma_start(keep_d[bass.ds(m, 1), :, :].rearrange("g p n -> p (g n)"),
                                   KEEP[:, :, :].rearrange("p t n -> p (t n)")).then_inc(scattered.sem, 16)
                    pool.wait_ge(scattered.sem, scattered.after(m, SCATTERS))
                    pool.sem_inc(scatter_free.sem, 1)

            first_pass(pool, first)

            def store_block(i, p):
                b = 3 * i + p
                pool.wait_ge(y_copied.sem, y_copied.after(b, 1))
                pool.dma_start(outs_d.rearrange("(b r) n -> b r n", r=128)[bass.ds(b, 1), :, :].rearrange("b r n -> r (b n)"), YB[:, p, :]).then_inc(out_rows[p], 16)

            over_blocks(pool, store_block)
            for p in range(3):
                pool.wait_ge(out_rows[p], 16 * (BLOCKS // 3))

            def gather(g, tiles):
                for t in tiles:
                    for k in range(2):
                        pool.indirect_dma_start(GA[:, t, k, :], None, outs_d[:, :],
                                                bass.IndirectOffsetOnAxis(slot_u[:, t, k:k + 1], 0)).then_inc(gathered.sem, 16)

            pool.wait_ge(rows_ready.sem, 1)
            gather(0, range(TILES))

            def part_a(g, tail):
                if g is not None:
                    for c in range(STEPS):
                        sum_step(Q, g, 0, c, YSUM, PAIR, y_added)
                        if not is_last(g):
                            if c == 2:
                                pool.wait_ge(rows_ready.sem, rows_ready.after(g + 1, 1))
                                pool.sem_inc(turn_taken, 1)
                            if c in (2, 3, 4):
                                gather(g + 1, (c - 2,))

            def part_b(g, tail, nxt):
                if g is not None:
                    for c in range(STEPS):
                        sum_step(Q, g, 1, c, YSUM, PAIR, y_added)
                if tail is not None:
                    pool.wait_ge(final.sem, final.after(tail, 1))
                    pool.dma_start(out_m[bass.ds(tail, 1), :, :].rearrange("g p t -> p (g t)"), Om[:, :]).then_inc(stored.sem, 16)
                    pool.dma_start(out_r[bass.ds(tail, 1), :, :].rearrange("g p t -> p (g t)"), Or[:, :]).then_inc(stored.sem, 16)
                    pool.wait_ge(stored.sem, stored.after(tail, 32))
                    pool.sem_inc(out_free.sem, 1)

            second_pass(pool, part_a, part_b)

        @block.scalar
        def _(act):
            act.dma_start(SELF[:, :], sel_d[:, :]).then_inc(s_sel, 16)
            act.wait_ge(s_const[0], 32)
            act.wait_ge(prep_pool, 1)
            nc.scalar.activation(dt0[:, :], cm("log_dt"), ACT.Exp).then_inc(prep_act, 1)
            act.wait_ge(prep_act, 1)
            nc.scalar.mul(neg_dt0[:, :], dt0[:, :], -1.0)
            nc.scalar.activation(posb_m[:, :], cm("posm"), ACT.Identity, bias=cm("tok_b", 0, 1))
            nc.scalar.activation(posb_r[:, :], cm("posr", p=DR), ACT.Identity, bias=cm("tok_b", 1, 2, p=DR)).then_inc(prep_act, 1)
            act.wait_ge(sel_ready, 2)
            nc.scalar.activation(negA[:, :], negA[:, :], ACT.Exp).then_inc(prep_act, 1)
            act.wait_ge(prep_act, 4)

            def squares(s, g, li):
                act.wait_ge(s.ln_centred.sem, s.ln_centred.after(g, 2 * li + 1))
                nc.scalar.activation(s.SQm, s.Cm[:, :], ACT.Square).then_inc(s.ln_squares.sem, 1)
                act.wait_ge(s.ln_centred.sem, s.ln_centred.after(g, 2 * li + 2))
                nc.scalar.activation(s.SQr[:, :], s.Cr[:, :], ACT.Square).then_inc(s.ln_squares.sem, 1)

            def power(s, rows, var, log, rstd, g, k):
                nc.scalar.activation(s.VE[0:rows, :], var, ACT.Ln, bias=eps_col[0:rows, :]).then_inc(log.sem, 1)
                act.wait_ge(log.sem, log.after(g, k))
                nc.scalar.activation(s.RS[0:rows, :], s.VE[0:rows, :], ACT.Exp, scale=-0.5).then_inc(rstd.sem, 1)

            def both_rstd(p, m):
                parts = [(s, g, bank) for s, g, bank in ((M, m, 7), (P, p, 4)) if g is not None]
                for s, g, bank in parts:
                    act.wait_ge(s.ln_var.sem, s.ln_var.after(g, 1))
                    nc.scalar.activation(s.VE[:, :], PS[:, bank, 0:T], ACT.Ln, bias=eps_col[:, :]).then_inc(s.ln_log.sem, 1)
                for s, g, bank in parts:
                    act.wait_ge(s.ln_log.sem, s.ln_log.after(g, 1))
                    nc.scalar.activation(s.RS[:, :], s.VE[:, :], ACT.Exp, scale=-0.5).then_inc(s.ln_rstd.sem, 1)

            def rstd(s, g, li, bank):
                act.wait_ge(s.ln_var.sem, s.ln_var.after(g, li + 1))
                power(s, 128, PS[:, bank, 0:T], s.ln_log, s.ln_rstd, g, li + 1)

            def copy_set(s, g, i, buf, bank, bias):
                act.wait_ge(s.set_mm.sem, s.set_mm.after(g, i + 1))
                kw = {} if bias is None else {"bias": bias}
                nc.scalar.activation(s.V[:, :], PS[:, bank, 0:T], ACT.Identity, **kw).then_inc(s.set_copied.sem, 1)
                nc.scalar.activation(s.S3[:, buf, :], PS[:, bank, 0:T], ACT.Identity, **kw).then_inc(s.set_copied.sem, 1)

            def logits(s, g, bank, bias):
                act.wait_ge(s.logits_mm.sem, s.logits_mm.after(g, 1))
                kw = {} if bias is None else {"bias": bias}
                nc.scalar.activation(s.LW[:, :], PS[0:EXPERTS, bank, 0:T], ACT.Identity, **kw).then_inc(s.logits_ready.sem, 1)

            def ratio(s, g):
                act.wait_ge(s.gap_ready.sem, s.gap_ready.after(g, 1))
                nc.scalar.activation(s.gs[0:TW, 3, :], s.gs[0:TW, 2, :], ACT.Exp).then_inc(s.ratio_ready.sem, 1)

            def hidden(g, first, last):
                for j in range(first, last):
                    act.wait_ge(hid_mm.sem, hid_mm.after(g, j + 1))
                    dst, rows = (HID[:, j, :], 128) if j < 10 else (HIDr[:, :], DR)
                    nc.scalar.activation(dst, PS[0:rows, HIDDEN_BANKS[j], 0:T], ACT.Silu,
                                         bias=cm("m1_b", j, j + 1, p=rows)).then_inc(hid_ready.sem, 1)

            def in_copies(g, k):
                act.wait_ge(in_mm.sem, in_mm.after(g, k + 1))
                nc.scalar.activation(XS, PS[:, X_BANK, 0:PK], ACT.Copy).then_inc(in_copied.sem, 1)
                nc.scalar.activation(DIRS[k].ZS, PS[:, Z_BANK[k], 0:PK], ACT.Silu)

            def inputs(g, k):
                s = DIRS[k]
                act.wait_ge(conv_ready.sem, conv_ready.after(g, k + 1))
                nc.scalar.activation(s.UP[:, :], s.CV, ACT.Silu)
                nc.scalar.activation(s.URr[:, 0:HALF], s.CV[0:DR, T:PK], ACT.Silu)
                nc.scalar.activation(s.URr[:, HALF:T], s.CV[DR:128, T:PK], ACT.Silu).then_inc(u_ready.sem, 1)

            def projected(g, k):
                act.wait_ge(dt24_mm.sem, dt24_mm.after(g, k + 1))
                nc.scalar.activation(DT24, PS[0:RANK, Z_BANK[k], 0:T], ACT.Copy).then_inc(dt24_ready.sem, 1)
                copy_set(DIRS[k], g, k, 0, X_BANK, None)

            def raw_steps(g, k):
                d = "fb"[k]
                act.wait_ge(dt_mm.sem, dt_mm.after(g, k + 1))
                for h, cols in enumerate(MAIN_REST):
                    last = nc.scalar.activation(DIRS[k].DL[:, cols], PS[:, Z_BANK[k], cols], ACT.Identity, bias=cm(d + "dtb", h, h + 1))
                last.then_inc(dt_raw.sem, 1)

            def softplus(g, k):
                s = DIRS[k]
                act.wait_ge(abs_dt.sem, abs_dt.after(g, k + 1))
                nc.scalar.activation(s.OM[:, :], s.TM[:, :], ACT.Exp, scale=-1.0).then_inc(exp_dt.sem, 1)
                act.wait_ge(exp_dt.sem, exp_dt.after(g, k + 1))
                nc.scalar.activation(LZ, s.OM[:, :], ACT.Ln, bias=1.0).then_inc(log_dt_ready.sem, 1)

            def q_decay(g, k, c):
                n = k * STEPS + c
                if c == 0:
                    act.wait_ge(Q.w_ready.sem, Q.w_ready.after(g, k + 1))
                if n >= 2 or not is_first(g):
                    act.wait_ge(Q.scanned.sem, Q.scanned.after(g, n - 1))
                for i in range(NC):
                    for h, cols in enumerate(MAIN_REST):
                        col = (2 * k + h) * NS + c * NC + i
                        last = nc.scalar.activation(dA[:, c % 2, i, cols], DIRS[k].DL[:, cols], ACT.Exp,
                                                    scale=negA[:, col:col + 1])
                last.then_inc(Q.da_ready.sem, 1)

            def p_decay(g, c):
                act.wait_ge(a_bc.sem, a_bc.after(g, c + 1))
                if c >= 2:
                    act.wait_ge(b_times_a.sem, b_times_a.after(g, c - 1))
                    act.wait_ge(ap_ready.sem, ap_ready.after(g, c - 1))
                for h, cols in enumerate(MAIN_REST):
                    last = nc.scalar.activation(dA[:, c % 2, :, cols], PS[:, A_BANK:A_BANK + NC, cols], ACT.Exp,
                                                scale=neg_dt0[:, h:h + 1])
                last.then_inc(P.da_ready.sem, 1)

            def output(g, k):
                act.wait_ge(out_mm.sem, out_mm.after(g, k + 1))
                nc.scalar.activation(DIRS[k].YT, PS[0:BN, AFTER_BANK[k], 0:T], ACT.Copy).then_inc(out_copied.sem, 1)

            def output_rstd(g, k):
                act.wait_ge(bn_centred.sem, bn_centred.after(g, k + 1))
                nc.scalar.activation(Q.SQm[0:BN, :], Q.Cm[0:BN, :], ACT.Square).then_inc(bn_squares.sem, 1)
                act.wait_ge(bn_var.sem, bn_var.after(g, k + 1))
                power(Q, BN, PS[0:BN, AFTER_BANK[k], 0:T], bn_log, bn_rstd, g, k + 1)

            def first(s, p, m):
                if s is not None:
                    p_decay(s, 0)
                for c in range(STEPS):
                    if c == 2:
                        both_rstd(p, m)
                    if s is not None and c + 1 < STEPS:
                        p_decay(s, c + 1)
                    if c == 1:
                        if m is not None:
                            squares(M, m, 0)
                        if p is not None:
                            squares(P, p, 0)
                    if c == 3:
                        if m is not None:
                            logits(M, m, 7, None)
                        if p is not None:
                            hidden(p, 0, 1)
                        if p is not None:
                            hidden(p, 1, 2)
                    if c == 4:
                        if p is not None:
                            hidden(p, 2, 4)
                        if m is not None:
                            ratio(M, m)
                            act.wait_ge(xtok_mm.sem, xtok_mm.after(m, 1))
                            act.wait_ge(scatter_free.sem, scatter_free.after(m, 1))
                            nc.scalar.activation(XTOK[0:TW, 0:2, :], PS[0:TW, 4, 0:2 * D].rearrange("p (t n) -> p t n", n=D), ACT.Copy).then_inc(xtok_copied.sem, 1)
                    if c == 5:
                        if m is not None:
                            act.wait_ge(xtok_mm.sem, xtok_mm.after(m, 2))
                            nc.scalar.activation(XTOK[0:TW, 2, :], PS[0:TW, 4, 0:D], ACT.Copy).then_inc(xtok_copied.sem, 1)
                        if p is not None:
                            hidden(p, 4, 5)
                            hidden(p, 5, 6)
                    if c == 6 and p is not None:
                        hidden(p, 6, 9)
                    if c == 7 and p is not None:
                        act.wait_ge(P.set_mm.sem, P.set_mm.after(p, 1))
                        nc.scalar.activation(P.V[:, :], PS[:, 7, 0:T], ACT.Identity, bias=cm("m2_b", 0, 1)).then_inc(P.set_copied.sem, 1)
                        hidden(p, 9, 11)
                if p is not None:
                    if s is not None:
                        act.wait_ge(P.c_bc.sem, P.c_bc.after(s, STEPS))
                    act.wait_ge(abs_ready.sem, abs_ready.after(p, 1))
                    nc.scalar.activation(P.S3[:, 0, :], P.V[:, :], ACT.Copy).then_inc(P.set_copied.sem, 1)
                    act.wait_ge(P.set_ready.sem, P.set_ready.after(p, 1))
                    copy_set(P, p, 1, 1, 4, cm("m2_b", 1, 2))
                    nc.scalar.activation(P.UP[:, 0:T], P.Xm[:, :], ACT.Copy)
                    nc.scalar.activation(P.UP[0:DR, T:PK], P.Xr[:, 0:HALF], ACT.Copy)
                    nc.scalar.activation(P.UP[DR:128, T:PK], P.Xr[:, HALF:T], ACT.Copy).then_inc(packed_x.sem, 1)
                    act.wait_ge(delta_mm.sem, delta_mm.after(p, 1))
                    if s is not None:
                        act.wait_ge(ap_ready.sem, ap_ready.after(s, STEPS))
                    nc.scalar.activation(P.DL[:, 0:T], PS[:, 7, 0:T], ACT.Sigmoid, bias=cm("d_b2", 0, 1))
                    nc.scalar.activation(P.DL[:, T:PK], PS[:, 7, T:PK], ACT.Sigmoid, bias=cm("d_b2", 1, 2)).then_inc(delta_ready.sem, 1)

            first_pass(act, first)

            def gelus(i, p):
                b = 3 * i + p
                if not early(b, 3):
                    act.wait_ge(narrow_mm.sem, narrow_mm.after(b - 3, 1))
                for h in range(2):
                    act.wait_ge(wide_mm.sem, wide_mm.after(b, h + 1))
                    for j in range(HALF_FT):
                        f = h * HALF_FT + j
                        last = nc.scalar.activation(HX[:, p, f, :], PS[:, WIDE_BANK + 2 * p + h, j * 128:(j + 1) * 128], ACT.Gelu,
                                                    bias=WX[:, p, FFN + FT * D + f:FFN + FT * D + f + 1])
                    last.then_inc(gelu_ready.sem, 1)

            over_blocks(act, gelus)

            def part_a(g, tail):
                if g is not None:
                    q_decay(g, 0, 0)
                for c in range(STEPS):
                    if g is not None and c + 1 < STEPS:
                        q_decay(g, 0, c + 1)
                    if g is not None and c == 0:
                        if tail is not None:
                            act.wait_ge(y_gated.sem, y_gated.after(tail, 2))
                        in_copies(g, 1)
                    if tail is not None:
                        if c == 0:
                            output(tail, 1)
                        if c == 1:
                            output_rstd(tail, 1)
                        if c == 4:
                            squares(Q, tail, 0)
                            rstd(Q, tail, 0, 5)
                        if c == 6:
                            logits(Q, tail, 5, cm("er_b", p=EXPERTS))
                        if c == 7:
                            ratio(Q, tail)
                            act.wait_ge(shift_ready.sem, shift_ready.after(tail, 1))
                            nc.scalar.activation(Q.gate[0:TW, 7], Q.gate[0:TW, 6], ACT.Exp).then_inc(shift_exp.sem, 1)
                    if g is not None:
                        if c == 1:
                            inputs(g, 1)
                        if c == 2:
                            projected(g, 1)
                        if c == 3:
                            raw_steps(g, 1)
                        if c == 5:
                            softplus(g, 1)

            def part_b(g, tail, nxt):
                if g is not None:
                    q_decay(g, 1, 0)
                for c in range(STEPS):
                    if g is not None:
                        if c + 1 < STEPS:
                            q_decay(g, 1, c + 1)
                        if c == 0:
                            output(g, 0)
                            act.wait_ge(M.residual.sem, M.residual.after(g, 1))
                            if tail is not None:
                                act.wait_ge(Q.residual.sem, Q.residual.after(tail, 1))
                            nc.scalar.activation(HBm, L.Hm[:, :], ACT.Copy)
                            nc.scalar.activation(HBr, L.Hr[:, :], ACT.Copy).then_inc(hb_copied.sem, 1)
                        if c == 1:
                            output_rstd(g, 0)
                    if nxt is not None:
                        if c == 2:
                            squares(L, nxt, 0)
                            rstd(L, nxt, 0, 5)
                        if c == 3:
                            act.wait_ge(bott_mm.sem, bott_mm.after(nxt, 1))
                            nc.scalar.activation(HB[:, :], PS[0:BN, 5, 0:T], ACT.Identity, bias=cm("down_b", p=BN)).then_inc(bott_ready.sem, 1)
                            in_copies(nxt, 0)
                        if c == 4:
                            inputs(nxt, 0)
                            projected(nxt, 0)
                        if c == 5:
                            raw_steps(nxt, 0)
                        if c == 6:
                            softplus(nxt, 0)

            act.wait_ge(s_const[2], 32)
            second_pass(act, part_a, part_b)

        @block.vector
        def _(dve):
            dve.wait_ge(s_sel, 16)
            nc.vector.tensor_copy(SEL[:, :], SELF[:, :]).then_inc(sel_ready, 1)
            dve.wait_ge(s_const[0], 32)
            nc.vector.tensor_scalar(negA[:, 0:2 * NS], cm("fAlog"), float(np.log(A_MAX)), None, ALU.min)
            nc.vector.tensor_scalar(negA[:, 2 * NS:4 * NS], cm("bAlog"), float(np.log(A_MAX)), None, ALU.min).then_inc(sel_ready, 1)
            dve.wait_ge(prep_act, 3)
            nc.vector.tensor_scalar(negA[:, :], negA[:, :], -1.0, -A_MIN, ALU.mult, ALU.min).then_inc(prep_act, 1)

            links = {}

            def link(s, g, ins):
                links[s] += 1
                ins.then_inc(s.chain.sem, 1)
                dve.wait_ge(s.chain.sem, s.chain.after(g, links[s]))

            def centre(s, src, g, li, bank):
                dve.wait_ge(s.ln_mean.sem, s.ln_mean.after(g, li + 1))
                nc.vector.tensor_tensor(s.Cm[:, :], src.Hm[:, :], PS[:, bank, 0:T], ALU.subtract).then_inc(s.ln_centred.sem, 1)
                nc.vector.tensor_tensor(s.Cr[:, :], src.Hr[:, :], PS[0:DR, bank, 0:T], ALU.subtract).then_inc(s.ln_centred.sem, 1)

            def scale(s, g, li):
                dve.wait_ge(s.ln_rstd.sem, s.ln_rstd.after(g, li + 1))
                nc.vector.tensor_tensor(s.Xm[:, :], s.Cm[:, :], s.RS[:, :], ALU.mult)
                nc.vector.tensor_tensor(s.Xr[:, :], s.Cr[:, :], s.RS[0:DR, :], ALU.mult).then_inc(s.ln_x.sem, 1)

            def split_set(s, g, i, buf, is_abs=False):
                dve.wait_ge(s.set_copied.sem, s.set_copied.after(g, 2 * i + 1))
                if is_abs:
                    nc.vector.scalar_tensor_tensor(s.V[:, :], s.V[:, :], cm("sign"), s.V[:, :], ALU.mult, ALU.max).then_inc(abs_ready.sem, 1)
                dve.wait_ge(s.set_copied.sem, s.set_copied.after(g, 2 * i + 2))
                link(s.work, g, nc.vector.tensor_tensor(s.R[64:128, :], s.V[64:128, :], s.S3[64:128, buf, :], ALU.subtract))
                link(s.work, g, nc.vector.tensor_copy(s.S3[64:128, buf, :], s.R[64:128, :]))
                nc.vector.tensor_tensor(s.S3[96:128, buf, :], s.R[96:128, :], s.S3[96:128, buf, :], ALU.subtract).then_inc(s.set_ready.sem, 1)

            def gate_views(s):
                L, q, oh1, oh2, L2, w = [s.gate[0:TW, j] for j in range(6)]
                if s is M:
                    oh1, oh2 = KEEP[:, :, 0:EXPERTS], KEEP[:, :, EXPERTS:2 * EXPERTS]
                return [L, q, oh1, oh2, L2, w], [s.gs[0:TW, j] for j in range(8)]

            def over(ap):
                return ap.unsqueeze(2).broadcast_to([TW, TILES, EXPERTS])

            def gates_top(s, g, bank):
                (L, q, oh1, oh2, L2, w), (m1, m2, gap, ratio, den, inv, w2, rk) = gate_views(s)
                rank = cm("rank", p=TW).unsqueeze(1).broadcast_to([TW, TILES, EXPERTS])
                dve.wait_ge(s.logits_T.sem, s.logits_T.after(g, 1))
                link(s, g, nc.vector.tensor_copy(L, PS[0:TW, bank, 0:TILES * EXPERTS].rearrange("p (t e) -> p t e", e=EXPERTS)))

                def pick(src, m, oh):
                    link(s, g, nc.vector.tensor_reduce(m, src, AX.X, ALU.max))
                    link(s, g, nc.vector.tensor_tensor(q, src, over(m), ALU.is_equal))
                    link(s, g, nc.vector.tensor_tensor(q, q, rank, ALU.mult))
                    link(s, g, nc.vector.tensor_reduce(rk, q, AX.X, ALU.max))
                    link(s, g, nc.vector.tensor_tensor(oh, q, over(rk), ALU.is_equal))

                pick(L, m1, oh1)
                link(s, g, nc.vector.scalar_tensor_tensor(L2, oh1, -3.0e38, L, ALU.mult, ALU.add))
                pick(L2, m2, oh2)
                nc.vector.tensor_tensor(gap, m2, m1, ALU.subtract).then_inc(s.gap_ready.sem, 1)
                if s is M:
                    nc.vector.tensor_tensor(w, oh1, oh2, ALU.add).then_inc(pair_ready.sem, 1)
                if s is Q:
                    nc.vector.tensor_tensor(s.gate[0:TW, 6], L, over(m1), ALU.subtract).then_inc(shift_ready.sem, 1)

            def gates_weights(s, g):
                (L, q, oh1, oh2, L2, w), (m1, m2, gap, ratio, den, inv, w2, rk) = gate_views(s)
                dve.wait_ge(s.ratio_ready.sem, s.ratio_ready.after(g, 1))
                link(s, g, nc.vector.tensor_scalar(den, ratio, 1.0, None, ALU.add))
                dve.wait_ge(shift_exp.sem, shift_exp.after(g, 1))
                link(s, g, nc.vector.tensor_reduce(rk, s.gate[0:TW, 7], AX.X, ALU.add))
                link(s, g, nc.vector.scalar_tensor_tensor(den, rk, 1e-9, den, ALU.mult, ALU.add))
                link(s, g, nc.vector.reciprocal(inv, den))
                link(s, g, nc.vector.tensor_tensor(w2, ratio, inv, ALU.mult))
                link(s, g, nc.vector.tensor_tensor(oh1, oh1, over(inv), ALU.mult))
                link(s, g, nc.vector.tensor_tensor(oh2, oh2, over(w2), ALU.mult))
                nc.vector.tensor_tensor(w, oh1, oh2, ALU.add).then_inc(s.gates_ready.sem, 1)

            def route(g):
                (L, q, oh1, oh2, pos, pair), (m1, m2, gap, ratio, den, inv, w2, rk) = gate_views(M)
                kw1, kw2 = (KEEP[:, :, 2 * EXPERTS + j] for j in range(2))
                dve.wait_ge(M.ratio_ready.sem, M.ratio_ready.after(g, 1))
                link(M, g, nc.vector.tensor_scalar(den, ratio, 1.0, None, ALU.add))
                link(M, g, nc.vector.reciprocal(kw1, den))
                nc.vector.tensor_tensor(kw2, ratio, kw1, ALU.mult)

            def give_slots(g):
                (L, q, oh1, oh2, pos, pair), _ = gate_views(M)
                slot1, slot2 = (KEEP[:, :, 2 * EXPERTS + j] for j in (2, 3))
                dve.wait_ge(ranks_mm.sem, ranks_mm.after(g, 1))
                link(M, g, nc.vector.tensor_tensor(pos, PS[0:TW, 7, 0:TILES * EXPERTS].rearrange("p (t e) -> p t e", e=EXPERTS),
                                                   run[:, :].unsqueeze(1).broadcast_to([TW, TILES, EXPERTS]), ALU.add))
                nc.vector.tensor_tensor(run[:, :], run[:, :], PS[0:TW, 7, TILES * EXPERTS:(TILES + 1) * EXPERTS], ALU.add)
                nc.vector.tensor_tensor(q, oh1, pos, ALU.mult)
                link(M, g, nc.vector.tensor_tensor(L, oh2, pos, ALU.mult))
                nc.vector.tensor_reduce(slot1, q, AX.X, ALU.add)
                link(M, g, nc.vector.tensor_reduce(slot2, L, AX.X, ALU.add))
                nc.vector.tensor_copy(slot_u[:, :, :], KEEP[:, :, 2 * EXPERTS + 2:2 * EXPERTS + 4]).then_inc(slots_ready.sem, 1)

            def gates_rows(s, g, bank):
                dve.wait_ge(s.gates_T.sem, s.gates_T.after(g, 1))
                nc.vector.tensor_copy(s.LW[:, :], PS[0:EXPERTS, bank, 0:T]).then_inc(s.gates_T_ready.sem, 1)

            def start_sum(s, g, bank01, bank2):
                dve.wait_ge(s.bias_mm.sem, s.bias_mm.after(g, 1))
                nc.vector.tensor_copy(s.ACC[0:TW, 0:2, :], PS[0:TW, bank01, 0:2 * D].rearrange("p (t n) -> p t n", n=D))
                nc.vector.tensor_copy(s.ACC[0:TW, 2, :], PS[0:TW, bank2, 0:D]).then_inc(s.acc_started.sem, 1)
                dve.wait_ge(s.acc_started.sem, s.acc_started.after(g, 1))

            def flat(ap, back):
                ap = ap.rearrange("p n t -> p (n t)")
                return ap[:, ::-1] if back else ap

            def scan_step(s, g, k, c):
                n, back = k * STEPS + c, s is BW
                dve.wait_ge(s.b_bc.sem, s.b_bc.after(g, n + 1))
                nc.vector.tensor_tensor(BB[:, c % 2], s.WV[:, :].unsqueeze(1).broadcast_to([128, NC, PK]),
                                        PS[:, B_BANK:B_BANK + NC, 0:PK], ALU.mult).then_inc(s.b_read.sem, 1)
                dve.wait_ge(s.b_read.sem, s.b_read.after(g, n + 1))
                dve.wait_ge(s.da_ready.sem, s.da_ready.after(g, n + 1))
                if s is P:
                    nc.vector.tensor_tensor(BB[:, c % 2], BB[:, c % 2], dA[:, c % 2], ALU.mult).then_inc(b_times_a.sem, 1)
                    dve.wait_ge(b_times_a.sem, b_times_a.after(g, c + 1))
                    dve.wait_ge(ap_ready.sem, ap_ready.after(g, c + 1))
                decay = aP if s is P else dA
                nc.vector.tensor_tensor_scan(flat(ST[:, :, :], back), flat(decay[:, c % 2], back),
                                             flat(BB[:, c % 2], back), 0.0, ALU.mult, ALU.add).then_inc(s.scanned.sem, 1)

            def output_step(s, g, k, c):
                n = k * STEPS + c
                dve.wait_ge(s.scanned.sem, s.scanned.after(g, n + 1))
                dve.wait_ge(s.c_bc.sem, s.c_bc.after(g, n + 1))
                if c >= 2 or not at_start(s, g, 0):
                    dve.wait_ge(s.summed.sem, s.summed.after(g, n - 1))
                nc.vector.tensor_tensor(PR[:, c % 2], ST[:, :, :], PS[:, C_BANK:C_BANK + NC, 0:PK], ALU.mult).then_inc(s.prod_ready.sem, 1)

            def tokens(g):
                for k in range(2):
                    Hs, rows, pos, cls, bank = ((P.Hm, 128, posb_m, "cls_m", 7), (P.Hr, DR, posb_r, "cls_r", 4))[k]
                    hv = seqs(Hs[:, :])
                    nc.vector.tensor_copy(hv[:, :, 0:2], cm(cls, p=rows).unsqueeze(1).broadcast_to([rows, IMG, 2]))
                    dve.wait_ge(tok_mm.sem, tok_mm.after(g, k + 1))
                    last = nc.vector.tensor_tensor(hv[:, :, 2:SEQ],
                                                   PS[0:rows, bank, 0:IMG * NP].rearrange("p (b t) -> p b t", t=NP),
                                                   pos[:, :].unsqueeze(1).broadcast_to([rows, IMG, NP]), ALU.add)
                last.then_inc(P.residual.sem, 1)
                dve.wait_ge(P.residual.sem, P.residual.after(g, 1))

            def first_scan_input(g):
                dve.wait_ge(delta_ready.sem, delta_ready.after(g, 1))
                dve.wait_ge(packed_x.sem, packed_x.after(g, 1))
                link(P, g, nc.vector.tensor_scalar(P.OM[:, :], P.DL[:, :], -1.0, 1.0, ALU.mult, ALU.add))
                for h, cols in enumerate(MAIN_REST):
                    nc.vector.scalar_tensor_tensor(P.WV[:, cols], P.OM[:, cols], dt0[:, h:h + 1], P.UP[:, cols], ALU.mult, ALU.mult)
                link(P, g, nc.vector.memset(seqs(P.DL[:, :])[:, :, 0:1], 0.0))
                for rows, cols, toks, feats in PARTS:
                    x, h, D0 = (P.Xm, P.Hm, cm("D0", 0, 1)) if feats.start == 0 else (P.Xr, P.Hr, cm("D0", 1, 2, p=DR))
                    last = nc.vector.scalar_tensor_tensor(BASE[rows, cols], x[:, toks], D0, h[:, toks], ALU.mult, ALU.add)
                last.then_inc(P.w_ready.sem, 1)
                dve.wait_ge(P.w_ready.sem, P.w_ready.after(g, 1))

            def first_scan_output(g, before):
                if before is not None:
                    dve.wait_ge(h_stored.sem, h_stored.after(before, 32))
                    dve.wait_ge(M.ln_centred.sem, M.ln_centred.after(before, 2))
                dve.wait_ge(y1_added.sem, y1_added.after(g, STEPS))
                for rows, cols, toks, feats in PARTS:
                    h = M.Hm if feats.start == 0 else M.Hr
                    last = nc.vector.tensor_tensor(h[:, toks], BASE[rows, cols], YSUM1[rows, cols], ALU.add)
                last.then_inc(scan_out.sem, 1)
                dve.wait_ge(scan_out.sem, scan_out.after(g, 1))

            def convolve(g, k):
                d, CV = "fb"[k], DIRS[k].CV
                links[PREP] = 10 * k
                dve.wait_ge(in_copied.sem, in_copied.after(g, k + 1))
                for h, cols in enumerate(MAIN_REST):
                    last = nc.vector.tensor_scalar(CV[:, cols], XS[:, cols], cm(d + "cw", 4 * h + 3, 4 * h + 4),
                                                   cm(d + "cb", h, h + 1), ALU.mult, ALU.add)
                link(PREP, g, last)
                for s in range(1, 4):
                    for h, cols in enumerate(MAIN_REST):
                        src, dst = seqs(XS[:, cols]), seqs(CV[:, cols])
                        if d == "b":
                            src, dst = src[:, :, s:SEQ], dst[:, :, 0:SEQ - s]
                        else:
                            src, dst = src[:, :, 0:SEQ - s], dst[:, :, s:SEQ]
                        last = nc.vector.scalar_tensor_tensor(dst, src, cm(d + "cw", 4 * h + 3 - s, 4 * h + 4 - s), dst,
                                                              ALU.mult, ALU.add)
                    if s < 3:
                        link(PREP, g, last)
                    else:
                        last.then_inc(conv_ready.sem, 1)

            def size_of_steps(g, k):
                s = DIRS[k]
                dve.wait_ge(dt_raw.sem, dt_raw.after(g, k + 1))
                nc.vector.scalar_tensor_tensor(s.TM[:, :], s.DL[:, :], -1.0, s.DL[:, :], ALU.mult, ALU.max).then_inc(abs_dt.sem, 1)

            def steps(g, k):
                s = DIRS[k]
                dve.wait_ge(exp_dt.sem, exp_dt.after(g, k + 1))
                link(PREP, g, nc.vector.tensor_scalar(s.TM[:, :], s.OM[:, :], 1.0, -1.0, ALU.add, ALU.add))
                dve.wait_ge(log_dt_ready.sem, log_dt_ready.after(g, k + 1))
                link(PREP, g, nc.vector.tensor_tensor(s.OM[:, :], s.OM[:, :], s.TM[:, :], ALU.subtract))
                link(PREP, g, nc.vector.tensor_tensor(s.OM[:, :], s.OM[:, :], LZ, ALU.add))
                link(PREP, g, nc.vector.scalar_tensor_tensor(s.DL[:, :], s.DL[:, :], 0.0, s.OM[:, :], ALU.max, ALU.add))
                link(PREP, g, nc.vector.tensor_tensor(s.WV[:, :], s.DL[:, :], s.UP[:, :], ALU.mult))
                assert links[PREP] == 10 * k + 10
                first = slice(SEQ - 1, SEQ) if k == 1 else slice(0, 1)
                nc.vector.memset(seqs(s.DL[:, :])[:, :, first], RESTART).then_inc(Q.w_ready.sem, 1)

            def gated_output(g, k):
                d, s = "fb"[k], DIRS[k]
                links[GATED] = k
                dve.wait_ge(y_added.sem, y_added.after(g, (k + 1) * STEPS))
                for h, cols in enumerate(MAIN_REST):
                    last = nc.vector.scalar_tensor_tensor(s.TM[:, cols], s.UP[:, cols], cm(d + "Dp", h, h + 1), YSUM[:, cols], ALU.mult, ALU.add)
                link(GATED, g, last)
                nc.vector.tensor_tensor(s.CV[:, 0:T], s.TM[:, 0:T], s.ZS[:, 0:T], ALU.mult)
                nc.vector.tensor_tensor(s.GRr[:, 0:HALF], s.TM[0:DR, T:PK], s.ZS[0:DR, T:PK], ALU.mult)
                nc.vector.tensor_tensor(s.GRr[:, HALF:T], s.TM[DR:128, T:PK], s.ZS[DR:128, T:PK], ALU.mult).then_inc(y_gated.sem, 1)

            def output_centre(g, k):
                dve.wait_ge(out_copied.sem, out_copied.after(g, k + 1))
                dve.wait_ge(bn_mean.sem, bn_mean.after(g, k + 1))
                nc.vector.tensor_tensor(Q.Cm[0:BN, :], DIRS[k].YT, PS[0:BN, AFTER_BANK[k], 0:T], ALU.subtract).then_inc(bn_centred.sem, 1)

            def output_norm(g, k):
                d = "fb"[k]
                links[NORM] = k
                dve.wait_ge(bn_rstd.sem, bn_rstd.after(g, k + 1))
                link(NORM, g, nc.vector.tensor_tensor(Q.Cm[0:BN, :], Q.Cm[0:BN, :], Q.RS[0:BN, :], ALU.mult))
                nc.vector.tensor_scalar(YS[:, k, :], Q.Cm[0:BN, :], cm(d + "lng", 0, 1, p=BN), cm(d + "lng", 1, 2, p=BN),
                                        ALU.mult, ALU.add).then_inc(bn_done.sem, 1)

            def first(s, p, m):
                links[M] = 0
                if s is not None:
                    links[P] = 4
                    first_scan_input(s)
                    assert links[P] == P.chain.per_group, links[P]
                for c in range(STEPS):
                    if s is not None:
                        scan_step(P, s, 0, c)
                    if p is not None and c == 1:
                        tokens(p)
                    if m is not None:
                        if c == 6:
                            give_slots(m)
                            assert links[M] == M.chain.per_group, ("M", links[M])
                    if s is not None:
                        output_step(P, s, 0, c)
                    if m is not None:
                        if c == 1:
                            centre(M, M, m, 0, 7)
                        if c == 2:
                            scale(M, m, 0)
                        if c == 4:
                            dve.wait_ge(scatter_free.sem, scatter_free.after(m, 1))
                            gates_top(M, m, 7)
                        if c == 5:
                            route(m)
                    if p is not None:
                        if c == 1:
                            centre(P, P, p, 0, 4)
                        if c == 2:
                            scale(P, p, 0)
                links[P] = 0
                if p is not None:
                    split_set(P, p, 0, 0, is_abs=True)
                if s is not None:
                    first_scan_output(s, m)
                if p is not None:
                    split_set(P, p, 1, 1)

            dve.wait_ge(prep_act, 3)
            dve.wait_ge(s_const[1], 32)
            nc.vector.tensor_copy(run[:, :], cm("eoff", p=TW)).then_inc(table, 1)
            dve.wait_ge(table, 1)
            first_pass(dve, first)

            done = [1]

            def then(ins):
                done[0] += 1
                ins.then_inc(table, 1)
                dve.wait_ge(table, done[0])

            used, blocks, start, delta, end, last_b = (counts[:, j, :] for j in range(6))
            which, expert, before, place, place2 = (block_f[:, j, :] for j in range(5))
            dve.wait_ge(slots_ready.sem, slots_ready.after(GROUPS, 0))
            then(nc.vector.tensor_tensor(used, run[:, :], cm("eoff", p=TW), ALU.subtract))
            then(nc.vector.tensor_tensor(steps80[:, :, :], used.unsqueeze(2).broadcast_to([TW, EXPERTS, CAP_BLOCKS]),
                                         cm("blk", p=TW).unsqueeze(1).broadcast_to([TW, EXPERTS, CAP_BLOCKS]), ALU.is_gt))
            then(nc.vector.tensor_reduce(blocks, steps80[:, :, :], AX.X, ALU.add))
            then(nc.vector.tensor_tensor(steps80[:, :, 0:EXPERTS], blocks.unsqueeze(1).broadcast_to([TW, EXPERTS, EXPERTS]),
                                         cm("below", p=TW).rearrange("p (a b) -> p a b", b=EXPERTS), ALU.mult))
            then(nc.vector.tensor_reduce(start, steps80[:, :, 0:EXPERTS], AX.X, ALU.add))
            nc.vector.scalar_tensor_tensor(delta, start, 128.0, cm("eoff", p=TW), ALU.mult, ALU.subtract)
            then(nc.vector.tensor_tensor(end, start, blocks, ALU.add))
            then(nc.vector.tensor_scalar(last_b[:, 0:1], end[:, EXPERTS - 1:EXPERTS], -1.0, None, ALU.add))
            then(nc.vector.tensor_scalar(which, cm("bid", p=TW), last_b[:, 0:1], None, ALU.min))
            then(nc.vector.tensor_tensor(passed[:, 0], which.unsqueeze(2).broadcast_to([TW, BLOCKS, EXPERTS]),
                                         end.unsqueeze(1).broadcast_to([TW, BLOCKS, EXPERTS]), ALU.is_ge))
            nc.vector.tensor_reduce(expert, passed[:, 0], AX.X, ALU.add)
            then(nc.vector.tensor_tensor(passed[:, 1], passed[:, 0], blocks.unsqueeze(1).broadcast_to([TW, BLOCKS, EXPERTS]), ALU.mult))
            then(nc.vector.tensor_reduce(before, passed[:, 1], AX.X, ALU.add))
            then(nc.vector.scalar_tensor_tensor(place, expert, float(CAP_BLOCKS), which, ALU.mult, ALU.add))
            then(nc.vector.tensor_tensor(place2, place, before, ALU.subtract))
            nc.vector.tensor_copy(tab_expert[:, :], expert[0:1, :])
            nc.vector.tensor_copy(tab_rows[:, :], place2[0:1, :]).then_inc(table_ready, 1)

            def copy_x(i, p):
                b = 3 * i + p
                dve.wait_ge(t_mm.sem, t_mm.after(b, 1))
                if not early(b, 3):
                    dve.wait_ge(wide_mm.sem, wide_mm.after(b - 3, 2))
                nc.vector.tensor_copy(XTm[:, p, :], PS[:, TURN_BANK, 0:128])
                nc.vector.tensor_copy(XTr[:, p, :], PS[0:DR, TURN_BANK, 128:256]).then_inc(xt_copied.sem, 1)

            def copy_y(i, p):
                b = 3 * i + p
                dve.wait_ge(narrow_mm.sem, narrow_mm.after(b, 1))
                if not early(b, 3):
                    dve.wait_ge(out_rows[p], 16 * i)
                nc.vector.tensor_copy(YB[:, p, :], PS[:, OUT_BANK, 0:D]).then_inc(y_copied.sem, 1)

            def copies(i, p):
                b = 3 * i + p
                if not is_end(b):
                    copy_x(*follower(i, p))
                if not early(b, 1):
                    copy_y(*previous(i, p))

            copy_x(0, 0)
            over_blocks(dve, copies)
            copy_y(BLOCKS // 3 - 1, 2)

            rows_links = [0]

            def rows_link(g, ins):
                rows_links[0] += 1
                ins.then_inc(rows_chain.sem, 1)
                dve.wait_ge(rows_chain.sem, rows_chain.after(g, rows_links[0]))

            def find_rows(g):
                rows_links[0] = 0
                (L, q, oh1, oh2, L2, w), _ = gate_views(M)
                dve.wait_ge(keep_loaded.sem, keep_loaded.after(g, 16))
                db = delta.unsqueeze(1).broadcast_to([TW, TILES, EXPERTS])
                nc.vector.tensor_tensor(q, oh1, db, ALU.mult)
                rows_link(g, nc.vector.tensor_tensor(L, oh2, db, ALU.mult))
                nc.vector.tensor_reduce(L2[:, :, 0], q, AX.X, ALU.add)
                rows_link(g, nc.vector.tensor_reduce(L2[:, :, 1], L, AX.X, ALU.add))
                rows_link(g, nc.vector.tensor_tensor(w[:, :, 0:2], L2[:, :, 0:2], KEEP[:, :, 2 * EXPERTS + 2:2 * EXPERTS + 4], ALU.add))
                nc.vector.tensor_copy(slot_u[:, :, :], w[:, :, 0:2]).then_inc(rows_ready.sem, 1)

            find_rows(0)

            def combine(g):
                dve.wait_ge(gathered.sem, gathered.after(g, 16 * 2 * TILES))
                for t in range(TILES):
                    last = nc.vector.tensor_scalar(M.ACC[0:TW, t, :], GA[:, t, 0, :], KEEP[:, t, 2 * EXPERTS:2 * EXPERTS + 1], None, ALU.mult)
                last.then_inc(M.acc_started.sem, 1)
                dve.wait_ge(M.acc_started.sem, M.acc_started.after(g, 1))
                for t in range(TILES):
                    nc.vector.scalar_tensor_tensor(M.ACC[0:TW, t, :], GA[:, t, 1, :], KEEP[:, t, 2 * EXPERTS + 1:2 * EXPERTS + 2],
                                                   M.ACC[0:TW, t, :], ALU.mult, ALU.add).then_inc(mixed.sem, 1)

            def second_mixture(g, u):
                t, j = u // 4, u % 4
                dve.wait_ge(lin_mm.sem, lin_mm.after(g, u + 1))
                for e in (2 * j, 2 * j + 1):
                    nc.vector.scalar_tensor_tensor(Q.ACC[0:TW, t, :], PS[0:TW, (4, 7)[u % 2], (e % 2) * D:(e % 2 + 1) * D],
                                                   Q.gate[0:TW, 5, t, e:e + 1], Q.ACC[0:TW, t, :],
                                                   ALU.mult, ALU.add).then_inc(lin_acc.sem, 1)
                    dve.wait_ge(lin_acc.sem, lin_acc.after(g, t * EXPERTS + e + 1))

            def part_a(g, tail):
                for c in range(STEPS):
                    if g is not None:
                        scan_step(FW, g, 0, c)
                    if tail is not None:
                        if c == 1:
                            output_centre(tail, 1)
                        if c == 2:
                            output_norm(tail, 1)
                            dve.wait_ge(bn_done.sem, bn_done.after(tail, 2))
                            nc.vector.tensor_tensor(YS[:, 0, :], YS[:, 0, :], YS[:, 1, :], ALU.add).then_inc(y_sum.sem, 1)
                        if c == 4:
                            centre(Q, Q, tail, 0, 5)
                        if c == 7:
                            links[Q] = 0
                            gates_top(Q, tail, 4)
                    if g is not None:
                        if c == 4:
                            size_of_steps(g, 1)
                        if c == 6:
                            steps(g, 1)
                        output_step(FW, g, 0, c)
                        if c == 1:
                            if tail is not None:
                                dve.wait_ge(out_mm.sem, out_mm.after(tail, 2))
                            convolve(g, 1)
                        if c == 2 and not is_last(g):
                            find_rows(g + 1)
                        if c == 3:
                            split_set(BW, g, 1, 0)
                    if tail is not None:
                        if c == 3:
                            dve.wait_ge(up_proj.sem, up_proj.after(tail, 1))
                            nc.vector.scalar_tensor_tensor(Q.Hm[:, :], PS[:, 5, 0:T], cm("up_b", 0, 1), HBm, ALU.add, ALU.add)
                            nc.vector.scalar_tensor_tensor(Q.Hr[:, :], PS[0:DR, 4, 0:T], cm("up_b", 1, 2, p=DR), HBr, ALU.add, ALU.add).then_inc(Q.residual.sem, 1)
                            dve.wait_ge(Q.residual.sem, Q.residual.after(tail, 1))
                        if c == 5:
                            scale(Q, tail, 0)
                        if c == 7:
                            gates_weights(Q, tail)
                            assert links[Q] == Q.chain.per_group, ("Q", links[Q])
                if g is not None:
                    gated_output(g, 0)
                if tail is not None:
                    gates_rows(Q, tail, 5)

            def part_b(g, tail, nxt):
                for c in range(STEPS):
                    if g is not None:
                        scan_step(BW, g, 1, c)
                    if tail is not None and c >= 2:
                        second_mixture(tail, 2 * c - 4)
                    if tail is not None and c == 0:
                        start_sum(Q, tail, 5, 4)
                    if nxt is not None:
                        if c == 0:
                            combine(nxt)
                        if c == 1:
                            dve.wait_ge(M.back_T.sem, M.back_T.after(nxt, 1))
                            dve.wait_ge(h_loaded.sem, h_loaded.after(nxt, 32))
                            if g is not None:
                                dve.wait_ge(hb_copied.sem, hb_copied.after(g, 1))
                            nc.vector.tensor_tensor(L.Hm[:, :], M.Hm[:, :], PS[:, 5, 0:T], ALU.add)
                            nc.vector.tensor_tensor(L.Hr[:, :], M.Hr[:, :], PS[0:DR, 6, 0:T], ALU.add).then_inc(M.residual.sem, 1)
                            dve.wait_ge(M.residual.sem, M.residual.after(nxt, 1))
                        if c == 2:
                            centre(L, L, nxt, 0, 5)
                        if c == 3:
                            scale(L, nxt, 0)
                        if c == 4:
                            if g is not None:
                                dve.wait_ge(out_mm.sem, out_mm.after(g, 1))
                            convolve(nxt, 0)
                        if c == 6:
                            split_set(FW, nxt, 0, 0)
                            size_of_steps(nxt, 0)
                        if c == 7:
                            steps(nxt, 0)
                    if g is not None:
                        output_step(BW, g, 1, c)
                        if c == 0:
                            output_centre(g, 0)
                        if c == 2:
                            output_norm(g, 0)
                    if tail is not None and c >= 2:
                        second_mixture(tail, 2 * c - 3)
                if g is not None:
                    gated_output(g, 1)
                if tail is not None:
                    dve.wait_ge(Q.back_T.sem, Q.back_T.after(tail, 1))
                    dve.wait_ge(out_free.sem, out_free.after(tail, 1))
                    nc.vector.tensor_tensor(Om[:, :], Q.Hm[:, :], PS[:, 7, 0:T], ALU.add)
                    nc.vector.tensor_tensor(Or[:, :], Q.Hr[:, :], PS[0:DR, 4, 0:T], ALU.add).then_inc(final.sem, 1)
                    dve.wait_ge(final.sem, final.after(tail, 1))

            second_pass(dve, part_a, part_b)

        @block.tensor
        def _(pe):
            pe.wait_ge(prep_pool, 1)
            pe.wait_ge(sel_ready, 2)

            def mm(out, lhsT, rhs, first, last):
                return nc.tensor.matmul(out, lhsT, rhs, start=first, stop=last)

            def both(out, s, wm, wr):
                mm(out, wm, s.Xm[:, :], True, False)
                return mm(out, wr, s.Xr[:, :], False, True)

            def mean(s, src, g, li, bank):
                mm(PS[:, bank, 0:T], ones_d[:, :], src.Hm[:, :], True, False)
                mm(PS[:, bank, 0:T], ones_d[0:DR, :], src.Hr[:, :], False, True).then_inc(s.ln_mean.sem, 1)

            def variance(s, g, li, bank):
                pe.wait_ge(s.ln_squares.sem, s.ln_squares.after(g, 2 * li + 2))
                mm(PS[:, bank, 0:T], ones_d[:, :], s.SQm, True, False)
                mm(PS[:, bank, 0:T], ones_d[0:DR, :], s.SQr[:, :], False, True).then_inc(s.ln_var.sem, 1)

            def hidden(g, first, last):
                for j in range(first, last):
                    a, b = j * 128, min(j * 128 + 128, 1344)
                    if HIDDEN_BEFORE[j] is not None:
                        pe.wait_ge(hid_ready.sem, hid_ready.after(g, HIDDEN_BEFORE[j] + 1))
                    both(PS[0:b - a, HIDDEN_BANKS[j], 0:T], P, cm("m1_w", a, b), cr("m1_w", a, b)).then_inc(hid_mm.sem, 1)

            def broadcast(s, bank, buf, state):
                for rows, cols, toks, _ in PARTS:
                    last = mm(PS[rows, bank, cols], SEL[:, state:state + 1].broadcast_to([128, rows.stop - rows.start]),
                              s.S3[:, buf, toks], True, True)
                return last

            def spread_b(s, g, k, c, buf, off):
                n = k * STEPS + c
                if not at_start(s, g, c):
                    pe.wait_ge(s.b_read.sem, s.b_read.after(g, n))
                for i in range(NC):
                    last = broadcast(s, B_BANK + i, buf, off + c * NC + i)
                last.then_inc(s.b_bc.sem, 1)

            def spread_c(s, g, k, c, buf, off):
                n = k * STEPS + c
                if not at_start(s, g, c):
                    pe.wait_ge(s.prod_ready.sem, s.prod_ready.after(g, n))
                for i in range(NC):
                    last = broadcast(s, C_BANK + i, buf, off + c * NC + i)
                last.then_inc(s.c_bc.sem, 1)

            def spread_a(g, c):
                if c:
                    pe.wait_ge(P.da_ready.sem, P.da_ready.after(g, c))
                for i in range(NC):
                    last = broadcast(P, A_BANK + i, 0, c * NC + i)
                last.then_inc(a_bc.sem, 1)

            def logits(s, g, bank, wm, wr):
                pe.wait_ge(s.ln_x.sem, s.ln_x.after(g, s.ln_x.per_group))
                both(PS[0:EXPERTS, bank, 0:T], s, wm, wr).then_inc(s.logits_mm.sem, 1)

            def logits_T(s, g, bank):
                pe.wait_ge(s.logits_ready.sem, s.logits_ready.after(g, 1))
                for t, a in enumerate(STARTS):
                    last = mm(PS[0:TW, bank, t * EXPERTS:(t + 1) * EXPERTS], s.LW[:, a:a + TW],
                              cm("ident", 0, EXPERTS, p=EXPERTS), True, True)
                last.then_inc(s.logits_T.sem, 1)

            def gates_T(s, g, bank):
                pe.wait_ge(s.gates_ready.sem, s.gates_ready.after(g, 1))
                for t, a in enumerate(STARTS):
                    last = nc.tensor.transpose(PS[0:EXPERTS, bank, a:a + TW], s.gate[0:TW, 5, t, :], cm("ident", 0, TW, p=TW))
                last.then_inc(s.gates_T.sem, 1)

            def biases(s, g, bank01, bank2, bias):
                pe.wait_ge(s.gates_T_ready.sem, s.gates_T_ready.after(g, 1))
                for t, a in enumerate(STARTS):
                    out = PS[0:TW, bank01, t * D:(t + 1) * D] if t < 2 else PS[0:TW, bank2, 0:D]
                    last = mm(out, s.LW[:, a:a + TW], bias, True, True)
                last.then_inc(s.bias_mm.sem, 1)

            def back(s, g, bank_m, bank_r):
                for t, a in enumerate(STARTS):
                    nc.tensor.transpose(PS[:, bank_m, a:a + TW], s.ACC[0:TW, t, 0:DM], cm("ident", 0, TW, p=TW))
                    last = nc.tensor.transpose(PS[0:DR, bank_r, a:a + TW], s.ACC[0:TW, t, DM:D], cm("ident", 0, TW, p=TW))
                last.then_inc(s.back_T.sem, 1)

            def project_half(k, z):
                for rows, cols, toks, feats in PARTS:
                    last = mm(PS[rows, (X_BANK, Z_BANK[k])[z], cols], cm("fb"[k] + "in", z * D + feats.start, z * D + feats.stop, p=BN),
                              HB[:, toks], True, True)
                return last

            def contract(out, name, main, rest, n):
                mm(out, cm(name, 0, n), main, True, False)
                return mm(out, cm(name + "_r", 0, n, p=DR), rest, False, True)

            def project_states(g, k):
                d, s = "fb"[k], DIRS[k]
                pe.wait_ge(u_ready.sem, u_ready.after(g, k + 1))
                contract(PS[0:RANK, Z_BANK[k], 0:T], d + "xdt", s.UP[:, 0:T], s.URr, RANK).then_inc(dt24_mm.sem, 1)
                contract(PS[:, X_BANK, 0:T], d + "xbc", s.UP[:, 0:T], s.URr, NBLK).then_inc(Q.set_mm.sem, 1)

            def project_steps(g, k):
                pe.wait_ge(dt24_ready.sem, dt24_ready.after(g, k + 1))
                for rows, cols, toks, feats in PARTS:
                    last = mm(PS[rows, Z_BANK[k], cols], cm("fb"[k] + "dtw", feats.start, feats.stop, p=RANK), DT24[:, toks], True, True)
                last.then_inc(dt_mm.sem, 1)

            def direction_out(g, k):
                pe.wait_ge(y_gated.sem, y_gated.after(g, k + 1))
                contract(PS[0:BN, AFTER_BANK[k], 0:T], "fb"[k] + "out", DIRS[k].CV[:, 0:T], DIRS[k].GRr, BN).then_inc(out_mm.sem, 1)
                pe.wait_ge(out_copied.sem, out_copied.after(g, k + 1))
                mm(PS[0:BN, AFTER_BANK[k], 0:T], ones_bn[:, :], DIRS[k].YT, True, True).then_inc(bn_mean.sem, 1)

            def direction_var(g, k):
                pe.wait_ge(bn_squares.sem, bn_squares.after(g, k + 1))
                mm(PS[0:BN, AFTER_BANK[k], 0:T], ones_bn[:, :], Q.SQm[0:BN, :], True, True).then_inc(bn_var.sem, 1)

            def scan_start(g, k):
                pe.wait_ge(Q.set_ready.sem, Q.set_ready.after(g, k + 1))
                pe.wait_ge(dt_raw.sem, dt_raw.after(g, k + 1))
                spread_b(DIRS[k], g, k, 0, 0, 0)
                spread_c(DIRS[k], g, k, 0, 0, NS)

            def token_rows(g, tiles):
                for t in tiles:
                    a, col = STARTS[t], t % 2 * D
                    mm(PS[0:TW, 4, col:col + DM], M.Xm[:, a:a + TW], cm("ident"), True, True)
                    last = mm(PS[0:TW, 4, col + DM:col + D], M.Xr[:, a:a + TW], cm("ident", 0, DR, p=DR), True, True)
                last.then_inc(xtok_mm.sem, 1)

            def ranks(g):
                pe.wait_ge(pair_ready.sem, pair_ready.after(g, 1))
                tri = cm("tri", p=TW)
                for t in range(TILES + 1):
                    out = PS[0:TW, 7, t * EXPERTS:(t + 1) * EXPERTS]
                    for u in range(min(t + 1, TILES)):
                        last = mm(out, tri if u == t else ones_tw[:, :], M.gate[0:TW, 5, u, :], u == 0, u == min(t, TILES - 1))
                last.then_inc(ranks_mm.sem, 1)

            def patch_products(g, k):
                lo, hi = ((0, DM), (DM, D))[k]
                for j in range(KP):
                    last = mm(PS[0:hi - lo, (7, 4)[k], 0:IMG * NP], cm("tok_W", j * D + lo, j * D + hi), xp[:, j, :], j == 0, j == KP - 1)
                last.then_inc(tok_mm.sem, 1)

            def first(s, p, m):
                if s is not None:
                    spread_a(s, 0)
                    spread_b(P, s, 0, 0, 0, NS)
                    spread_c(P, s, 0, 0, 1, 0)
                for c in range(STEPS):
                    if s is not None and c + 1 < STEPS:
                        spread_a(s, c + 1)
                        spread_b(P, s, 0, c + 1, 0, NS)
                    if c == 0:
                        if s is not None:
                            pe.wait_ge(delta_ready.sem, delta_ready.after(s, 1))
                        if p is not None:
                            pe.wait_ge(s_const[0], 32)
                            pe.wait_ge(s_x, 16 * p + 16)
                            patch_products(p, 0)
                            patch_products(p, 1)
                    if c == 1:
                        if p is not None:
                            pe.wait_ge(P.residual.sem, P.residual.after(p, 1))
                        if m is not None:
                            pe.wait_ge(scan_out.sem, scan_out.after(m, 1))
                            mean(M, M, m, 0, 7)
                        if p is not None:
                            mean(P, P, p, 0, 4)
                    if c == 3:
                        if m is not None:
                            pe.wait_ge(s_const[1], 32)
                            logits(M, m, 7, cm("r_w"), cr("r_w"))
                        if p is not None:
                            pe.wait_ge(P.ln_x.sem, P.ln_x.after(p, 1))
                            hidden(p, 0, 1)
                    if c == 4:
                        if p is not None:
                            hidden(p, 2, 3)
                    if c == 5:
                        if m is not None:
                            pe.wait_ge(xtok_copied.sem, xtok_copied.after(m, 1))
                            token_rows(m, (2,))
                            pe.wait_ge(M.chain.sem, M.chain.after(m, 1))
                        if p is not None:
                            hidden(p, 4, 5)
                    if c == 6:
                        if p is not None:
                            hidden(p, 6, 7)
                    if s is not None and c + 1 < STEPS:
                        spread_c(P, s, 0, c + 1, 1, 0)
                    if c == 1:
                        if m is not None:
                            variance(M, m, 0, 7)
                        if p is not None:
                            variance(P, p, 0, 4)
                    if c == 3:
                        if p is not None:
                            hidden(p, 1, 2)
                        if m is not None:
                            logits_T(M, m, 7)
                    if c == 4:
                        if p is not None:
                            hidden(p, 3, 4)
                        if m is not None:
                            if p is not None:
                                pe.wait_ge(hid_ready.sem, hid_ready.after(p, 4))
                            token_rows(m, (0, 1))
                    if c == 5:
                        if p is not None:
                            if m is not None:
                                pe.wait_ge(xtok_copied.sem, xtok_copied.after(m, 2))
                            hidden(p, 5, 6)
                        if m is not None:
                            if p is not None:
                                pe.wait_ge(hid_ready.sem, hid_ready.after(p, 5))
                            ranks(m)
                    if c == 6:
                        if m is not None:
                            pe.wait_ge(slots_ready.sem, slots_ready.after(m, 1))
                        if p is not None:
                            hidden(p, 7, 9)
                    if c == 7 and p is not None:
                        for i, (name, first, count, bank) in enumerate((("m2_w0", 0, 6, 7), ("m2_w1", 6, 3, 4))):
                            pe.wait_ge(hid_ready.sem, hid_ready.after(p, (8, 10)[i]))
                            for j in range(count):
                                last = mm(PS[:, bank, 0:T], cm(name, j * NBLK, (j + 1) * NBLK), HID[:, first + j, :], j == 0, j == count - 1)
                            last.then_inc(P.set_mm.sem, 1)
                            if i == 0:
                                hidden(p, 9, 10)
                                pe.wait_ge(P.set_copied.sem, P.set_copied.after(p, 1))
                                hidden(p, 10, 11)
                if p is not None:
                    pe.wait_ge(hid_ready.sem, hid_ready.after(p, 11))
                    for rows, cols, toks, feats in PARTS:
                        mm(PS[rows, 7, cols], cm("d_w2", feats.start, feats.stop), HID[:, 9, toks], True, False)
                        last = mm(PS[rows, 7, cols], cr("d_w2", feats.start, feats.stop), HIDr[:, toks], False, True)
                    last.then_inc(delta_mm.sem, 1)
                    pe.wait_ge(P.set_ready.sem, P.set_ready.after(p, 2))

            first_pass(pe, first)

            def turn(i, p):
                b = 3 * i + p
                pe.wait_ge(s_block[p], 16 * i + 16)
                if not early(b, 1):
                    pe.wait_ge(xt_copied.sem, xt_copied.after(b - 1, 1))
                mm(PS[:, TURN_BANK, 0:128], XB[:, p, 0:DM], cm("ident"), True, True)
                mm(PS[0:DR, TURN_BANK, 128:256], XB[:, p, DM:D], cm("ident"), True, True).then_inc(t_mm.sem, 1)

            def widen(i, p):
                b = 3 * i + p
                pe.wait_ge(xt_copied.sem, xt_copied.after(b, 1))
                pe.wait_ge(s_weights[p], 48 * i + 48)
                if not early(b, 3):
                    pe.wait_ge(gelu_ready.sem, gelu_ready.after(b - 3, 2))
                for h in range(2):
                    for j in range(HALF_FT):
                        out, f = PS[:, WIDE_BANK + 2 * p + h, j * 128:(j + 1) * 128], h * HALF_FT + j
                        mm(out, WX[:, p, f * 128:(f + 1) * 128], XTm[:, p, :], True, False)
                        last = mm(out, WXR[:, p, f * 128:(f + 1) * 128], XTr[:, p, :], False, True)
                    last.then_inc(wide_mm.sem, 1)

            def narrow(i, p):
                b = 3 * i + p
                pe.wait_ge(gelu_ready.sem, gelu_ready.after(b, 2))
                if not early(b, 1):
                    pe.wait_ge(y_copied.sem, y_copied.after(b - 1, 1))
                out = PS[:, OUT_BANK, 0:D]
                mm(out, ones_row[:, :], WXB[:, p, :], True, False)
                for f in range(FT):
                    w = FFN + f * D
                    last = mm(out, HX[:, p, f, :], WX[:, p, w:w + D], False, f == FT - 1)
                last.then_inc(narrow_mm.sem, 1)

            def experts(i, p):
                b = 3 * i + p
                widen(i, p)
                if not is_end(b):
                    turn(*follower(i, p))
                if not early(b, 1):
                    narrow(*previous(i, p))

            turn(0, 0)
            over_blocks(pe, experts)
            narrow(BLOCKS // 3 - 1, 2)

            def second_mixture(g, beside, u):
                t, j, bank = u // 4, u % 4, (4, 7)[u % 2]
                if u == 0:
                    pe.wait_ge(Q.acc_started.sem, Q.acc_started.after(g, 1))
                elif u == 1:
                    if beside is not None:
                        pe.wait_ge(bn_log.sem, bn_log.after(beside, 1))
                elif u >= 2:
                    pe.wait_ge(lin_acc.sem, lin_acc.after(g, 2 * (u - 1)))
                a = STARTS[t]
                mm(PS[0:TW, bank, 0:2 * D], Q.Xm[:, a:a + TW], cm("ew", 2 * j * D, 2 * (j + 1) * D), True, False)
                mm(PS[0:TW, bank, 0:2 * D], Q.Xr[:, a:a + TW], cr("ew", 2 * j * D, 2 * (j + 1) * D), False, True).then_inc(lin_mm.sem, 1)

            def part_a(g, tail):
                if g is not None:
                    scan_start(g, 0)
                    project_half(1, 0)
                if tail is not None:
                    pe.wait_ge(final.sem, final.after(tail, 0))
                if g is not None:
                    project_half(1, 1).then_inc(in_mm.sem, 1)
                for c in range(STEPS):
                    if g is not None and c + 1 < STEPS:
                        spread_b(FW, g, 0, c + 1, 0, 0)
                    if tail is not None:
                        if c == 0:
                            direction_out(tail, 1)
                        if c == 4:
                            variance(Q, tail, 0, 5)
                        if c == 6:
                            logits(Q, tail, 5, cm("er_w"), cr("er_w"))
                    if g is not None and c == 2:
                        project_states(g, 1)
                    if g is not None and c + 1 < STEPS:
                        spread_c(FW, g, 0, c + 1, 0, NS)
                    if tail is not None:
                        if c == 1:
                            direction_var(tail, 1)
                        if c == 2:
                            pe.wait_ge(y_sum.sem, y_sum.after(tail, 1))
                            mm(PS[:, 5, 0:T], cm("up", 0, DM, p=BN), YS[:, 0, :], True, True)
                            mm(PS[0:DR, 4, 0:T], cm("up", DM, D, p=BN), YS[:, 0, :], True, True).then_inc(up_proj.sem, 1)
                        if c == 3:
                            pe.wait_ge(Q.residual.sem, Q.residual.after(tail, 1))
                            mean(Q, Q, tail, 0, 5)
                        if c == 6:
                            logits_T(Q, tail, 4)
                    if g is not None and c == 2:
                        project_steps(g, 1)
                if tail is not None:
                    gates_T(Q, tail, 5)

            def part_b(g, tail, nxt):
                if g is not None:
                    scan_start(g, 1)
                if tail is not None:
                    biases(Q, tail, 5, 4, cm("eb", p=EXPERTS))
                for c in range(STEPS):
                    if g is not None and c + 1 < STEPS:
                        spread_b(BW, g, 1, c + 1, 0, 0)
                    if g is not None:
                        if c == 0:
                            direction_out(g, 0)
                        if c == 1:
                            direction_var(g, 0)
                    if nxt is not None and c == 5:
                        project_steps(nxt, 0)
                    if tail is not None and 2 <= c < STEPS - 1:
                        second_mixture(tail, g, 2 * c - 2)
                    if g is not None and c + 1 < STEPS:
                        spread_c(BW, g, 1, c + 1, 0, NS)
                    if nxt is not None:
                        if c == 0:
                            pe.wait_ge(mixed.sem, mixed.after(nxt, TILES))
                            back(M, nxt, 5, 6)
                        if c == 1:
                            pe.wait_ge(M.residual.sem, M.residual.after(nxt, 1))
                            mean(L, L, nxt, 0, 5)
                        if c == 2:
                            variance(L, nxt, 0, 5)
                        if c == 3:
                            pe.wait_ge(L.ln_x.sem, L.ln_x.after(nxt, 1))
                            both(PS[0:BN, 5, 0:T], L, cm("down"), cr("down")).then_inc(bott_mm.sem, 1)
                            pe.wait_ge(bott_ready.sem, bott_ready.after(nxt, 1))
                            project_half(0, 0)
                            project_half(0, 1).then_inc(in_mm.sem, 1)
                    if tail is not None:
                        if c == 0:
                            second_mixture(tail, g, 0)
                        if c == 1:
                            second_mixture(tail, g, 1)
                        if 2 <= c < STEPS - 1:
                            second_mixture(tail, g, 2 * c - 1)
                    if nxt is not None and c == 4:
                        project_states(nxt, 0)
                if tail is not None:
                    pe.wait_ge(lin_acc.sem, lin_acc.after(tail, TILES * EXPERTS))
                    back(Q, tail, 7, 4)

            second_pass(pe, part_a, part_b)


def _rows(a):
    a = np.asarray(a)
    return a.reshape(a.shape[0], -1)


def _main_rest(v):
    v = np.asarray(v).reshape(D, -1)
    return np.concatenate([v[0:DM], np.concatenate([v[DM:D], v[DM:D]])], axis=1)


def _state_columns(parts):
    rows = parts[0].shape[0]
    out = np.zeros((rows, 4, 2, NS), np.float32)
    for i, w in parts.items() if isinstance(parts, dict) else enumerate(parts):
        out[:, :, i, :] = np.asarray(w)[:, None, :]
    return out.reshape(rows, NBLK)


def _arrays(inp):
    I = {k: np.asarray(v) for k, v in inp.items()}
    x = I["x"].reshape(GROUPS, IMG, 3, GRID, 16, GRID, 16).transpose(0, 2, 4, 6, 1, 3, 5)
    x_p = np.ascontiguousarray(x.reshape(GROUPS, KP, 128, IMG * NP).transpose(0, 2, 1, 3))
    c128, c64 = np.zeros((128, C128), np.float32), np.zeros((DR, C64), np.float32)

    def put(name, a):
        a = _rows(a)
        at, width = AT[name]
        assert a.shape[1] == width, (name, a.shape, width)
        c128[0:a.shape[0], at:at + width] = a

    def put_both(name, w):
        w = _rows(w)
        put(name, w[0:DM])
        at, width = ATR[name]
        c64[:, at:at + width] = w[DM:D]

    put("tok_W", I["L0_tok_W"].reshape(KP, 128, D).transpose(1, 0, 2))
    near = np.arange(GRID) * 14 // GRID
    pos = I["L0_tok_positions"][0][:, near][:, :, near].reshape(D, NP)
    put("posm", pos[0:DM])
    put("posr", pos[DM:D])
    put("tok_b", _main_rest(I["L0_tok_b"]))
    cls = np.stack([I["cls_tok"][0, 0], I["L0_tok_cls_embedding"][0, 0]], axis=1)
    put("cls_m", cls[0:DM])
    put("cls_r", cls[DM:D])
    put("ident", np.eye(128, dtype=np.float32))
    put("log_dt", _main_rest(I["L0_attn_log_dt"]))
    row = np.arange(128) % 32
    put("sign", np.where(row < NS, -1.0, 1.0).astype(np.float32)[:, None])
    a = "L0_attn_"
    put_both("m1_w", np.concatenate([I[a + n + "_w1"] for n in "ABCd"], axis=1))
    b1 = np.concatenate([I[a + n + "_b1"] for n in "ABCd"])
    b1 = np.concatenate([b1, np.zeros(64, np.float32)]).reshape(11, 128).T
    put("m1_b", b1)
    none = np.zeros((128, NS), np.float32)
    w2 = {n: I[a + n + "_w2"].reshape(3, 128, NS) for n in "ABC"}
    put("m2_w0", np.stack([_state_columns([w2["A"][j], none]) for j in range(3)] +
                          [_state_columns([none, w2["B"][j]]) for j in range(3)], axis=1))
    put("m2_w1", np.stack([_state_columns([w2["C"][j], none]) for j in range(3)], axis=1))
    bias = [_state_columns([I[a + "A_b2"][None], I[a + "B_b2"][None]]), _state_columns([I[a + "C_b2"][None], none[0:1]])]
    put("m2_b", np.stack([b[0] for b in bias], axis=1))
    put_both("d_w2", I[a + "d_w2"])
    put("d_b2", _main_rest(I[a + "d_b2"]))
    put("D0", _main_rest(I[a + "D_param"]))
    put("rank", np.broadcast_to(np.arange(EXPERTS, 0, -1, dtype=np.float32), (128, EXPERTS)))
    put_both("r_w", I["L0_ffn_Wr"].T)
    put("eoff", np.broadcast_to(np.arange(EXPERTS, dtype=np.float32) * CAP_BLOCKS * 128, (128, EXPERTS)))
    put("blk", np.broadcast_to(np.arange(CAP_BLOCKS, dtype=np.float32) * 128, (128, CAP_BLOCKS)))
    e = np.arange(EXPERTS)
    put("below", np.broadcast_to((e[None, :] < e[:, None]).astype(np.float32).reshape(1, -1), (128, EXPERTS * EXPERTS)))
    put("bid", np.broadcast_to(np.arange(BLOCKS, dtype=np.float32), (128, BLOCKS)))
    t = np.arange(TW)
    put("tri", (t[:, None] < t[None, :]).astype(np.float32))
    wi = I["L0_ffn_Wi"].transpose(0, 2, 1)
    wo = I["L0_ffn_Wo"].reshape(EXPERTS, D, FT, 128).transpose(0, 3, 2, 1).reshape(EXPERTS, 128, FT * D)
    bi = I["L0_ffn_bi"].reshape(EXPERTS, FT, 128).transpose(0, 2, 1)
    ex_m = np.ascontiguousarray(np.concatenate([wi[:, 0:DM], wo, bi], axis=2))
    ex_r = np.ascontiguousarray(wi[:, DM:D])
    ex_b = np.ascontiguousarray(I["L0_ffn_bo"].reshape(EXPERTS, 1, D))
    b = "L1_attn_"
    put_both("down", I[b + "down_W"])
    put("down_b", I[b + "down_b"][:, None])
    put("up", I[b + "up_W"])
    put("up_b", _main_rest(I[b + "up_b"]))
    for d in "fb":
        p = b + d + "_"
        put(d + "in", I[p + "in_W"])
        put(d + "cw", _main_rest(I[p + "conv_w"]))
        put(d + "cb", _main_rest(I[p + "conv_b"]))
        xw = _main_rest(I[p + "xproj_W"]).reshape(128, 2, RANK + 2 * NS)
        for h, tail in enumerate(("", "_r")):
            put(d + "xdt" + tail, xw[:, h, 0:RANK])
            put(d + "xbc" + tail, _state_columns([xw[:, h, RANK:RANK + NS], xw[:, h, RANK + NS:]]))
        put(d + "dtw", I[p + "dt_W"])
        put(d + "dtb", _main_rest(I[p + "dt_b"]))
        put(d + "Alog", _main_rest(I[p + "A_log"]))
        put(d + "Dp", _main_rest(I[p + "D"]))
        ow = _main_rest(I[p + "out_W"]).reshape(128, 2, BN)
        put(d + "out", ow[:, 0])
        put(d + "out_r", ow[:, 1])
        put(d + "lng", np.stack([I[p + "ln_g"], I[p + "ln_b"]], axis=1))
    put_both("er_w", I["L1_ffn_router_w"].T)
    put("er_b", I["L1_ffn_router_b"][:, None])
    put_both("ew", I["L1_ffn_expert_w"].transpose(2, 0, 1))
    put("eb", I["L1_ffn_expert_b"])
    r, n = np.arange(128)[:, None], np.arange(2 * NS)[None, :]
    sel = ((r % 32 == n) & (r // 32 != 1)).astype(np.float32)
    return {"x_p": x_p, "c128": c128, "c64": c64, "sel_d": sel, "ex_m": ex_m, "ex_r": ex_r, "ex_b": ex_b}


def kernel(**inputs):
    import concourse.bacc as bacc
    from concourse.bass_utils import run_bass_kernel_spmd

    nc = bacc.Bacc("TRN2", target_bir_lowering=False, num_devices=1)
    arrays = _arrays(inputs)
    args = [nc.dram_tensor(n, a.shape, mybir.dt.from_np(a.dtype), kind="ExternalInput").ap() for n, a in arrays.items()]
    out_m = nc.dram_tensor("out_m", (GROUPS, DM, T), mybir.dt.float32, kind="ExternalOutput").ap()
    out_r = nc.dram_tensor("out_r", (GROUPS, DR, T), mybir.dt.float32, kind="ExternalOutput").ap()
    vit_tower(nc, *args, out_m, out_r)
    got = run_bass_kernel_spmd(nc, [arrays], core_ids=[0]).results[0]
    both = np.concatenate([got["out_m"], got["out_r"]], axis=1).reshape(GROUPS, D, IMG, SEQ)
    return np.ascontiguousarray(both.transpose(0, 2, 3, 1).reshape(BATCH, SEQ, D))
```
